# Optimizing a Trainium2 kernel written in Bass

```python
import numpy as np
import jax
import jax.numpy as jnp

def _softmax(x, axis=-1):
    return jax.nn.softmax(x, axis=axis)

def _gelu(x):
    return jax.nn.gelu(x, approximate=True)

def _silu(x):
    return jax.nn.silu(x)

def _sigmoid(x):
    return jax.nn.sigmoid(x)

def _layernorm(x, axis=-1, eps=1e-05):
    m = jnp.mean(x, axis=axis, keepdims=True)
    v = jnp.var(x, axis=axis, keepdims=True)
    return (x - m) / jnp.sqrt(v + eps)

def _scatter_add(tgt, idx, src, axis=0):
    return tgt.at[idx].add(src)

def _segment_sum(src, seg, n):
    return jax.ops.segment_sum(src, seg, n)
kernel_name = 'mk_adj_ffn_d2_adj_r2_27ba50'

def setup_inputs(seed: int=0):
    np.random.seed(seed)
    _w = jnp.asarray

    def _rec_inputs():
        import jax
        import jax.numpy as jnp
        _gk = jax.random.key(seed)
        x = -0.000929 + 1 * jax.random.normal(jax.random.fold_in(_gk, 1), (64, 128, 128), jnp.float32)
        _a = jax.random.bernoulli(jax.random.fold_in(_gk, 2), 0.125, (128, 128))
        _a = jnp.logical_or(_a, jnp.eye(128, dtype=bool))
        adj = _a.astype(jnp.int32)
        return (x, adj)
    x, adj = _rec_inputs()

    def _L0_gnn_setup():
        import jax, jax.numpy as jnp
        import numpy as np
        ALPHA = 0.2
        EPS = 1e-06
        key = jax.random.key(seed)
        ks = jax.random.split(key, 8)
        B, N, D, H = (2, 1024, 128, 8)
        dh = D // H
        x = jax.random.normal(ks[0], (B, N, D), dtype=jnp.float32)
        adj = jax.random.randint(ks[1], (N, N), 0, 2, dtype=jnp.int32)
        adj = jnp.maximum(adj, jnp.eye(N, dtype=jnp.int32))
        p = jax.random.uniform(ks[2], (B, N, N), dtype=jnp.float32)
        prior = p / jnp.sum(p, axis=-1, keepdims=True)
        W = jax.random.normal(ks[3], (H, D, dh), dtype=jnp.float32) * (1.0 / np.sqrt(D))
        a_src = jax.random.normal(ks[4], (H, dh), dtype=jnp.float32) * (1.0 / np.sqrt(dh))
        a_dst = jax.random.normal(ks[5], (H, dh), dtype=jnp.float32) * (1.0 / np.sqrt(dh))
        beta_tilde = jnp.ones((), dtype=jnp.float32)
        W_out = jax.random.normal(ks[6], (D, D), dtype=jnp.float32) * (1.0 / np.sqrt(D))
        return {'x': x, 'adj': adj, 'prior': prior, 'W': W, 'a_src': a_src, 'a_dst': a_dst, 'beta_tilde': beta_tilde, 'W_out': W_out}
    _L0_gnn_all = _L0_gnn_setup()
    _L0_gnn_in = {k: v for k, v in _L0_gnn_all.items() if k in ('W', 'a_src', 'a_dst', 'beta_tilde', 'W_out')}
    del _L0_gnn_all

    def _L0_ffn_setup():
        import jax, jax.numpy as jnp
        import numpy as np
        B, S, D, F, E, K = (8, 1024, 128, 512, 8, 2)
        key = jax.random.key(seed)
        ks = jax.random.split(key, 10)
        s = 0.02
        return {'x': jax.random.normal(ks[0], (B, S, D), dtype=jnp.float32), 'Wr': jax.random.normal(ks[1], (D, E), dtype=jnp.float32) * s, 'W1s': jax.random.normal(ks[2], (D, F), dtype=jnp.float32) * s, 'b1s': jnp.zeros((F,), dtype=jnp.float32), 'W2s': jax.random.normal(ks[3], (F, D), dtype=jnp.float32) * s, 'b2s': jnp.zeros((D,), dtype=jnp.float32), 'W1p': jax.random.normal(ks[4], (E, D, F), dtype=jnp.float32) * s, 'b1p': jnp.zeros((E, F), dtype=jnp.float32), 'W2p': jax.random.normal(ks[5], (E, F, D), dtype=jnp.float32) * s, 'b2p': jnp.zeros((E, D), dtype=jnp.float32)}
    _L0_ffn_all = _L0_ffn_setup()
    _L0_ffn_in = {k: v for k, v in _L0_ffn_all.items() if k in ('Wr', 'W1s', 'b1s', 'W2s', 'b2s', 'W1p', 'b1p', 'W2p', 'b2p')}
    del _L0_ffn_all

    def _L1_gnn_setup():
        import jax, jax.numpy as jnp
        import numpy as np
        ALPHA = 0.2
        NEG_INF = -9000000000000000.0

        def _gat(inp, adj_mask, W, a):
            h = jnp.matmul(inp, W)
            F_ = h.shape[-1]
            f1 = jnp.matmul(h, a[:F_, 0])
            f2 = jnp.matmul(h, a[F_:, 0])
            e = jax.nn.leaky_relu(f1[:, :, None] + f2[:, None, :], ALPHA)
            if adj_mask is not None:
                e = jnp.where(adj_mask[None, :, :] > 0, e, NEG_INF)
            att = jax.nn.softmax(e, axis=2)
            h_prime = jnp.einsum('bij,bjf->bif', att, h)
            return jax.nn.elu(h_prime)
        key = jax.random.key(seed)
        ks = jax.random.split(key, 10)
        B, N, Fin, H, O = (16, 512, 128, 256, 128)

        def xavier(k, shape):
            fan_in, fan_out = (shape[0], shape[-1])
            bound = 1.414 * np.sqrt(6.0 / (fan_in + fan_out))
            return jax.random.uniform(k, shape, jnp.float32, -bound, bound)
        return {'x': jax.random.normal(ks[0], (B, N, Fin), jnp.float32), 'adj': jax.random.randint(ks[1], (N, N), 0, 2, jnp.int32), 'mlp1_w': xavier(ks[2], (Fin, H)), 'mlp1_b': jnp.zeros((H,), jnp.float32), 'mlp2_w': xavier(ks[3], (H, O)), 'mlp2_b': jnp.zeros((O,), jnp.float32), 'W_fc': xavier(ks[4], (H, H)), 'a_fc': xavier(ks[5], (2 * H, 1)), 'W_hand': xavier(ks[6], (O, O)), 'a_hand': xavier(ks[7], (2 * O, 1))}
    _L1_gnn_all = _L1_gnn_setup()
    _L1_gnn_in = {k: v for k, v in _L1_gnn_all.items() if k in ('mlp1_w', 'mlp1_b', 'mlp2_w', 'mlp2_b', 'W_fc', 'a_fc', 'W_hand', 'a_hand')}
    del _L1_gnn_all

    def _L1_ffn_setup():
        import jax, jax.numpy as jnp
        import numpy as np
        B, S, D = (8, 2048, 128)
        H = 4 * D
        CAPACITY = 0.5
        key = jax.random.key(seed)
        ks = jax.random.split(key, 6)
        x = jax.random.normal(ks[0], (B, S, D), dtype=jnp.float32)
        attention_mask = jnp.zeros((B, 1, 1, S), dtype=jnp.float32)
        wr = jax.random.normal(ks[1], (D, 1), dtype=jnp.float32) * 0.02
        br = jnp.zeros((1,), dtype=jnp.float32)
        w1 = jax.random.normal(ks[2], (D, H), dtype=jnp.float32) * 0.02
        b1 = jnp.zeros((H,), dtype=jnp.float32)
        w2 = jax.random.normal(ks[3], (H, D), dtype=jnp.float32) * 0.02
        b2 = jnp.zeros((D,), dtype=jnp.float32)
        return {'x': x, 'attention_mask': attention_mask, 'wr': wr, 'br': br, 'w1': w1, 'b1': b1, 'w2': w2, 'b2': b2}
    _L1_ffn_all = _L1_ffn_setup()
    _L1_ffn_in = {k: v for k, v in _L1_ffn_all.items() if k in ('attention_mask', 'wr', 'br', 'w1', 'b1', 'w2', 'b2')}
    del _L1_ffn_all
    return {'x': x, 'adj': adj, 'L0_gnn_W': _L0_gnn_in['W'], 'L0_gnn_a_src': _L0_gnn_in['a_src'], 'L0_gnn_a_dst': _L0_gnn_in['a_dst'], 'L0_gnn_beta_tilde': _L0_gnn_in['beta_tilde'], 'L0_gnn_W_out': _L0_gnn_in['W_out'], 'L0_ffn_Wr': _L0_ffn_in['Wr'], 'L0_ffn_W1s': _L0_ffn_in['W1s'], 'L0_ffn_b1s': _L0_ffn_in['b1s'], 'L0_ffn_W2s': _L0_ffn_in['W2s'], 'L0_ffn_b2s': _L0_ffn_in['b2s'], 'L0_ffn_W1p': _L0_ffn_in['W1p'], 'L0_ffn_b1p': _L0_ffn_in['b1p'], 'L0_ffn_W2p': _L0_ffn_in['W2p'], 'L0_ffn_b2p': _L0_ffn_in['b2p'], 'L1_gnn_mlp1_w': _L1_gnn_in['mlp1_w'], 'L1_gnn_mlp1_b': _L1_gnn_in['mlp1_b'], 'L1_gnn_mlp2_w': _L1_gnn_in['mlp2_w'], 'L1_gnn_mlp2_b': _L1_gnn_in['mlp2_b'], 'L1_gnn_W_fc': _L1_gnn_in['W_fc'], 'L1_gnn_a_fc': _L1_gnn_in['a_fc'], 'L1_gnn_W_hand': _L1_gnn_in['W_hand'], 'L1_gnn_a_hand': _L1_gnn_in['a_hand'], 'L1_ffn_attention_mask': _L1_ffn_in['attention_mask'], 'L1_ffn_wr': _L1_ffn_in['wr'], 'L1_ffn_br': _L1_ffn_in['br'], 'L1_ffn_w1': _L1_ffn_in['w1'], 'L1_ffn_b1': _L1_ffn_in['b1'], 'L1_ffn_w2': _L1_ffn_in['w2'], 'L1_ffn_b2': _L1_ffn_in['b2']}

def reference(x, adj, L0_gnn_W, L0_gnn_a_src, L0_gnn_a_dst, L0_gnn_beta_tilde, L0_gnn_W_out, L0_ffn_Wr, L0_ffn_W1s, L0_ffn_b1s, L0_ffn_W2s, L0_ffn_b2s, L0_ffn_W1p, L0_ffn_b1p, L0_ffn_W2p, L0_ffn_b2p, L1_gnn_mlp1_w, L1_gnn_mlp1_b, L1_gnn_mlp2_w, L1_gnn_mlp2_b, L1_gnn_W_fc, L1_gnn_a_fc, L1_gnn_W_hand, L1_gnn_a_hand, L1_ffn_attention_mask, L1_ffn_wr, L1_ffn_br, L1_ffn_w1, L1_ffn_b1, L1_ffn_w2, L1_ffn_b2):
    import jax
    import jax.numpy as jnp

    def _L0_gnn_ref(x, adj, prior, W, a_src, a_dst, beta_tilde, W_out):
        import jax, jax.numpy as jnp
        import numpy as np
        ALPHA = 0.2
        EPS = 1e-06
        B, N, D = x.shape
        x_proj = jnp.einsum('bnd,hdf->bhnf', x, W)
        e_src = jnp.einsum('bhnf,hf->bhn', x_proj, a_src)
        e_dst = jnp.einsum('bhnf,hf->bhn', x_proj, a_dst)
        e = jax.nn.leaky_relu(e_src[..., :, None] + e_dst[..., None, :], ALPHA)
        beta = jax.nn.softplus(beta_tilde)
        e = e + (beta * jnp.log(prior + EPS))[:, None, :, :]
        neg_inf = jnp.finfo(e.dtype).min
        e = jnp.where(adj[None, None, :, :] > 0, e, neg_inf)
        attn = jax.nn.softmax(e, axis=-1)
        h = jnp.einsum('bhij,bhjf->bhif', attn, x_proj)
        h = h.transpose(0, 2, 1, 3).reshape(B, N, D)
        return h @ W_out.T

    def _L0_ffn_ref(x, Wr, W1s, b1s, W2s, b2s, W1p, b1p, W2p, b2p):
        import jax, jax.numpy as jnp
        import numpy as np
        B, S, D, F, E, K = (8, 1024, 128, 512, 8, 2)
        gelu = lambda t: jax.nn.gelu(t, approximate=False)
        shared = gelu(x @ W1s + b1s) @ W2s + b2s
        rw = jax.nn.softmax(x @ Wr, axis=-1)
        topw, topi = jax.lax.top_k(rw, K)
        topw = topw / jnp.sum(topw, axis=-1, keepdims=True)
        mask = jnp.sum(jax.nn.one_hot(topi, E, dtype=topw.dtype) * topw[..., None], axis=-2)
        h = gelu(jnp.einsum('bsd,edf->bsef', x, W1p) + b1p)
        priv = jnp.einsum('bsef,efd->bsed', h, W2p) + b2p
        routed = jnp.einsum('bsed,bse->bsd', priv, mask)
        return shared + routed

    def _L1_gnn_ref(x, adj, mlp1_w, mlp1_b, mlp2_w, mlp2_b, W_fc, a_fc, W_hand, a_hand):
        import jax, jax.numpy as jnp
        import numpy as np
        ALPHA = 0.2
        NEG_INF = -9000000000000000.0

        def _gat(inp, adj_mask, W, a):
            h = jnp.matmul(inp, W)
            F_ = h.shape[-1]
            f1 = jnp.matmul(h, a[:F_, 0])
            f2 = jnp.matmul(h, a[F_:, 0])
            e = jax.nn.leaky_relu(f1[:, :, None] + f2[:, None, :], ALPHA)
            if adj_mask is not None:
                e = jnp.where(adj_mask[None, :, :] > 0, e, NEG_INF)
            att = jax.nn.softmax(e, axis=2)
            h_prime = jnp.einsum('bij,bjf->bif', att, h)
            return jax.nn.elu(h_prime)
        out = jax.nn.relu(jnp.matmul(x, mlp1_w) + mlp1_b)
        residual = out
        out = _gat(jax.nn.relu(out), None, W_fc, a_fc)
        out = jax.nn.elu(out) + residual
        out = jax.nn.relu(jnp.matmul(out, mlp2_w) + mlp2_b)
        residual = out
        out = _gat(jax.nn.relu(out), adj, W_hand, a_hand)
        out = jax.nn.elu(out) + residual
        return jax.nn.relu(out)

    def _L1_ffn_ref(x, attention_mask, wr, br, w1, b1, w2, b2):
        import jax, jax.numpy as jnp
        import numpy as np
        B, S, D = (8, 2048, 128)
        H = 4 * D
        CAPACITY = 0.5
        b, s, d = x.shape
        weights = (jnp.einsum('bsd,do->bso', x, wr) + br)[..., 0]
        k = max(1, int(CAPACITY * s))
        kk = k - 1 if k > 1 else 1
        _, idx = jax.lax.top_k(weights, k)
        sel_idx = idx[:, :kk]
        sel = jnp.take_along_axis(x, sel_idx[:, :, None], axis=1)
        h = jax.nn.gelu(jnp.einsum('bkd,dh->bkh', sel, w1) + b1)
        y = jnp.einsum('bkh,hd->bkd', h, w2) + b2
        w_sel = jnp.take_along_axis(weights, sel_idx, axis=1)
        y = y * w_sel[..., None]
        batch_idx = jnp.arange(b)[:, None]
        processed = jnp.zeros_like(x).at[batch_idx, sel_idx].set(y)
        return processed + x
    x = x + _L0_gnn_ref(_layernorm(x, axis=-1), adj, adj[None], L0_gnn_W, L0_gnn_a_src, L0_gnn_a_dst, L0_gnn_beta_tilde, L0_gnn_W_out)
    x = x + _L0_ffn_ref(_layernorm(x, axis=-1), L0_ffn_Wr, L0_ffn_W1s, L0_ffn_b1s, L0_ffn_W2s, L0_ffn_b2s, L0_ffn_W1p, L0_ffn_b1p, L0_ffn_W2p, L0_ffn_b2p)
    x = x + _L1_gnn_ref(_layernorm(x, axis=-1), adj, L1_gnn_mlp1_w, L1_gnn_mlp1_b, L1_gnn_mlp2_w, L1_gnn_mlp2_b, L1_gnn_W_fc, L1_gnn_a_fc, L1_gnn_W_hand, L1_gnn_a_hand)
    x = x + _L1_ffn_ref(_layernorm(x, axis=-1), L1_ffn_attention_mask, L1_ffn_wr, L1_ffn_br, L1_ffn_w1, L1_ffn_b1, L1_ffn_w2, L1_ffn_b2)
    return x

_drawn_inputs = setup_inputs


def setup_inputs(seed=0):
    import zlib

    import numpy as np

    out = dict(_drawn_inputs(seed))
    spreads = {'L0_ffn_b1s': (0.0, 0.342),
     'L0_ffn_b2s': (0.0, 0.1),
     'L0_ffn_b1p': (0.0, 0.597),
     'L0_ffn_b2p': (0.0, 0.1),
     'L1_gnn_mlp1_b': (0.0, 0.1),
     'L1_gnn_mlp2_b': (0.0, 0.1),
     'L1_ffn_b1': (0.0, 0.8),
     'L1_ffn_b2': (0.0, 0.8)}
    factors = {'L1_ffn_wr': 8.0, 'L1_ffn_w1': 8.0, 'L1_ffn_w2': 8.0}
    for name, (base, spread) in spreads.items():
        noise = np.random.default_rng([zlib.crc32(name.encode()), seed]).standard_normal(out[name].shape)
        drawn = base * np.exp(spread * noise) if base else spread * noise
        out[name] = jnp.asarray(drawn.astype(out[name].dtype))
    for name, factor in factors.items():
        out[name] = (out[name] * factor).astype(out[name].dtype)
    return out
```

```python
from contextlib import ExitStack

import concourse.bass as bass
from concourse import mybir

F32 = mybir.dt.float32
BF16 = mybir.dt.bfloat16
I32 = mybir.dt.int32
ALU = mybir.AluOpType
ACT = mybir.ActivationFunctionType
AX = mybir.AxisListType

P = 128
BATCHES, TOKENS, D = 64, 128, 128
GB = 4
GROUPS = BATCHES // GB
HEADS, DH = 8, 16
HB = GB * HEADS
VW = DH + 1
EPS_LN = 1e-5
EPS_PRIOR = 1e-6
EXP_LN_TABLES = 6
BIG = 3.0e38
NEG_INF_L1 = -9.0e15


class Buffers:
    pass


def wait(eng, sem, count):
    if isinstance(count, int) and count <= 0:
        return
    eng.wait_ge(sem, count)


def exp_ln_tables(nc, act):
    act.add_instruction(mybir.InstLoadActFuncSet(
        name=nc.get_next_instruction_name(), engine=mybir.EngineType.Activation,
        act_func_set_id=EXP_LN_TABLES, ins=[], outs=[]))


class PhaseSemaphores:

    def __init__(self, nc, prefix):
        self.nc, self.prefix, self.mine = nc, prefix, []

    def make(self, name):
        self.mine.append(self.nc.alloc_semaphore(name=self.prefix + name))
        return self.mine[-1]

    def clear(self):
        self.nc.clear_and_free_semaphores(self.mine)
        with self.nc.Block():
            pass


def setup_phase(nc, k, a):
    with ExitStack() as ctx:
        def sb(name, shape, dt=F32):
            return ctx.enter_context(nc.sbuf_tensor(name, shape, dt))

        def sem(name):
            return ctx.enter_context(nc.semaphore(name))

        adj_i = sb("adj_i", [P, P], I32)
        adj_f = sb("adj_f", [P, P])
        mask = sb("mask", [P, P])
        logw = sb("logw", [P, P])
        m_ij = sb("m_ij", [P, P])
        u_ij = sb("u_ij", [P, P])
        row_stat = sb("row_stat", [P, 4])
        beta = sb("beta", [P, 4])
        w_out_in = sb("w_out_in", [P, D])
        a_heads = sb("a_heads", [P, 2, HEADS, DH])
        wa_prod = sb("wa_prod", [P, 2, HEADS, DH])
        wa = sb("wa", [P, 2, HEADS])
        fold_a1 = sb("fold_a1", [P, 2, 256])
        fold_p1 = sb("fold_p1", [P, 2, 2, 256])
        fold_a2 = sb("fold_a2", [P, 2, P])
        fold_p2 = sb("fold_p2", [P, 2, P])
        fold_1 = sb("fold_1", [P, 2, 2])
        fold_2 = sb("fold_2", [P, 2])
        tri_f = sb("tri_f", [P, P])

        load_x, load_w, load_adj, load_cap = sem("load_x"), sem("load_w"), sem("load_adj"), sem("load_cap")
        pool_made, ones_made, dve_s, act_s, pe_t = (sem("pool_made"), sem("ones_made"), sem("dve_s"),
                                                    sem("act_s"), sem("pe_t"))
        tr = ctx.enter_context(nc.psum_tensor("setup_tr", [P, 4, 512], F32))
        W_LOADS = []

        with nc.Block() as block:
            @block.sync
            def _(sp):
                sp.dma_start(adj_i[:], a["adj"]).then_inc(load_adj, 16)
                sp.dma_start(beta[:, 0:1], a["L0_gnn_beta_tilde"].partition_broadcast(P)).then_inc(load_adj, 16)
                def load(dst, src):
                    W_LOADS.append(1)
                    sp.dma_start(dst, src, allow_slow_non_contiguous=True).then_inc(load_w, 16)
                load(w_out_in[:], a["L0_gnn_W_out"])
                load(k.w_heads[:, 0:D].rearrange("d (h f) -> d h f", h=HEADS), a["L0_gnn_W"].rearrange("h d f -> d h f"))
                load(a_heads[:, 0].rearrange("p h f -> p (h f)"),
                     a["L0_gnn_a_src"].rearrange("h f -> (h f)").partition_broadcast(P))
                load(a_heads[:, 1].rearrange("p h f -> p (h f)"),
                     a["L0_gnn_a_dst"].rearrange("h f -> (h f)").partition_broadcast(P))
                load(k.w_fc[:, :, 0:256], a["L1_gnn_W_fc"].rearrange("(c p) n -> p c n", p=P))
                load(fold_a1[:].rearrange("p t n -> p (t n)"),
                     a["L1_gnn_a_fc"].rearrange("n o -> (n o)").partition_broadcast(P))
                load(k.w_hand[:, 0:D], a["L1_gnn_W_hand"])
                load(fold_a2[:].rearrange("p t n -> p (t n)"),
                     a["L1_gnn_a_hand"].rearrange("n o -> (n o)").partition_broadcast(P))
                load(k.w_mlp1[:], a["L1_gnn_mlp1_w"])
                load(k.w_mlp2[:], a["L1_gnn_mlp2_w"].rearrange("(c p) n -> p c n", p=P))
                load(k.b_mlp1[:], a["L1_gnn_mlp1_b"].rearrange("(c p) -> p c", p=P))
                load(k.b_mlp2[:], a["L1_gnn_mlp2_b"].rearrange("(p o) -> p o", o=1))
                load(k.w_router[:], a["L0_ffn_Wr"])
                load(k.w1_shared[:], a["L0_ffn_W1s"])
                load(k.w2_shared[:], a["L0_ffn_W2s"].rearrange("(c p) n -> p c n", p=P))
                load(k.b1_shared[:], a["L0_ffn_b1s"].rearrange("(c p) -> p c", p=P))
                load(k.b2_shared[:], a["L0_ffn_b2s"].partition_broadcast(P))
                load(k.w1_last[:], a["L1_ffn_w1"])
                load(k.w2_last[:], a["L1_ffn_w2"].rearrange("(c p) n -> p c n", p=P))
                load(k.b1_last[:], a["L1_ffn_b1"].rearrange("(c p) -> p c", p=P))
                load(k.b2_last[:], a["L1_ffn_b2"].partition_broadcast(P))
                load(k.wr_last[:], a["L1_ffn_wr"])
                load(k.br_last[:], a["L1_ffn_br"].partition_broadcast(P))
                sp.wait_ge(load_x, 16 * 4)
                sp.wait_ge(load_w, 16 * len(W_LOADS))

            @block.gpsimd
            def _(pool):
                pool.memset(k.ident[:], 0.0).then_inc(pool_made, 1)
                pool.wait_ge(pool_made, 1)
                pool.affine_select(out=k.ident[:], in_=k.ident[:], compare_op=ALU.not_equal, fill=1.0, base=0,
                                   pattern=[[-1, P]], channel_multiplier=1).then_inc(pool_made, 1)
                pool.memset(k.diag32[:], 0.0).then_inc(pool_made, 1)
                pool.wait_ge(pool_made, 3)
                for q in range(4):
                    pool.affine_select(out=k.diag32[:], in_=k.diag32[:], compare_op=ALU.not_equal, fill=1.0,
                                       base=-32 * q, pattern=[[-1, 32]], channel_multiplier=1).then_inc(pool_made, 1)
                    pool.wait_ge(pool_made, 4 + q)
                pool.memset(k.ones[:], 1.0).then_inc(ones_made, 1)
                pool.memset(tri_f[:], 1.0).then_inc(ones_made, 1)
                pool.wait_ge(ones_made, 2)
                pool.affine_select(out=k.tri[:], in_=tri_f[:], compare_op=ALU.is_gt, fill=0.0, base=0,
                                   pattern=[[1, P]], channel_multiplier=-1).then_inc(ones_made, 1)
                pool.memset(k.zeros[:], 0.0).then_inc(ones_made, 1)
                pool.wait_ge(ones_made, 4)

            @block.scalar
            def _(act):
                for q in range(4):
                    act.dma_start(k.x[:, 16 * q:16 * q + 16, :],
                                  a["x"][16 * q:16 * q + 16].rearrange("b t d -> t b d")).then_inc(load_x, 16)
                exp_ln_tables(nc, act)
                act.wait_ge(load_adj, 32)
                nc.scalar.activation(beta[:, 1:2], beta[:, 0:1], ACT.Abs).then_inc(act_s, 1)
                act.wait_ge(act_s, 1)
                nc.scalar.activation(beta[:, 2:3], beta[:, 1:2], ACT.Exp, scale=-1.0).then_inc(act_s, 1)
                act.wait_ge(act_s, 2)
                act.wait_ge(ones_made, 1)
                nc.scalar.activation(beta[:, 3:4], beta[:, 2:3], ACT.Ln, bias=k.ones[:, 0:1]).then_inc(act_s, 1)
                act.wait_ge(dve_s, 4)
                nc.scalar.activation(logw[:], adj_f[:], ACT.Ln, bias=k.eps_prior[:]).then_inc(act_s, 1)
                act.wait_ge(dve_s, 9)
                nc.scalar.activation(m_ij[:], logw[:], ACT.Exp, bias=row_stat[:, 0:1]).then_inc(act_s, 1)
                act.wait_ge(pe_t, 1)
                nc.scalar.copy(k.w_outT[:], tr[:, 2, 0:P]).then_inc(act_s, 1)
                act.wait_ge(act_s, 6)

            @block.vector
            def _(dve):
                n = [0]

                def chain(ins):
                    n[0] += 1
                    ins.then_inc(dve_s, 1)
                    dve.wait_ge(dve_s, n[0])

                dve.wait_ge(load_adj, 32)
                chain(dve.memset(k.eps_prior[:], EPS_PRIOR))
                dve.memset(k.neg_one[:], -1.0)
                chain(dve.memset(k.eps_ln[:], EPS_LN))
                chain(dve.tensor_copy(adj_f[:], adj_i[:]))
                chain(dve.tensor_scalar(adj_f[:], adj_f[:], 0.0, None, ALU.max))
                dve.wait_ge(act_s, 4)
                chain(dve.tensor_scalar(mask[:], adj_f[:], 0.0, None, ALU.is_gt))
                chain(dve.scalar_tensor_tensor(beta[:, 0:1], beta[:, 0:1], 0.0, beta[:, 3:4], ALU.max, ALU.add))
                chain(dve.tensor_scalar(k.cap[:], mask[:], BIG, -BIG, ALU.mult, ALU.add))
                chain(dve.scalar_tensor_tensor(logw[:], logw[:], beta[:, 0:1], k.cap[:], ALU.mult, ALU.add))
                chain(dve.tensor_reduce(row_stat[:, 0:1], logw[:], AX.X, ALU.max, negate=True))
                dve.wait_ge(act_s, 5)
                chain(dve.tensor_tensor(m_ij[:], m_ij[:], mask[:], ALU.mult))
                chain(dve.tensor_reduce(row_stat[:, 1:2], mask[:], AX.X, ALU.max))
                chain(dve.tensor_scalar(u_ij[:], mask[:], 0.0, row_stat[:, 1:2], ALU.mult, ALU.subtract))
                chain(dve.tensor_scalar(u_ij[:], u_ij[:], 1.0, None, ALU.add))
                chain(dve.tensor_scalar(k.cap[:], mask[:], BIG, NEG_INF_L1, ALU.mult, ALU.add))
                dve.wait_ge(pool_made, 7)
                for q in range(4):
                    rows = slice(32 * q, 32 * q + 32)
                    mine, other = (k.sel_s, k.sel_d) if q % 2 == 0 else (k.sel_d, k.sel_s)
                    dve.tensor_copy(mine[rows], k.diag32[rows].unsqueeze(2).to_broadcast([32, HB, P]))
                    dve.memset(other[rows], 0.0)
                dve.wait_ge(load_w, 16 * len(W_LOADS))
                chain(dve.tensor_tensor(wa_prod[:],
                                        k.w_heads[:, 0:D].rearrange("d (o h f) -> d o h f", o=1, h=HEADS)
                                        .to_broadcast([P, 2, HEADS, DH]), a_heads[:], ALU.mult))
                chain(dve.tensor_reduce(wa[:], wa_prod[:], AX.X, ALU.add))
                dve.tensor_copy(k.w_heads[:, D:D + 16], wa[:].rearrange("p t h -> p (t h)"))
                chain(dve.tensor_copy(k.w_heads[:, D + 16:D + 32], wa[:].rearrange("p t h -> p (t h)")))
                for c in range(2):
                    for t in range(2):
                        ins = dve.tensor_tensor(fold_p1[:, c, t], k.w_fc[:, c, 0:256], fold_a1[:, t], ALU.mult)
                chain(ins)
                chain(dve.tensor_reduce(fold_1[:], fold_p1[:], AX.X, ALU.add))
                for t in range(2):
                    ins = dve.tensor_tensor(fold_p2[:, t], k.w_hand[:, 0:D], fold_a2[:, t], ALU.mult)
                chain(ins)
                chain(dve.tensor_reduce(fold_2[:], fold_p2[:], AX.X, ALU.add))
                dve.tensor_copy(k.w_fc[:, :, 256:258], fold_1[:])
                dve.tensor_copy(k.w_hand[:, D:D + 2], fold_2[:])
                dve.tensor_copy(k.wr_rep[:], k.wr_last[:].to_broadcast([P, P]))
                dve.tensor_copy(k.w_f2_fc[:], fold_1[:, :, 1:2].to_broadcast([P, 2, P]))
                chain(dve.tensor_copy(k.w_f2_hand[:], fold_2[:, 1:2].to_broadcast([P, P])))
                dve.wait_ge(pe_t, 2)
                dve.tensor_copy(k.mT[:], tr[:, 0, 0:P])
                dve.tensor_scalar(k.neg_mT[:], tr[:, 0, 0:P], -1.0, None, ALU.mult)
                chain(dve.tensor_scalar(k.neg_uT[:], tr[:, 1, 0:P], -1.0, None, ALU.mult))
                dve.memset(k.v17[0][:, :, DH:VW], 1.0)
                chain(dve.memset(k.v17[1][:, :, DH:VW], 1.0))

            @block.tensor
            def _(pe):
                pe.wait_ge(pool_made, 2)
                pe.wait_ge(load_w, 16 * len(W_LOADS))
                pe.transpose(tr[:, 2, 0:P], w_out_in[:], k.ident[:]).then_inc(pe_t, 1)
                pe.wait_ge(dve_s, 13)
                pe.transpose(tr[:, 0, 0:P], m_ij[:], k.ident[:])
                pe.transpose(tr[:, 1, 0:P], u_ij[:], k.ident[:]).then_inc(pe_t, 1)


def head_attention_phase(nc, k):
    with ExitStack() as ctx:
        def sb(name, shape, dt=F32):
            return ctx.enter_context(nc.sbuf_tensor(name, shape, dt))

        def ps(name, shape):
            return ctx.enter_context(nc.psum_tensor(name, shape, F32))

        sems = PhaseSemaphores(nc, "l0_")
        sem = sems.make

        st = sb("l0_st", [P, GB, 6])
        mv = [sb(f"l0_mv{p}", [P, GB, 2]) for p in range(2)]
        lnv = sb("l0_lnv", [P, GB])
        rstd = [sb(f"l0_rstd{p}", [P, GB]) for p in range(2)]
        xn = sb("l0_xn", [P, GB, D])
        xnT = [sb(f"l0_xnT{p}", [P, GB * P]) for p in range(2)]
        sd = [sb(f"l0_sd{p}", [P, 4, GB, HEADS]) for p in range(2)]
        dmax = sb("l0_dmax", [P, 1])
        dmdiag = sb("l0_dmdiag", [P, HB])
        sparts = [sb(f"l0_sparts{p}", [P, P], BF16) for p in range(2)]
        fence = sb("l0_fence", [P, 1])
        pk = [sb(f"l0_pk{p}", [P, 4, HB]) for p in range(2)]
        us = sb("l0_us", [P, HB])
        bdfg = [sb(f"l0_bdfg{p}", [P, 4, HB]) for p in range(2)]
        vp = sb("l0_vp", [P, HB, 2 * VW])
        vres = sb("l0_vres", [P, HB, 2 * VW])
        vb = [sb(f"l0_vb{p}", [P, 3, HB, 2 * VW], BF16) for p in range(2)]
        mi = sb("l0_mi", [P, 2, HEADS, P], BF16)
        t1s = [sb(f"l0_t1{b}", [P, HEADS, VW]) for b in range(2)]
        t2s = [sb(f"l0_t2{b}", [P, HEADS, VW]) for b in range(2)]
        rdens = [sb(f"l0_rden{b}", [P, HEADS]) for b in range(2)]
        hn = [sb(f"l0_hn{p}", [P, GB, D]) for p in range(2)]
        hT = sb("l0_hT", [P, GB * P])

        tT = ps("l0_tT", [P, 512])
        vs = ps("l0_vs", [P, 2, 512])
        cc = ps("l0_cc", [P, 512])
        sbc = ps("l0_sbc", [P, 2, 512])
        oo = ps("l0_oo", [P, 512])
        yy = ps("l0_yy", [P, 512])

        names = ("stats", "var", "lnv_done", "rstd_ok", "xn_ok", "xT_ps", "xT_ok", "vs_ps", "vs_ok", "t_ps",
                 "hi_ok", "dg_self", "diag_ok", "dm_ps", "mid_ok", "sp_ok", "us_self", "pk_ok", "bdfg_ok",
                 "vp_ok", "vh_ok", "vr_ok", "vm_ok", "vb_ok", "s_ps", "mi_ok", "pv_ps", "o_read", "num_ok", "rden_ok",
                 "hn_ok", "hT_ps", "hT_ok", "y_ps", "x_ok")
        s = {n: sem(n) for n in names}

        def xs(g):
            return k.x[:, bass.ds(g * GB, GB), :]

        def dve_x_stats(dve, g, p):
            for b in range(GB):
                ins = dve.bn_stats(st[:, b, :], k.x[:, bass.ds(g * GB + b, 1), :].rearrange("p o d -> p (o d)"))
            ins.then_inc(s["stats"], 1)
            wait(dve, s["stats"], g + 1)
            dve.memset(fence[:], 0.0)
            for b in range(GB):
                ins = dve.bn_aggr(mv[p][:, b, :], st[:, b, :])
            ins.then_inc(s["var"], 1)

        def act_x_rstd(act, g, p):
            wait(act, s["var"], g + 1)
            nc.scalar.activation(lnv[:], mv[p][:, :, 1], ACT.Ln, bias=k.eps_ln[:]).then_inc(s["lnv_done"], 1)
            wait(act, s["lnv_done"], g + 1)
            nc.scalar.activation(rstd[p][:], lnv[:], ACT.Exp, scale=-0.5).then_inc(s["rstd_ok"], 1)

        def dve_x_apply(dve, g, p):
            wait(dve, s["rstd_ok"], g + 1)
            wait(dve, s["xT_ps"], g)
            for b in range(GB):
                ins = dve.tensor_scalar(xn[:, b:b + 1, :], k.x[:, bass.ds(g * GB + b, 1), :], mv[p][:, b, 0:1],
                                        rstd[p][:, b:b + 1], ALU.subtract, ALU.mult)
            ins.then_inc(s["xn_ok"], 1)

        def pe_x_transpose(pe, g, p):
            wait(pe, s["xn_ok"], g + 1)
            wait(pe, s["xT_ok"], g)
            wait(pe, s["hT_ok"], g - 3)
            for b in range(GB):
                ins = pe.transpose(tT[:, b * P:(b + 1) * P], xn[:, b, :], k.ident[:])
            ins.then_inc(s["xT_ps"], 1)

        def act_x_xT(act, g, p):
            wait(act, s["xT_ps"], g + 1)
            wait(act, s["vs_ps"], g - 1)
            nc.scalar.copy(xnT[p][:], tT[:]).then_inc(s["xT_ok"], 1)

        def pe_x_values(pe, g, p):
            wait(pe, s["xT_ok"], g + 1)
            wait(pe, s["vs_ok"], g)
            for b in range(GB):
                ins = pe.matmul(vs[:, b // 2, (b % 2) * 160:(b % 2) * 160 + 160], xnT[p][:, b * P:(b + 1) * P],
                                k.w_heads[:], start=(b % 2 == 0), stop=(b % 2 == 1), skip_group_check=True)
            ins.then_inc(s["vs_ps"], 1)

        def act_x_values(act, g, p):
            wait(act, s["vs_ps"], g + 1)
            wait(act, s["vb_ok"], g - 1)
            wait(act, s["pv_ps"], (g - 1) * GB)
            wait(act, s["pk_ok"], g - 1)
            for h in range(2):
                both = vs[:, h, 0:320].rearrange("p (b c) -> p b c", b=2)
                nc.scalar.copy(k.v17[p][:, 16 * h:16 * h + 16, 0:DH].rearrange("p (b h) f -> p b h f", b=2),
                               both[:, :, 0:D].rearrange("p b (h f) -> p b h f", h=HEADS))
                ins = nc.scalar.copy(sd[p][:, :, 2 * h:2 * h + 2, :].rearrange("p k b h -> p b k h"),
                                     both[:, :, D:160].rearrange("p b (k h) -> p b k h", k=4))
            ins.then_inc(s["vs_ok"], 1)

        def pe_y_transpose(pe, g, p):
            wait(pe, s["vs_ok"], g + 1)
            wait(pe, s["pk_ok"], g)
            pe.transpose(cc[:, 0:P], sd[p][:].rearrange("p k b h -> p (k b h)"), k.ident[:]).then_inc(s["t_ps"], 1)

        def act_y_hi(act, g, p):
            wait(act, s["t_ps"], g + 1)
            wait(act, s["s_ps"], (g - 1) * 2 * GB)
            nc.scalar.copy(sparts[p][:], cc[:, 0:P]).then_inc(s["hi_ok"], 1)

        def dve_y_max(dve, g, p):
            wait(dve, s["hi_ok"], g + 1)
            wait(dve, s["dm_ps"], g)
            dve.tensor_reduce(dmax[32:64, :], cc[32:64, 0:P], AX.X, ALU.max).then_inc(s["dg_self"], 1)
            dve.tensor_tensor(sparts[p][64:128, :], cc[64:128, 0:P], sparts[p][64:128, :], ALU.subtract)\
                .then_inc(s["sp_ok"], 1)
            wait(dve, s["dg_self"], g + 1)
            dve.tensor_scalar(dmdiag[32:64, :], k.diag32[32:64, :], dmax[32:64, :], None, ALU.mult)\
                .then_inc(s["diag_ok"], 1)

        def pe_y_maxima(pe, g, p):
            wait(pe, s["diag_ok"], g + 1)
            pe.matmul(cc[:, P:P + HB], k.ones[32:64, :], dmdiag[32:64, :], start=True, stop=True)\
                .then_inc(s["dm_ps"], 1)

        def dve_y_small(dve, g, p):
            wait(dve, s["dm_ps"], g + 1)
            wait(dve, s["bdfg_ok"], g - 1)
            s_i = sd[p][:, 0].rearrange("p b h -> p (b h)")
            d_j = sd[p][:, 1].rearrange("p b h -> p (b h)")
            dve.tensor_tensor(pk[p][:, 0], d_j, cc[:, P:P + HB], ALU.subtract)
            dve.tensor_tensor(us[:], cc[:, P:P + HB], s_i, ALU.add).then_inc(s["us_self"], 1)
            wait(dve, s["us_self"], g + 1)
            dve.tensor_scalar(pk[p][:, 1], pk[p][:, 0], 0.2, None, ALU.mult)
            dve.tensor_scalar(pk[p][:, 2], us[:], 0.8, 0.0, ALU.mult, ALU.min)
            dve.tensor_scalar(pk[p][:, 3], us[:], -0.8, 0.0, ALU.mult, ALU.min).then_inc(s["pk_ok"], 1)

        def act_y_exp(act, g, p):
            wait(act, s["pk_ok"], g + 1)
            wait(act, s["o_read"], (g - 1) * GB)
            nc.scalar.activation(bdfg[p][:], pk[p][:], ACT.Exp).then_inc(s["bdfg_ok"], 1)

        def pool_y_scale(pool, g, p):
            wait(pool, s["bdfg_ok"], g + 1)
            wait(pool, s["vh_ok"], g)
            pool.tensor_tensor(vp[:, :, 0:VW], k.v17[p][:], bdfg[p][:, 0].unsqueeze(2).to_broadcast([P, HB, VW]),
                               ALU.mult)
            pool.tensor_tensor(vp[:, :, VW:2 * VW], k.v17[p][:],
                               bdfg[p][:, 1].unsqueeze(2).to_broadcast([P, HB, VW]), ALU.mult).then_inc(s["vp_ok"], 1)

        def act_y_vhi(act, g, p):
            wait(act, s["vp_ok"], g + 1)
            wait(act, s["pv_ps"], (g - 1) * GB)
            nc.scalar.copy(vb[p][:, 0], vp[:]).then_inc(s["vh_ok"], 1)

        def pool_y_res(pool, g, p):
            wait(pool, s["vh_ok"], g + 1)
            wait(pool, s["vm_ok"], g)
            pool.tensor_tensor(vres[:], vp[:], vb[p][:, 0], ALU.subtract).then_inc(s["vr_ok"], 1)

        def act_y_vmid(act, g, p):
            wait(act, s["vr_ok"], g + 1)
            nc.scalar.copy(vb[p][:, 1], vres[:]).then_inc(s["vm_ok"], 1)

        def pool_y_lo(pool, g, p):
            wait(pool, s["vm_ok"], g + 1)
            pool.tensor_tensor(vb[p][:, 2], vres[:], vb[p][:, 1], ALU.subtract).then_inc(s["vb_ok"], 1)

        def pe_z_scores(pe, g, p, b):
            if b == 0:
                wait(pe, s["sp_ok"], g + 1)
            for h in range(2):
                wait(pe, s["mi_ok"], g * 2 * GB + 2 * b + h - 1)
                c = b * HEADS + 4 * h
                pe.matmul(sbc[:, h, :].rearrange("p (q i) -> p q i", q=4), sparts[p][:], k.sel_d[:, c:c + 4, :],
                          start=True, stop=False, skip_group_check=True)
                for q in range(4):
                    ins = pe.matmul(sbc[:, h, q * P:(q + 1) * P], k.sel_s[:, c + q, :], sparts[p][:],
                                    start=False, stop=(q == 3), skip_group_check=True)
                ins.then_inc(s["s_ps"], 1)

        def dve_z_compare(dve, g, p, b, h):
            wait(dve, s["s_ps"], g * 2 * GB + 2 * b + h + 1)
            if h == 0:
                wait(dve, s["pv_ps"], g * GB + b - 1)
            ins = dve.scalar_tensor_tensor(mi[:, b % 2, 4 * h:4 * h + 4, :],
                                           sbc[:, h, :].rearrange("p (q i) -> p q i", q=4), 0.0,
                                           k.mT[:].unsqueeze(1).to_broadcast([P, 4, P]), ALU.is_gt, ALU.mult)
            ins.then_inc(s["mi_ok"], 1)

        def pe_z_sums(pe, g, p, b):
            if b == 0:
                wait(pe, s["vb_ok"], g + 1)
            wait(pe, s["o_read"], g * GB + b)
            out = oo[:, 0:HEADS * 2 * VW].rearrange("p (h c) -> p h c", h=HEADS)
            rows = slice(b * HEADS, (b + 1) * HEADS)
            for part in range(3):
                pe.matmul(out[:, :, VW:2 * VW], k.neg_mT[:], vb[p][:, part, rows, VW:2 * VW],
                          start=(part == 0), stop=False, skip_group_check=True)
            pe.matmul(out[:, :, VW:2 * VW], k.neg_uT[:], k.v17[p][:, rows, :], start=False, stop=False,
                      skip_group_check=True)
            for h in range(HEADS):
                if h % 4 == 0:
                    wait(pe, s["mi_ok"], g * 2 * GB + 2 * b + h // 4 + 1)
                for part in range(3):
                    ins = pe.matmul(out[:, h, :], mi[:, b % 2, h, :], vb[p][:, part, b * HEADS + h, :],
                                    start=False, stop=(h == HEADS - 1 and part == 2), skip_group_check=True)
            ins.then_inc(s["pv_ps"], 1)

        def dve_z_post(dve, g, p, b):
            rows = slice(b * HEADS, (b + 1) * HEADS)
            out = oo[:, 0:HEADS * 2 * VW].rearrange("p (h c) -> p h c", h=HEADS)
            t1, t2 = t1s[b % 2], t2s[b % 2]
            wait(dve, s["hn_ok"], g * GB + b - 1)
            wait(dve, s["pv_ps"], g * GB + b + 1)
            dve.tensor_tensor(t1[:], out[:, :, 0:VW],
                              bdfg[p][:, 2, rows].unsqueeze(2).to_broadcast([P, HEADS, VW]), ALU.mult)
            dve.tensor_tensor(t2[:], out[:, :, VW:2 * VW],
                              bdfg[p][:, 3, rows].unsqueeze(2).to_broadcast([P, HEADS, VW]), ALU.mult)\
                .then_inc(s["o_read"], 1)

        def pool_z_post(pool, g, p, b):
            n = g * GB + b
            t1, t2, rden = t1s[b % 2], t2s[b % 2], rdens[b % 2]
            wait(pool, s["o_read"], n + 1)
            pool.tensor_tensor(t1[:], t1[:], t2[:], ALU.subtract).then_inc(s["num_ok"], 1)
            if b == 0:
                wait(pool, s["hT_ps"], g - 1)
            wait(pool, s["rden_ok"], n + 1)
            pool.tensor_tensor(hn[p][:, b, :].rearrange("p (h f) -> p h f", h=HEADS), t1[:, :, 0:DH],
                               rden[:].unsqueeze(2).to_broadcast([P, HEADS, DH]), ALU.mult).then_inc(s["hn_ok"], 1)

        def dve_z_rden(dve, g, p, b):
            n = g * GB + b
            wait(dve, s["num_ok"], n + 1)
            dve.reciprocal(rdens[b % 2][:], t1s[b % 2][:, :, DH]).then_inc(s["rden_ok"], 1)

        def pe_w_transpose(pe, g, p):
            wait(pe, s["hn_ok"], (g + 1) * GB)
            wait(pe, s["xT_ok"], min(g + 4, GROUPS) if isinstance(g, int) else g + 4)
            for b in range(GB):
                ins = pe.transpose(tT[:, b * P:(b + 1) * P], hn[p][:, b, :], k.ident[:])
            ins.then_inc(s["hT_ps"], 1)

        def act_w_hT(act, g, p):
            wait(act, s["hT_ps"], g + 1)
            wait(act, s["y_ps"], g)
            nc.scalar.copy(hT[:], tT[:]).then_inc(s["hT_ok"], 1)

        def pe_w_project(pe, g, p):
            wait(pe, s["hT_ok"], g + 1)
            wait(pe, s["x_ok"], g)
            for b in range(GB):
                ins = pe.matmul(yy[:, b * P:(b + 1) * P], hT[:, b * P:(b + 1) * P], k.w_outT[:],
                                start=(b == 0), stop=(b == GB - 1), skip_group_check=True)
            ins.then_inc(s["y_ps"], 1)

        def dve_w_add(dve, g, p):
            wait(dve, s["y_ps"], g + 1)
            dve.scalar_tensor_tensor(xs(g), yy[:].rearrange("p (b d) -> p b d", b=GB), 1.0, xs(g),
                                     ALU.mult, ALU.add).then_inc(s["x_ok"], 1)

        def pe_slot(pe, g, p, on):
            q = 1 - p
            if on["x"]:
                pe_x_transpose(pe, g + 2, p)
            if on["z"]:
                pe_z_scores(pe, g, p, 0)
            if on["y"]:
                pe_y_transpose(pe, g + 1, q)
            if on["z"]:
                pe_z_scores(pe, g, p, 1)
                pe_z_sums(pe, g, p, 0)
            if on["w"]:
                pe_w_transpose(pe, g - 1, q)
            if on["y"]:
                pe_y_maxima(pe, g + 1, q)
            if on["x"]:
                pe_x_values(pe, g + 2, p)
            if on["z"]:
                pe_z_scores(pe, g, p, 2)
                pe_z_sums(pe, g, p, 1)
            if on["w"]:
                pe_w_project(pe, g - 1, q)
            if on["z"]:
                pe_z_scores(pe, g, p, 3)
                pe_z_sums(pe, g, p, 2)
                pe_z_sums(pe, g, p, 3)

        def dve_slot(dve, g, p, on):
            q = 1 - p
            if on["z"]:
                dve_z_compare(dve, g, p, 0, 0)
            if on["w"]:
                dve_z_rden(dve, g - 1, q, 3)
            if on["y"]:
                dve_y_max(dve, g + 1, q)
            if on["z"]:
                dve_z_compare(dve, g, p, 0, 1)
                dve_z_compare(dve, g, p, 1, 0)
            if on["y"]:
                dve_y_small(dve, g + 1, q)
            if on["z"]:
                dve_z_post(dve, g, p, 0)
                dve_z_compare(dve, g, p, 1, 1)
                dve_z_rden(dve, g, p, 0)
                dve_z_compare(dve, g, p, 2, 0)
            if on["n"]:
                dve_x_stats(dve, g + 3, q)
            if on["z"]:
                dve_z_post(dve, g, p, 1)
                dve_z_compare(dve, g, p, 2, 1)
                dve_z_rden(dve, g, p, 1)
                dve_z_compare(dve, g, p, 3, 0)
            if on["w"]:
                dve_w_add(dve, g - 1, q)
            if on["z"]:
                dve_z_post(dve, g, p, 2)
                dve_z_compare(dve, g, p, 3, 1)
                dve_z_rden(dve, g, p, 2)
            if on["n"]:
                dve_x_apply(dve, g + 3, q)
            if on["z"]:
                dve_z_post(dve, g, p, 3)

        def act_slot(act, g, p, on):
            q = 1 - p
            if on["y"]:
                act_x_values(act, g + 1, q)
                act_y_hi(act, g + 1, q)
            if on["x"]:
                act_x_xT(act, g + 2, p)
            if on["w"]:
                act_w_hT(act, g - 1, q)
            if on["y"]:
                act_y_exp(act, g + 1, q)
                act_y_vhi(act, g + 1, q)
            if on["n"]:
                act_x_rstd(act, g + 3, q)
            if on["y"]:
                act_y_vmid(act, g + 1, q)

        def pool_slot(pool, g, p, on):
            q = 1 - p
            if on["w"]:
                pool_z_post(pool, g - 1, q, 3)
            if on["y"]:
                pool_y_scale(pool, g + 1, q)
            if on["z"]:
                pool_z_post(pool, g, p, 0)
            if on["y"]:
                pool_y_res(pool, g + 1, q)
            if on["z"]:
                pool_z_post(pool, g, p, 1)
            if on["y"]:
                pool_y_lo(pool, g + 1, q)
            if on["z"]:
                pool_z_post(pool, g, p, 2)

        def slots(slot, eng):
            def on(g):
                return dict(w=g - 1 >= 0, z=0 <= g < GROUPS, y=0 <= g + 1 < GROUPS,
                                       x=0 <= g + 2 < GROUPS, n=0 <= g + 3 < GROUPS)
            everything = dict(w=True, z=True, y=True, x=True, n=True)
            first, last = 2, GROUPS - 4
            for g in range(-2, first):
                slot(eng, g, g % 2, on(g))
            with eng.Fori(first // 2, last // 2) as i:
                for p in range(2):
                    slot(eng, i * 2 + p, p, everything)
            for g in range(last, GROUPS + 1):
                slot(eng, g, g % 2, on(g))

        with nc.Block() as block:
            @block.sync
            def _(sp):
                rows = k.rows_in.rearrange("(p n) d -> p (n d)", p=P)
                for c in range(k.zero_dmas):
                    sp.dma_start(rows[:, 2048 * c:2048 * c + 2048], k.zeros[:]).then_inc(k.slots_zeroed, 16)
                sp.wait_ge(k.slots_zeroed, 16 * k.zero_dmas)

            @block.vector
            def _(dve):
                dve_x_stats(dve, 0, 0)
                dve_x_apply(dve, 0, 0)
                slots(dve_slot, dve)

            @block.scalar
            def _(act):
                exp_ln_tables(nc, act)
                act_x_rstd(act, 0, 0)
                slots(act_slot, act)

            @block.gpsimd
            def _(pool):
                slots(pool_slot, pool)

            @block.tensor
            def _(pe):
                slots(pe_slot, pe)
        sems.clear()


def persistent(nc, ctx):
    def sb(name, shape, dt=F32):
        return ctx.enter_context(nc.sbuf_tensor(name, shape, dt))
    k = Buffers()
    k.x = sb("x_tok", [P, BATCHES, D])
    k.ident = sb("ident", [P, P])
    k.ones = sb("ones", [P, P])
    k.tri = sb("tri", [P, P])
    k.cap = sb("cap", [P, P])
    k.eps_ln = sb("eps_ln", [P, 1])
    k.eps_prior = sb("eps_prior", [P, 1])
    k.neg_one = sb("neg_one", [P, 1])
    k.w_fc = sb("w_fc", [P, 2, 258])
    k.w_hand = sb("w_hand", [P, D + 2])
    k.w_f2_fc = sb("w_f2_fc", [P, 2, P])
    k.w_f2_hand = sb("w_f2_hand", [P, P])
    k.w_mlp1 = sb("w_mlp1", [P, 256])
    k.w_mlp2 = sb("w_mlp2", [P, 2, D])
    k.b_mlp1 = sb("b_mlp1", [P, 2])
    k.b_mlp2 = sb("b_mlp2", [P, 1])
    k.w_router = sb("w_router", [P, 8])
    k.w1_shared = sb("w1_shared", [P, 512])
    k.w2_shared = sb("w2_shared", [P, 4, D])
    k.b1_shared = sb("b1_shared", [P, 4])
    k.b2_shared = sb("b2_shared", [P, D])
    k.w1_last = sb("w1_last", [P, 512])
    k.w2_last = sb("w2_last", [P, 4, D])
    k.b1_last = sb("b1_last", [P, 4])
    k.b2_last = sb("b2_last", [P, D])
    k.wr_last = sb("wr_last", [P, 1])
    k.br_last = sb("br_last", [P, 1])
    k.wr_rep = sb("wr_rep", [P, P])
    k.mean_var = sb("mean_var", [P, BATCHES, 2])
    k.slots = sb("slots", [P, 2, BATCHES], I32)
    k.weights = sb("weights", [P, 2, BATCHES])
    k.tile_expert = sb("tile_expert", [1, 72], I32)
    k.rows_in = nc.dram_tensor("slot_rows_in", [72 * 256, D], F32, kind="Internal").ap()
    k.rows_out = nc.dram_tensor("slot_rows_out", [72 * 256, D], F32, kind="Internal").ap()
    k.slots_zeroed = ctx.enter_context(nc.semaphore("slots_zeroed"))
    k.zero_dmas = 9
    k.expert_dmas = 32
    k.experts_loaded = ctx.enter_context(nc.semaphore("experts_loaded"))
    return k


def add_attention_buffers(nc, ctx, k):
    def sb(name, shape, dt=F32):
        return ctx.enter_context(nc.sbuf_tensor(name, shape, dt))
    k.diag32, k.zeros = sb("diag32", [P, 32]), sb("zeros", [P, 2048])
    k.sel_s, k.sel_d = sb("sel_s", [P, HB, P], BF16), sb("sel_d", [P, HB, P], BF16)
    k.mT, k.neg_mT, k.neg_uT = sb("mT", [P, P], BF16), sb("neg_mT", [P, P], BF16), sb("neg_uT", [P, P])
    k.w_heads, k.w_outT = sb("w_heads", [P, D + 32]), sb("w_outT", [P, D])
    k.v17 = [sb(f"v17_{p}", [P, HB, VW]) for p in range(2)]


def add_expert_buffers(nc, ctx, k):
    def sb(name, shape, dt=F32):
        return ctx.enter_context(nc.sbuf_tensor(name, shape, dt))
    k.xn, k.xnT = sb("xn_all", [P, BATCHES, D]), sb("xnT_all", [P, BATCHES, P])
    k.w_experts = sb("w_experts", [P, 8, 1024 + 4 + 128])


EXPERTS, F, FC = 8, 512, 4
TOPK = 2
TILE = 256
TILES = -(-(TOPK * BATCHES * TOKENS // TILE + EXPERTS - 1) // 2) * 2
SLOTS = TILES * TILE
MAX_TILES_OF_ONE = BATCHES * TOKENS // TILE
FETCHED = F + FC + D
EW = FETCHED + F


def layer_norm_stats(dve, x_of, st, mv, fence, stats, n_stats, var):
    for b in range(GB):
        ins = dve.bn_stats(st[:, b, :], x_of(b))
    ins.then_inc(stats, 1)
    wait(dve, stats, n_stats)
    dve.memset(fence[:], 0.0)
    for b in range(GB):
        ins = dve.bn_aggr(mv[:, b, :], st[:, b, :])
    ins.then_inc(var, 1)


def router_phase(nc, k, a):
    with ExitStack() as ctx:
        def sb(name, shape, dt=F32):
            return ctx.enter_context(nc.sbuf_tensor("r_" + name, shape, dt))

        def ps(name, shape):
            return ctx.enter_context(nc.psum_tensor("r_" + name, shape, F32))

        def sem(name):
            return ctx.enter_context(nc.semaphore("r_" + name))

        st = [sb(f"st{p}", [P, GB, 6]) for p in range(2)]
        mv = [sb(f"mv{p}", [P, GB, 2]) for p in range(2)]
        fence = sb("fence", [P, 1])
        lnv = [sb(f"lnv{p}", [P, GB]) for p in range(2)]
        rstd = [sb(f"rstd{p}", [P, GB]) for p in range(2)]
        xn = [sb(f"xn{p}", [P, GB, D]) for p in range(2)]
        xnT = [sb(f"xnT{p}", [P, GB * P]) for p in range(2)]
        BE = [P, BATCHES, EXPERTS]
        logits, cand, left = sb("logits", BE), sb("cand", BE), sb("left", BE)
        first, second, both = sb("first", BE), sb("second", BE), sb("both", BE)
        top = sb("top", [P, 2, BATCHES])
        which = sb("which", [P, 2, BATCHES])
        em8 = sb("em8", [P, EXPERTS])
        k256 = sb("k256", [P, MAX_TILES_OF_ONE])
        tiles_i = sb("tiles_i", [P, TILES])
        tot_b = sb("tot_b", [BATCHES, EXPERTS])
        prefix_rhs = sb("prefix_rhs", [BATCHES, BATCHES, EXPERTS])
        total = sb("total", [P, EXPERTS])
        over = sb("over", [P, EXPERTS, MAX_TILES_OF_ONE])
        n_tiles, end, base = sb("n_tiles", [P, EXPERTS]), sb("end", [P, EXPERTS]), sb("base", [P, EXPERTS])
        upto = sb("upto", [P, EXPERTS, EXPERTS])
        slot_f = sb("slot_f", [P, 2, BATCHES])
        past = sb("past", [1, TILES, EXPERTS])
        tile_e = sb("tile_e", [1, TILES])

        tT = [ps(f"tT{p}", [P, 512]) for p in range(2)]
        lg = [ps(f"lg{p}", [P, GB * EXPERTS]) for p in range(2)]
        prefix = ps("prefix", [P, BATCHES * EXPERTS])
        counts = ps("counts", [P, 512])

        s = {n: sem(n) for n in (
            "stats", "var", "lnv_done", "rstd_ok", "xn_ok", "xT_ps", "xT_ok", "lg_ps", "lg_ok", 
            "iota", "d", "e", "tot_ps", "pre_ps")}
        kept = [sem(f"kept{p}") for p in range(2)]

        def dve_norm(dve, g, p):
            layer_norm_stats(dve, lambda b: k.x[:, bass.ds(g * GB + b, 1), :].rearrange("p o d -> p (o d)"),
                             st[p], mv[p], fence, s["stats"], g + 1, s["var"])

        def dve_apply(dve, g, half, p):
            wait(dve, s["rstd_ok"], g + 1)
            wait(dve, s["xT_ps"], g - 1)
            wait(dve, kept[p], half * 32)
            for b in range(GB):
                ins = dve.tensor_scalar(xn[p][:, b:b + 1, :], k.x[:, bass.ds(g * GB + b, 1), :], mv[p][:, b, 0:1],
                                        rstd[p][:, b:b + 1], ALU.subtract, ALU.mult)
            ins.then_inc(s["xn_ok"], 1)

        def dve_logits(dve, g, p):
            wait(dve, s["lg_ps"], g + 1)
            dve.tensor_scalar(logits[:, bass.ds(g * GB, GB), :],
                              lg[p][:].rearrange("p (b e) -> p b e", b=GB), 1.0, None, ALU.mult).then_inc(s["lg_ok"], 1)

        def act_rstd(act, g, p):
            wait(act, s["var"], g + 1)
            wait(act, s["xn_ok"], g - 1)
            nc.scalar.activation(lnv[p][:], mv[p][:, :, 1], ACT.Ln, bias=k.eps_ln[:]).then_inc(s["lnv_done"], 1)
            wait(act, s["lnv_done"], g + 1)
            nc.scalar.activation(rstd[p][:], lnv[p][:], ACT.Exp, scale=-0.5).then_inc(s["rstd_ok"], 1)

        def act_xT(act, g, half, p):
            wait(act, s["xT_ps"], g + 1)
            wait(act, s["lg_ps"], g - 1)
            wait(act, kept[p], half * 32)
            nc.scalar.copy(xnT[p][:], tT[p][:]).then_inc(s["xT_ok"], 1)

        def pe_transpose(pe, g, p):
            wait(pe, s["xn_ok"], g + 1)
            wait(pe, s["xT_ok"], g - 1)
            for b in range(GB):
                ins = pe.transpose(tT[p][:, b * P:(b + 1) * P], xn[p][:, b, :], k.ident[:])
            ins.then_inc(s["xT_ps"], 1)

        def pe_logits(pe, g, p):
            wait(pe, s["xT_ok"], g + 1)
            wait(pe, s["lg_ok"], g - 1)
            for b in range(GB):
                ins = pe.matmul(lg[p][:, b * EXPERTS:(b + 1) * EXPERTS], xnT[p][:, b * P:(b + 1) * P], k.w_router[:],
                                start=(b == 0), stop=(b == GB - 1), skip_group_check=True)
            ins.then_inc(s["lg_ps"], 1)

        def pool_keep(pool, g, p):
            wait(pool, s["xn_ok"], g + 1)
            pool.dma_start(k.xn[:, bass.ds(g * GB, GB), :], xn[p][:]).then_inc(kept[p], 16)
            wait(pool, s["xT_ok"], g + 1)
            pool.dma_start(k.xnT[:, bass.ds(g * GB, GB), :],
                         xnT[p][:].rearrange("p (b t) -> p b t", b=GB)).then_inc(kept[p], 16)

        def skewed(slot, eng, before, after):
            first = 2
            last = (GROUPS - before) // 2 * 2
            for g in range(-before, first):
                slot(eng, g, g // 2, g % 2)
            with eng.Fori(first // 2, last // 2) as i:
                for p in range(2):
                    slot(eng, i * 2 + p, i, p)
            for g in range(last, GROUPS + after):
                slot(eng, g, g // 2, g % 2)

        def runs(g):
            return not isinstance(g, int) or 0 <= g < GROUPS

        def dve_slot(dve, g, half, p):
            if runs(g + 2):
                dve_norm(dve, g + 2, p)
            if runs(g + 1):
                dve_apply(dve, g + 1, half + p, 1 - p)
            if runs(g):
                dve_logits(dve, g, p)

        def act_slot(act, g, half, p):
            if runs(g + 2):
                act_rstd(act, g + 2, p)
            if runs(g):
                act_xT(act, g, half, p)

        def pe_slot(pe, g, half, p):
            if runs(g):
                pe_transpose(pe, g, p)
                pe_logits(pe, g, p)

        def pool_slot(pool, g, half, p):
            if runs(g):
                pool_keep(pool, g, p)

        def over_experts(ap):
            return ap.unsqueeze(2).to_broadcast(BE)

        with nc.Block() as block:
            @block.sync
            def _(sp):
                for e in range(EXPERTS):
                    def load(dst, src):
                        sp.dma_start(dst, src, allow_slow_non_contiguous=True).then_inc(k.experts_loaded, 16)
                    load(k.w_experts[:, e, 0:F], a["L0_ffn_W1p"][e])
                    load(k.w_experts[:, e, F:F + FC], a["L0_ffn_b1p"][e].rearrange("(c p) -> p c", p=P))
                    load(k.w_experts[:, e, F + FC:FETCHED], a["L0_ffn_b2p"][e].partition_broadcast(P))
                    load(k.w_experts[:, e, FETCHED:EW].rearrange("p (c n) -> p c n", c=FC),
                         a["L0_ffn_W2p"][e].rearrange("(c p) n -> p c n", p=P))

            @block.gpsimd
            def _(pool):
                pool.iota(em8[:], [[1, EXPERTS]], base=-EXPERTS, channel_multiplier=0,
                          allow_small_or_imprecise_dtypes=True)
                pool.iota(k256[:], [[TILE, MAX_TILES_OF_ONE]], base=0, channel_multiplier=0,
                          allow_small_or_imprecise_dtypes=True)
                pool.iota(tiles_i[:], [[1, TILES]], base=0, channel_multiplier=0,
                          allow_small_or_imprecise_dtypes=True).then_inc(s["iota"], 1)
                skewed(pool_slot, pool, 2, 0)
                for p in range(2):
                    pool.wait_ge(kept[p], GROUPS * 16)

            @block.scalar
            def _(act):
                exp_ln_tables(nc, act)
                skewed(act_slot, act, 2, 0)
                act.wait_ge(s["d"], 11)
                nc.scalar.activation(top[:, 1], which[:, 0], ACT.Exp).then_inc(s["e"], 1)

            @block.tensor
            def _(pe):
                skewed(pe_slot, pe, 2, 0)
                pe.wait_ge(s["d"], 10)
                for e in range(EXPERTS):
                    pe.matmul(counts[0:BATCHES, e:e + 1], both[:, :, e], k.ones[:, 0:1], start=(e == 0),
                              stop=(e == EXPERTS - 1), skip_group_check=True)
                pe.matmul(prefix[:], k.tri[:], both[:].rearrange("p b e -> p (b e)"), start=True, stop=False,
                          skip_group_check=True).then_inc(s["tot_ps"], 1)
                pe.wait_ge(s["d"], 16)
                pe.matmul(prefix[:], k.ones[0:BATCHES, :], prefix_rhs[:].rearrange("p b e -> p (b e)"),
                          start=False, stop=True, skip_group_check=True)
                pe.matmul(counts[:, 64:64 + EXPERTS], k.ones[0:BATCHES, :], tot_b[:], start=True, stop=True)\
                    .then_inc(s["pre_ps"], 1)

            @block.vector
            def _(dve):
                skewed(dve_slot, dve, 2, 0)
                n = [0]

                def chain(ins):
                    n[0] += 1
                    ins.then_inc(s["d"], 1)
                    dve.wait_ge(s["d"], n[0])

                dve.wait_ge(s["lg_ok"], GROUPS)
                dve.wait_ge(s["iota"], 1)
                e_of = em8[:].unsqueeze(1).to_broadcast(BE)
                chain(dve.tensor_reduce(top[:, 0], logits[:], AX.X, ALU.max))
                chain(dve.tensor_tensor(cand[:], logits[:], over_experts(top[:, 0]), ALU.is_equal))
                chain(dve.tensor_tensor(cand[:], cand[:], e_of, ALU.mult))
                chain(dve.tensor_reduce(which[:, 0], cand[:], AX.X, ALU.min))
                chain(dve.tensor_tensor(first[:], over_experts(which[:, 0]), e_of, ALU.is_equal))
                chain(dve.scalar_tensor_tensor(left[:], first[:], -BIG, logits[:], ALU.mult, ALU.add))
                dve.tensor_reduce(top[:, 1], left[:], AX.X, ALU.max).then_inc(s["e"], 1)
                dve.wait_ge(s["e"], 1)
                chain(dve.tensor_tensor(cand[:], left[:], over_experts(top[:, 1]), ALU.is_equal))
                dve.tensor_tensor(cand[:], cand[:], e_of, ALU.mult).then_inc(s["e"], 1)
                dve.wait_ge(s["e"], 2)
                chain(dve.tensor_reduce(which[:, 1], cand[:], AX.X, ALU.min))
                chain(dve.tensor_tensor(second[:], over_experts(which[:, 1]), e_of, ALU.is_equal))
                chain(dve.tensor_tensor(both[:], first[:], second[:], ALU.add))
                chain(dve.tensor_tensor(which[:, 0], top[:, 1], top[:, 0], ALU.subtract))
                dve.wait_ge(s["e"], 3)
                chain(dve.tensor_scalar(top[:, 0], top[:, 1], 1.0, None, ALU.add))
                chain(dve.reciprocal(k.weights[:, 0], top[:, 0]))
                chain(dve.tensor_tensor(k.weights[:, 1], top[:, 1], k.weights[:, 0], ALU.mult))
                dve.wait_ge(s["tot_ps"], 1)
                chain(dve.tensor_copy(tot_b[:], counts[0:BATCHES, 0:EXPERTS]))
                chain(dve.tensor_tensor(prefix_rhs[:],
                                        k.tri[0:BATCHES, 0:BATCHES].unsqueeze(2)
                                        .to_broadcast([BATCHES, BATCHES, EXPERTS]),
                                        tot_b[:].unsqueeze(1).to_broadcast([BATCHES, BATCHES, EXPERTS]),
                                        ALU.mult))
                dve.wait_ge(s["pre_ps"], 1)
                chain(dve.tensor_copy(total[:], counts[:, 64:64 + EXPERTS]))
                OV = [P, EXPERTS, MAX_TILES_OF_ONE]
                chain(dve.tensor_tensor(over[:], total[:].unsqueeze(2).to_broadcast(OV),
                                        k256[:].unsqueeze(1).to_broadcast(OV), ALU.is_gt))
                chain(dve.tensor_reduce(n_tiles[:], over[:], AX.X, ALU.add))
                EE = [P, EXPERTS, EXPERTS]
                chain(dve.tensor_tensor(upto[:], em8[:].unsqueeze(2).to_broadcast(EE),
                                        em8[:].unsqueeze(1).to_broadcast(EE), ALU.is_ge))
                chain(dve.tensor_tensor(upto[:], upto[:], n_tiles[:].unsqueeze(1).to_broadcast(EE), ALU.mult))
                chain(dve.tensor_reduce(end[:], upto[:], AX.X, ALU.add))
                chain(dve.tensor_tensor(base[:], end[:], n_tiles[:], ALU.subtract))
                chain(dve.tensor_scalar(base[:], base[:], float(TILE), None, ALU.mult))
                chain(dve.tensor_tensor(left[:], prefix[:].rearrange("p (b e) -> p b e", b=BATCHES),
                                        base[:].unsqueeze(1).to_broadcast(BE), ALU.add))
                dve.tensor_tensor(first[:], first[:], left[:], ALU.mult)
                chain(dve.tensor_tensor(second[:], second[:], left[:], ALU.mult))
                dve.tensor_reduce(slot_f[:, 0], first[:], AX.X, ALU.add)
                chain(dve.tensor_reduce(slot_f[:, 1], second[:], AX.X, ALU.add))
                chain(dve.tensor_copy(k.slots[:], slot_f[:]))
                TE = [1, TILES, EXPERTS]
                chain(dve.tensor_tensor(past[:], tiles_i[0:1].unsqueeze(2).to_broadcast(TE),
                                        end[0:1].unsqueeze(1).to_broadcast(TE), ALU.is_ge))
                chain(dve.tensor_reduce(tile_e[:], past[:], AX.X, ALU.add))
                chain(dve.tensor_scalar(tile_e[:], tile_e[:], float(EXPERTS - 1), None, ALU.min))
                chain(dve.tensor_copy(k.tile_expert[:], tile_e[:]))


def shared_expert_phase(nc, k):
    with ExitStack() as ctx:
        def sb(name, shape, dt=F32):
            return ctx.enter_context(nc.sbuf_tensor("s_" + name, shape, dt))

        def ps(name, shape):
            return ctx.enter_context(nc.psum_tensor("s_" + name, shape, F32))

        def sem(name):
            return ctx.enter_context(nc.semaphore("s_" + name))

        hT = [sb(f"hT{p}", [P, FC, GB * P]) for p in range(2)]
        yb = [sb(f"yb{p}", [P, GB, D]) for p in range(2)]
        hp = ps("hp", [P, FC, 512])
        yp = [ps(f"yp{p}", [P, 512]) for p in range(2)]
        s = {n: sem(n) for n in ("h_ps", "h_ok", "y_ps", "y_read", "x_ok", "scattered")}

        def pe_up(pe, g, p):
            for c in range(FC):
                wait(pe, s["h_ok"], (g - 1) * FC + c + 1)
                pe.matmul(hp[:, c, :], k.w1_shared[:, c * P:(c + 1) * P],
                          k.xnT[:, bass.ds(g * GB, GB), :], start=True, stop=True).then_inc(s["h_ps"], 1)

        def pe_down(pe, g, p):
            wait(pe, s["y_read"], g - 1)
            for c in range(FC):
                wait(pe, s["h_ok"], g * FC + c + 1)
                for b in range(GB):
                    ins = pe.matmul(yp[p][:, b * P:(b + 1) * P], hT[p][:, c, b * P:(b + 1) * P], k.w2_shared[:, c, :],
                                    start=(c == 0 and b == 0), stop=(c == FC - 1), skip_group_check=True)
            ins.then_inc(s["y_ps"], 1)

        def act_gelu(act, g, p):
            wait(act, s["y_ps"], g - 1)
            for c in range(FC):
                wait(act, s["h_ps"], g * FC + c + 1)
                nc.scalar.activation(hT[p][:, c, :], hp[:, c, :], ACT.Gelu, bias=k.b1_shared[:, c:c + 1])\
                    .then_inc(s["h_ok"], 1)

        def dve_add(dve, g, p):
            wait(dve, s["y_ps"], g + 1)
            wait(dve, s["x_ok"], g - 1)
            dve.tensor_tensor(yb[p][:], yp[p][:].rearrange("p (b d) -> p b d", b=GB),
                              k.b2_shared[:].unsqueeze(1).to_broadcast([P, GB, D]), ALU.add).then_inc(s["y_read"], 1)
            wait(dve, s["y_read"], g + 1)
            xg = k.x[:, bass.ds(g * GB, GB), :]
            dve.tensor_tensor(xg, xg, yb[p][:], ALU.add).then_inc(s["x_ok"], 1)

        def paired(body, eng):
            for g in range(2):
                body(eng, g, g)
            with eng.Fori(1, GROUPS // 2) as i:
                for p in range(2):
                    body(eng, i * 2 + p, p)

        def pe_slot(pe, g, p):
            if not isinstance(g, int) or g + 1 < GROUPS:
                pe_up(pe, g + 1, 1 - p)
            pe_down(pe, g, p)

        with nc.Block() as block:
            @block.tensor
            def _(pe):
                pe_up(pe, 0, 0)
                for g in range(2):
                    pe_slot(pe, g, g)
                with pe.Fori(1, GROUPS // 2 - 1) as i:
                    for p in range(2):
                        pe_slot(pe, i * 2 + p, p)
                for g in range(GROUPS - 2, GROUPS):
                    pe_slot(pe, g, g % 2)

            @block.scalar
            def _(act):
                paired(act_gelu, act)

            @block.vector
            def _(dve):
                paired(dve_add, dve)

            @block.gpsimd
            def _(pool):
                pool.wait_ge(k.slots_zeroed, 16 * k.zero_dmas)
                for b in range(BATCHES):
                    for c in range(TOPK):
                        pool.indirect_dma_start(k.rows_in, bass.IndirectOffsetOnAxis(ap=k.slots[:, c, b:b + 1], axis=0),
                                                k.xn[:, b, :], None).then_inc(s["scattered"], 16)
                pool.wait_ge(s["scattered"], 16 * TOPK * BATCHES)


def routed_experts_phase(nc, k):
    with ExitStack() as ctx:
        def sb(name, shape, dt=F32):
            return ctx.enter_context(nc.sbuf_tensor("e_" + name, shape, dt))

        def ps(name, shape):
            return ctx.enter_context(nc.psum_tensor("e_" + name, shape, F32))

        def sem(name):
            return ctx.enter_context(nc.semaphore("e_" + name))

        H = TILE // P
        U = 4
        wt = [sb(f"wt{q}", [P, FETCHED]) for q in range(U)]
        xt = [sb(f"xt{q}", [P, H, D]) for q in range(U)]
        xT = [sb(f"xT{p}", [P, TILE]) for p in range(2)]
        hT = [sb(f"hT{p}", [P, FC, TILE]) for p in range(2)]
        yt = [sb(f"yt{q}", [P, H, D]) for q in range(U)]
        tp = ps("tp", [P, TILE])
        hp = [ps(f"hp{c}", [P, 512]) for c in range(FC)]
        yp = [ps(f"yp{p}", [P, H * D]) for p in range(2)]
        s = {n: sem(n) for n in ("tp_ps", "xT_ok", "h_ps", "h_ok", "y_ps", "y_ok")}
        w_in, x_in = [sem(f"w_in{q}") for q in range(U)], [sem(f"x_in{q}") for q in range(U)]
        out = [sem(f"out{q}") for q in range(U)]

        def expert_of(eng, t):
            return eng.value_load(k.tile_expert[0:1, bass.ds(t, 1)], min_val=0, max_val=EXPERTS - 1)

        def sp_load(sp, i, q):
            t = i * U + q
            wait(sp, s["tp_ps"], t - U + 1)
            wait(sp, s["y_ok"], t - U + 1)
            sp.dma_start(xt[q][:], k.rows_in[bass.ds(t * TILE, TILE), :].rearrange("(h p) d -> p h d", p=P))\
                .then_inc(x_in[q], 16)
            e = expert_of(sp, t)
            sp.dma_start(wt[q][:], k.w_experts[:, bass.ds(e, 1), 0:FETCHED].rearrange("p o n -> p (o n)"))\
                .then_inc(w_in[q], 16)

        def act_store(act, i, q):
            t = i * U + q
            wait(act, s["y_ok"], t + 1)
            act.dma_start(k.rows_out[bass.ds(t * TILE, TILE), :].rearrange("(h p) d -> p h d", p=P), yt[q][:])\
                .then_inc(out[q], 16)

        def pe_transpose(pe, i, q):
            t = i * U + q
            wait(pe, x_in[q], i * 16 + 16)
            wait(pe, s["xT_ok"], t)
            for h in range(H):
                ins = pe.transpose(tp[:, h * P:(h + 1) * P], xt[q][:, h, :], k.ident[:])
            ins.then_inc(s["tp_ps"], 1)

        def dve_xT(dve, i, q):
            t = i * U + q
            wait(dve, s["tp_ps"], t + 1)
            wait(dve, s["h_ps"], (t - 1) * FC)
            dve.tensor_copy(xT[q % 2][:], tp[:]).then_inc(s["xT_ok"], 1)

        def pe_up(pe, i, q):
            t = i * U + q
            wait(pe, w_in[q], i * 16 + 16)
            wait(pe, s["xT_ok"], t + 1)
            for c in range(FC):
                wait(pe, s["h_ok"], (t - 1) * FC + c + 1)
                pe.matmul(hp[c][:, 0:TILE], wt[q][:, c * P:(c + 1) * P], xT[q % 2][:], start=True, stop=True)\
                    .then_inc(s["h_ps"], 1)

        def act_gelu(act, i, q):
            t = i * U + q
            wait(act, s["y_ps"], t - 1)
            for c in range(FC):
                wait(act, s["h_ps"], t * FC + c + 1)
                nc.scalar.activation(hT[q % 2][:, c, :], hp[c][:, 0:TILE], ACT.Gelu,
                                     bias=wt[q][:, F + c:F + c + 1]).then_inc(s["h_ok"], 1)

        def pe_down(pe, i, q):
            t = i * U + q
            e = expert_of(pe, t)
            wait(pe, s["y_ok"], t - 1)
            for c in range(FC):
                wait(pe, s["h_ok"], t * FC + c + 1)
                w2 = k.w_experts[:, bass.ds(e, 1), FETCHED + c * D:FETCHED + (c + 1) * D]
                for h in range(H):
                    ins = pe.matmul(yp[q % 2][:, h * D:(h + 1) * D], hT[q % 2][:, c, h * P:(h + 1) * P], w2,
                                    start=(c == 0 and h == 0), stop=(c == FC - 1), skip_group_check=True)
            ins.then_inc(s["y_ps"], 1)

        def dve_bias(dve, i, q):
            t = i * U + q
            wait(dve, s["y_ps"], t + 1)
            wait(dve, out[q], i * 16)
            dve.tensor_tensor(yt[q][:], yp[q % 2][:].rearrange("p (h d) -> p h d", h=H),
                              wt[q][:, F + FC:FETCHED].unsqueeze(1).to_broadcast([P, H, D]), ALU.add)\
                .then_inc(s["y_ok"], 1)

        def ahead(i, q, n):
            return (i + (q + n) // U, (q + n) % U)

        def pe_slot(pe, i, q, more):
            if more > 1:
                pe_transpose(pe, *ahead(i, q, 2))
            if more > 0:
                pe_up(pe, *ahead(i, q, 1))
            pe_down(pe, i, q)

        def dve_slot(dve, i, q, more):
            if more > 1:
                dve_xT(dve, *ahead(i, q, 2))
            dve_bias(dve, i, q)

        def act_slot(act, i, q, more):
            if more > 0:
                act_gelu(act, *ahead(i, q, 1))
            act_store(act, i, q)

        def sp_slot(sp, i, q, more):
            if more >= U:
                sp_load(sp, i + 1, q)

        def tiles(slot, eng):
            for q in range(U):
                slot(eng, 0, q, U)
            with eng.Fori(1, TILES // U - 1) as i:
                for q in range(U):
                    slot(eng, i, q, U)
            for q in range(U):
                slot(eng, TILES // U - 1, q, U - 1 - q)

        with nc.Block() as block:
            @block.sync
            def _(sp):
                sp.wait_ge(k.experts_loaded, 16 * k.expert_dmas)
                for q in range(U):
                    sp_load(sp, 0, q)
                tiles(sp_slot, sp)

            @block.tensor
            def _(pe):
                pe.wait_ge(k.experts_loaded, 16 * k.expert_dmas)
                pe_transpose(pe, 0, 0)
                pe_up(pe, 0, 0)
                pe_transpose(pe, 0, 1)
                tiles(pe_slot, pe)

            @block.vector
            def _(dve):
                dve_xT(dve, 0, 0)
                dve_xT(dve, 0, 1)
                tiles(dve_slot, dve)

            @block.scalar
            def _(act):
                act_gelu(act, 0, 0)
                tiles(act_slot, act)
                for q in range(U):
                    act.wait_ge(out[q], 16 * (TILES // U))


H1, FD = 2, 2 * D
W1C = FD + 1
W2C = D + 1


def combine_graph_phase(nc, k):
    with ExitStack() as ctx:
        def sb(name, shape, dt=F32):
            return ctx.enter_context(nc.sbuf_tensor("g_" + name, shape, dt))

        def ps(name, shape):
            return ctx.enter_context(nc.psum_tensor("g_" + name, shape, F32))

        def sem(name):
            return ctx.enter_context(nc.semaphore("g_" + name))

        G4 = [P, GB, P]
        y_slot = [sb(f"y{c}", [P, BATCHES, D]) for c in range(TOPK)]
        st, fence, lnv = sb("st", [P, GB, 6]), sb("fence", [P, 1]), sb("lnv", [P, GB])
        mv = [sb(f"mv{p}", [P, GB, 2]) for p in range(2)]
        mv4 = sb("mv4", [P, GB, 2])
        rstd = [sb(f"rstd{p}", [P, GB]) for p in range(2)]
        xn, xT = sb("xn", G4), sb("xT", [P, GB * P])
        r1T = [sb(f"r1T{p}", [P, H1, GB * P]) for p in range(2)]
        h1 = [sb(f"h1{p}", [P, GB, W1C]) for p in range(2)]
        y1, e1, p1, pn1 = sb("sum1", G4), sb("e1", G4), sb("p1", G4), sb("pn1", G4)
        nmax1, den1, rden1 = sb("nmax1", [P, GB]), sb("den1", [P, GB]), sb("rden1", [P, GB])
        p1T = sb("p1T", [P, GB * P])
        v1, w1, t1, u1 = (sb(n, [P, H1, GB * P]) for n in ("v1", "w1", "t1", "u1"))
        r2T = [sb(f"r2T{p}", [P, GB * P]) for p in range(2)]
        h2 = sb("h2", [P, GB, W2C])
        y2, l2, e2, p2 = sb("sum2", G4), sb("l2", G4), sb("e2", G4), sb("p2", G4)
        nmax2, den2 = sb("nmax2", [P, GB]), sb("den2", [P, GB])
        rden2 = [sb(f"rden2{p}", [P, GB]) for p in range(2)]
        p2T = sb("p2T", [P, GB * P])
        q2, v2, w2, t2, s2 = (sb(n, G4) for n in ("q2", "v2", "w2", "t2", "s2"))

        tb = ps("tb", [P, 512])
        mm = ps("mm", [P, H1, 512])
        hh = ps("hh", [P, 2, 512])
        ff = ps("ff", [P, 512])
        rr = ps("rr", [P, 512])
        av = ps("av", [P, 512])

        s = {n: sem(n) for n in (
            "one_in", "comb", "stats", "var", "lnv_done", "rstd_ok", "xn_ok",
            "xT_ps", "xT_ok", "r1_ps", "r1_ok",
            "h1_ps", "h1_ok", "f1_ps", "y1_ok", "l1_ok", "max1_ok", "p1_ok", "rden1_ok", "pn1_ok", "p1T_ps", "p1T_ok",
            "av1_ps", "v1_ok", "v1_cut", "w1_ok", "t1_ok", "u1_ok", "r2_ps", "r2_ok",
            "h2_ps", "h2_ok", "f2_ps", "y2_ok", "l2_ok", "e2_ok", "max2_ok", "p2_ok", "rden2_ok", "p2T_ps", "p2T_ok",
            "r2T_ps", "av2_ps", "q2_ok", "v2_ok", "v2_cut", "w2_ok", "t2_ok", "s2_ok", "x_ok", "stats4", "var4", "kept4")}
        gathered = [sem(f"gathered{p}") for p in range(2)]
        PER_GROUP = 16 * TOPK * GB

        def full(count, g, ahead):
            return count(min(g + ahead, GROUPS - 1) + 1) if isinstance(g, int) else count(g + ahead + 1)

        def batch(ap, g, b):
            return ap[:, bass.ds(g * GB + b, 1), :]

        def pool_gather(pool, g, which):
            for n in which:
                if n == 0:
                    wait(pool, gathered[g % 2], PER_GROUP * (g // 2))
                b, c = g * GB + n // TOPK, n % TOPK
                pool.indirect_dma_start(y_slot[c][:, b, :], None, k.rows_out,
                                        bass.IndirectOffsetOnAxis(ap=k.slots[:, c, b:b + 1], axis=0))\
                    .then_inc(gathered[g % 2], 16)

        def dve_n_combine(dve, g, half, p):
            wait(dve, gathered[p], (half + 1) * PER_GROUP)
            for c in range(TOPK):
                for b in range(GB):
                    ins = dve.scalar_tensor_tensor(batch(k.x, g, b), batch(y_slot[c], g, b),
                                                   k.weights[:, c, bass.ds(g * GB + b, 1)], batch(k.x, g, b),
                                                   ALU.mult, ALU.add)
                if c == 0:
                    ins.then_inc(s["one_in"], 1)
                    wait(dve, s["one_in"], g + 1)
            ins.then_inc(s["comb"], 1)

        def dve_n_stats(dve, g, p):
            wait(dve, s["comb"], g + 1)
            dve.memset(fence[:], 0.0)
            layer_norm_stats(dve, lambda b: batch(k.x, g, b).rearrange("p o d -> p (o d)"),
                             st, mv[p], fence, s["stats"], g + 1, s["var"])

        def act_n_rstd(act, g, p):
            wait(act, s["var"], g + 1)
            nc.scalar.activation(lnv[:], mv[p][:, :, 1], ACT.Ln, bias=k.eps_ln[:]).then_inc(s["lnv_done"], 1)
            wait(act, s["lnv_done"], g + 1)
            nc.scalar.activation(rstd[p][:], lnv[:], ACT.Exp, scale=-0.5).then_inc(s["rstd_ok"], 1)

        def dve_n_apply(dve, g, p):
            wait(dve, s["xT_ps"], g)
            wait(dve, s["rstd_ok"], g + 1)
            for b in range(GB):
                ins = dve.tensor_scalar(xn[:, b:b + 1, :], batch(k.x, g, b), mv[p][:, b, 0:1],
                                        rstd[p][:, b:b + 1], ALU.subtract, ALU.mult)
            ins.then_inc(s["xn_ok"], 1)

        def pe_a_transpose(pe, g):
            wait(pe, s["xT_ok"], g)
            wait(pe, s["p1T_ok"], g - 1)
            wait(pe, s["xn_ok"], g + 1)
            for b in range(GB):
                ins = pe.transpose(tb[:, b * P:(b + 1) * P], xn[:, b, :], k.ident[:])
            ins.then_inc(s["xT_ps"], 1)

        def act_a_xT(act, g):
            wait(act, s["xT_ps"], g + 1)
            wait(act, s["r1_ps"], g * H1)
            nc.scalar.copy(xT[:], tb[:]).then_inc(s["xT_ok"], 1)

        def pe_a_dense(pe, g):
            wait(pe, s["t1_ok"], g - 1)
            wait(pe, s["r1_ok"], g * H1)
            wait(pe, s["xT_ok"], g + 1)
            for c in range(H1):
                pe.matmul(mm[:, c, :], k.w_mlp1[:, c * P:(c + 1) * P], xT[:], start=True, stop=True)\
                    .then_inc(s["r1_ps"], 1)

        def act_a_r1(act, g, p):
            wait(act, s["u1_ok"], g - 1)
            for c in range(H1):
                wait(act, s["r1_ps"], g * H1 + c + 1)
                nc.scalar.activation(r1T[p][:, c, :], mm[:, c, :], ACT.Relu, bias=k.b_mlp1[:, c:c + 1])\
                    .then_inc(s["r1_ok"], 1)

        def pe_b_h1(pe, g, p):
            wait(pe, s["r1_ok"], (g + 1) * H1)
            wait(pe, s["h2_ok"], g - 1)
            for b in range(GB):
                wait(pe, s["h1_ok"], g * GB + b - 1)
                for c in range(H1):
                    ins = pe.matmul(hh[:, b % 2, 0:W1C], r1T[p][:, c, b * P:(b + 1) * P], k.w_fc[:, c, 0:W1C],
                                    start=(c == 0), stop=(c == H1 - 1))
                ins.then_inc(s["h1_ps"], 1)

        def pe_b_f2(pe, g, p):
            wait(pe, s["y1_ok"], g)
            wait(pe, s["y2_ok"], g - 1)
            for c in range(H1):
                ins = pe.matmul(ff[:], k.w_f2_fc[:, c, :], r1T[p][:, c, :], start=(c == 0), stop=(c == H1 - 1))
            ins.then_inc(s["f1_ps"], 1)

        def act_b_h1(act, g, p, b):
            if b == 0:
                wait(act, s["av1_ps"], g - 1)
            wait(act, s["h1_ps"], g * GB + b + 1)
            nc.scalar.copy(h1[p][:, b, :], hh[:, b % 2, 0:W1C]).then_inc(s["h1_ok"], 1)

        def act_b_sum(act, g, p):
            wait(act, s["l1_ok"], g)
            wait(act, s["h1_ok"], (g + 1) * GB)
            wait(act, s["f1_ps"], g + 1)
            for b in range(GB):
                ins = nc.scalar.activation(y1[:, b, :], ff[:, b * P:(b + 1) * P], ACT.Identity,
                                           bias=h1[p][:, b, FD:W1C])
            ins.then_inc(s["y1_ok"], 1)

        def dve_b_leaky(dve, g):
            wait(dve, s["p1_ok"], g)
            wait(dve, s["y1_ok"], g + 1)
            dve.scalar_tensor_tensor(e1[:], y1[:], 0.2, y1[:], ALU.mult, ALU.max).then_inc(s["l1_ok"], 1)
            wait(dve, s["l1_ok"], g + 1)
            dve.tensor_reduce(nmax1[:], e1[:], AX.X, ALU.max, negate=True).then_inc(s["max1_ok"], 1)

        def act_b_exp(act, g):
            wait(act, s["pn1_ok"], g)
            wait(act, s["max1_ok"], g + 1)
            for b in range(GB):
                ins = nc.scalar.activation(p1[:, b, :], e1[:, b, :], ACT.Exp, bias=nmax1[:, b:b + 1],
                                           accum_out=den1[:, b:b + 1])
            ins.then_inc(s["p1_ok"], 1)

        def dve_b_rden(dve, g):
            wait(dve, s["p1_ok"], g + 1)
            dve.reciprocal(rden1[:], den1[:]).then_inc(s["rden1_ok"], 1)

        def pool_b_scale(pool, g):
            wait(pool, s["p1T_ps"], g)
            wait(pool, s["rden1_ok"], g + 1)
            pool.tensor_tensor(pn1[:], p1[:], rden1[:].unsqueeze(2).to_broadcast(G4), ALU.mult).then_inc(s["pn1_ok"], 1)

        def pe_b_transpose(pe, g):
            wait(pe, s["xT_ok"], full(lambda n: n, g, 1))
            wait(pe, s["p2T_ok"], g - 1)
            wait(pe, s["p1T_ok"], g)
            wait(pe, s["pn1_ok"], g + 1)
            for b in range(GB):
                ins = pe.transpose(tb[:, b * P:(b + 1) * P], pn1[:, b, :], k.ident[:])
            ins.then_inc(s["p1T_ps"], 1)

        def dve_b_p1T(dve, g):
            wait(dve, s["av1_ps"], g)
            wait(dve, s["p1T_ps"], g + 1)
            dve.tensor_copy(p1T[:], tb[:]).then_inc(s["p1T_ok"], 1)

        def pe_b_sums(pe, g, p):
            wait(pe, s["r1_ok"], full(lambda n: n * H1, g, 1))
            wait(pe, s["t1_ok"], g)
            wait(pe, s["p1T_ok"], g + 1)
            for c in range(H1):
                for b in range(GB):
                    ins = pe.matmul(mm[:, c, b * P:(b + 1) * P], h1[p][:, b, c * P:(c + 1) * P],
                                    p1T[:, b * P:(b + 1) * P], start=(b == 0), stop=(b == GB - 1),
                                    skip_group_check=True)
            ins.then_inc(s["av1_ps"], 1)

        def act_c_exp(act, g):
            wait(act, s["w1_ok"], g)
            wait(act, s["av1_ps"], g + 1)
            nc.scalar.activation(v1[:], mm[:], ACT.Exp).then_inc(s["v1_ok"], 1)

        def dve_c_cut(dve, g):
            wait(dve, s["v1_ok"], g + 1)
            dve.tensor_scalar(v1[:], v1[:], 1.0, None, ALU.min).then_inc(s["v1_cut"], 1)

        def act_c_exp2(act, g):
            wait(act, s["t1_ok"], g)
            wait(act, s["v1_cut"], g + 1)
            nc.scalar.activation(w1[:], v1[:], ACT.Exp, bias=k.neg_one[:]).then_inc(s["w1_ok"], 1)

        def dve_c_max(dve, g):
            wait(dve, s["u1_ok"], g)
            wait(dve, s["w1_ok"], g + 1)
            dve.scalar_tensor_tensor(t1[:], w1[:], -1.0, mm[:], ALU.add, ALU.max).then_inc(s["t1_ok"], 1)

        def pool_c_residual(pool, g, p):
            wait(pool, s["r2_ps"], g)
            wait(pool, s["t1_ok"], g + 1)
            pool.tensor_tensor(u1[:], t1[:], r1T[p][:], ALU.add).then_inc(s["u1_ok"], 1)

        def pe_c_dense(pe, g):
            wait(pe, s["s2_ok"], g - 1)
            wait(pe, s["r2_ok"], g)
            wait(pe, s["u1_ok"], g + 1)
            for c in range(H1):
                ins = pe.matmul(rr[:], k.w_mlp2[:, c, :], u1[:, c, :], start=(c == 0), stop=(c == H1 - 1))
            ins.then_inc(s["r2_ps"], 1)

        def act_c_r2(act, g, p):
            wait(act, s["r2T_ps"], g - 1)
            wait(act, s["r2_ps"], g + 1)
            nc.scalar.activation(r2T[p][:], rr[:], ACT.Relu, bias=k.b_mlp2[:]).then_inc(s["r2_ok"], 1)

        def pe_d_h2(pe, g, p):
            wait(pe, s["h1_ok"], full(lambda n: n * GB, g, 1))
            wait(pe, s["h2_ok"], g)
            wait(pe, s["r2_ok"], g + 1)
            for b in range(GB):
                ins = pe.matmul(hh[:, b // 2, (b % 2) * W2C:(b % 2 + 1) * W2C], r2T[p][:, b * P:(b + 1) * P],
                                k.w_hand[:, 0:W2C], start=(b % 2 == 0), stop=(b % 2 == 1), skip_group_check=True)
            ins.then_inc(s["h2_ps"], 1)

        def pe_d_f2(pe, g, p):
            wait(pe, s["y1_ok"], full(lambda n: n, g, 1))
            wait(pe, s["y2_ok"], g)
            pe.matmul(ff[:], k.w_f2_hand[:], r2T[p][:], start=True, stop=True).then_inc(s["f2_ps"], 1)

        def dve_d_h2(dve, g):
            wait(dve, s["av2_ps"], g)
            wait(dve, s["h2_ps"], g + 1)
            dve.tensor_copy(h2[:].rearrange("p (t b) c -> p t (b c)", t=2), hh[:, :, 0:2 * W2C]).then_inc(s["h2_ok"], 1)

        def act_d_sum(act, g):
            wait(act, s["l2_ok"], g)
            wait(act, s["h2_ok"], g + 1)
            wait(act, s["f2_ps"], g + 1)
            for b in range(GB):
                ins = nc.scalar.activation(y2[:, b, :], ff[:, b * P:(b + 1) * P], ACT.Identity,
                                           bias=h2[:, b, D:W2C])
            ins.then_inc(s["y2_ok"], 1)

        def dve_d_leaky(dve, g):
            wait(dve, s["p2_ok"], g)
            wait(dve, s["y2_ok"], g + 1)
            dve.scalar_tensor_tensor(l2[:], y2[:], 0.2, y2[:], ALU.mult, ALU.max).then_inc(s["l2_ok"], 1)
            wait(dve, s["l2_ok"], g + 1)
            dve.tensor_tensor(e2[:], l2[:], k.cap[:].unsqueeze(1).to_broadcast(G4), ALU.min).then_inc(s["e2_ok"], 1)
            wait(dve, s["e2_ok"], g + 1)
            dve.tensor_reduce(nmax2[:], e2[:], AX.X, ALU.max, negate=True).then_inc(s["max2_ok"], 1)

        def act_d_exp(act, g):
            wait(act, s["p2T_ps"], g)
            wait(act, s["rden2_ok"], g)
            wait(act, s["max2_ok"], g + 1)
            for b in range(GB):
                ins = nc.scalar.activation(p2[:, b, :], e2[:, b, :], ACT.Exp, bias=nmax2[:, b:b + 1],
                                           accum_out=den2[:, b:b + 1])
            ins.then_inc(s["p2_ok"], 1)

        def dve_d_rden(dve, g, p):
            wait(dve, s["p2_ok"], g + 1)
            dve.reciprocal(rden2[p][:], den2[:]).then_inc(s["rden2_ok"], 1)

        def pe_d_transpose(pe, g):
            wait(pe, s["xT_ok"], full(lambda n: n, g, 3))
            wait(pe, s["p1T_ok"], full(lambda n: n, g, 1))
            wait(pe, s["p2T_ok"], g)
            wait(pe, s["p2_ok"], g + 1)
            for b in range(GB):
                ins = pe.transpose(tb[:, b * P:(b + 1) * P], p2[:, b, :], k.ident[:])
            ins.then_inc(s["p2T_ps"], 1)

        def act_d_p2T(act, g):
            wait(act, s["av2_ps"], g)
            wait(act, s["p2T_ps"], g + 1)
            nc.scalar.copy(p2T[:], tb[:]).then_inc(s["p2T_ok"], 1)

        def pe_d_r2(pe, g, p):
            wait(pe, s["r2_ok"], full(lambda n: n, g, 1))
            wait(pe, s["s2_ok"], g)
            for b in range(GB):
                ins = pe.transpose(rr[:, b * P:(b + 1) * P], r2T[p][:, b * P:(b + 1) * P], k.ident[:])
            ins.then_inc(s["r2T_ps"], 1)

        def pe_d_sums(pe, g):
            wait(pe, s["q2_ok"], g)
            wait(pe, s["p2T_ok"], g + 1)
            for b in range(GB):
                ins = pe.matmul(av[:, b * P:(b + 1) * P], p2T[:, b * P:(b + 1) * P], h2[:, b, 0:D],
                                start=(b == 0), stop=(b == GB - 1), skip_group_check=True)
            ins.then_inc(s["av2_ps"], 1)

        def as_batches(ap):
            return ap.rearrange("p (b d) -> p b d", b=GB)

        def dve_e_quotient(dve, g, p):
            wait(dve, s["t2_ok"], g)
            wait(dve, s["rden2_ok"], g + 1)
            wait(dve, s["av2_ps"], g + 1)
            dve.tensor_tensor(q2[:], as_batches(av[:]), rden2[p][:].unsqueeze(2).to_broadcast(G4), ALU.mult)\
                .then_inc(s["q2_ok"], 1)

        def act_e_exp(act, g):
            wait(act, s["w2_ok"], g)
            wait(act, s["q2_ok"], g + 1)
            nc.scalar.activation(v2[:], q2[:], ACT.Exp).then_inc(s["v2_ok"], 1)

        def dve_e_cut(dve, g):
            wait(dve, s["v2_ok"], g + 1)
            dve.tensor_scalar(v2[:], v2[:], 1.0, None, ALU.min).then_inc(s["v2_cut"], 1)

        def act_e_exp2(act, g):
            wait(act, s["t2_ok"], g)
            wait(act, s["v2_cut"], g + 1)
            nc.scalar.activation(w2[:], v2[:], ACT.Exp, bias=k.neg_one[:]).then_inc(s["w2_ok"], 1)

        def dve_e_out(dve, g):
            wait(dve, s["s2_ok"], g)
            wait(dve, s["w2_ok"], g + 1)
            dve.scalar_tensor_tensor(t2[:], w2[:], -1.0, q2[:], ALU.add, ALU.max).then_inc(s["t2_ok"], 1)
            wait(dve, s["x_ok"], g)
            wait(dve, s["r2T_ps"], g + 1)
            wait(dve, s["t2_ok"], g + 1)
            dve.tensor_tensor(s2[:], t2[:], as_batches(rr[:]), ALU.add).then_inc(s["s2_ok"], 1)
            wait(dve, s["s2_ok"], g + 1)
            xg = k.x[:, bass.ds(g * GB, GB), :]
            dve.scalar_tensor_tensor(xg, s2[:], 0.0, xg, ALU.max, ALU.add).then_inc(s["x_ok"], 1)

        def dve_e_stats(dve, g):
            wait(dve, s["x_ok"], g + 1)
            dve.memset(fence[:], 0.0)
            layer_norm_stats(dve, lambda b: batch(k.x, g, b).rearrange("p o d -> p (o d)"),
                             st, mv4, fence, s["stats4"], g + 1, s["var4"])
            wait(dve, s["var4"], g + 1)
            dve.tensor_scalar(k.mean_var[:, bass.ds(g * GB, GB), :], mv4[:], 1.0, None, ALU.mult)\
                .then_inc(s["kept4"], 1)

        def pe_slot(pe, g, half, p, on):
            q = 1 - p
            if on["d"]:
                pe_d_h2(pe, g, p)
                pe_d_f2(pe, g, p)
            if on["b"]:
                pe_b_h1(pe, g + 2, p)
                pe_b_f2(pe, g + 2, p)
            if on["a"]:
                pe_a_transpose(pe, g + 3)
            if on["c"]:
                pe_c_dense(pe, g + 1)
            if on["d"]:
                pe_d_transpose(pe, g)
            if on["a"]:
                pe_a_dense(pe, g + 3)
            if on["d"]:
                pe_d_r2(pe, g, p)
                pe_d_sums(pe, g)
            if on["b"]:
                pe_b_transpose(pe, g + 2)
                pe_b_sums(pe, g + 2, p)

        def act_slot(act, g, half, p, on):
            q = 1 - p
            if on["c"]:
                act_c_exp(act, g + 1)
            if on["e"]:
                act_e_exp(act, g - 1)
            if on["c"]:
                act_c_exp2(act, g + 1)
            if on["e"]:
                act_e_exp2(act, g - 1)
            if on["b"]:
                act_b_h1(act, g + 2, p, 0)
            if on["d"]:
                act_d_sum(act, g)
            if on["b"]:
                for b in range(1, GB):
                    act_b_h1(act, g + 2, p, b)
            if on["d"]:
                act_d_exp(act, g)
            if on["a"]:
                act_a_xT(act, g + 3)
            if on["b"]:
                act_b_sum(act, g + 2, p)
            if on["c"]:
                act_c_r2(act, g + 1, q)
            if on["d"]:
                act_d_p2T(act, g)
            if on["b"]:
                act_b_exp(act, g + 2)
            if on["n"]:
                act_n_rstd(act, g + 4, p)
            if on["a"]:
                act_a_r1(act, g + 3, q)

        def dve_slot(dve, g, half, p, on):
            q = 1 - p
            if on["e"]:
                dve_e_quotient(dve, g - 1, q)
            if on["c"]:
                dve_c_cut(dve, g + 1)
            if on["d"]:
                dve_d_h2(dve, g)
            if on["e"]:
                dve_e_cut(dve, g - 1)
            if on["c"]:
                dve_c_max(dve, g + 1)
            if on["d"]:
                dve_d_leaky(dve, g)
            if on["e"]:
                dve_e_out(dve, g - 1)
            if on["d"]:
                dve_d_rden(dve, g, p)
            if on["n"]:
                dve_n_combine(dve, g + 4, half + 2, p)
            if on["b"]:
                dve_b_leaky(dve, g + 2)
            if on["n"]:
                dve_n_stats(dve, g + 4, p)
            if on["b"]:
                dve_b_rden(dve, g + 2)
            if on["n"]:
                dve_n_apply(dve, g + 4, p)
            if on["e"]:
                dve_e_stats(dve, g - 1)
            if on["b"]:
                dve_b_p1T(dve, g + 2)

        def stages(g):
            def runs(group):
                return 0 <= group < GROUPS
            return dict(n=runs(g + 4), a=runs(g + 3), b=runs(g + 2), c=runs(g + 1), d=runs(g), e=runs(g - 1))

        def slots(slot, eng):
            everything = dict(n=True, a=True, b=True, c=True, d=True, e=True)
            first, last = 2, GROUPS - 4
            for g in range(-4, first):
                slot(eng, g, g // 2, g % 2, stages(g))
            with eng.Fori(first // 2, last // 2) as i:
                for p in range(2):
                    slot(eng, i * 2 + p, i, p, everything)
            for g in range(last, GROUPS + 1):
                slot(eng, g, g // 2, g % 2, stages(g))

        with nc.Block() as block:
            @block.vector
            def _(dve):
                slots(dve_slot, dve)

            @block.scalar
            def _(act):
                exp_ln_tables(nc, act)
                slots(act_slot, act)

            @block.gpsimd
            def _(pool):
                pool_gather(pool, 0, range(8))
                for g in range(-4, GROUPS):
                    on = stages(g)
                    more = g + 5 < GROUPS
                    if more:
                        pool_gather(pool, g + 5, range(0, 3))
                    if on["c"]:
                        pool_c_residual(pool, g + 1, (g + 1) % 2)
                    if more:
                        pool_gather(pool, g + 5, range(3, 8))
                    if on["b"]:
                        pool_b_scale(pool, g + 2)

            @block.tensor
            def _(pe):
                slots(pe_slot, pe)


def last_ffn_phase(nc, k, out):
    KEPT = max(1, TOKENS // 2) - 1
    FC = 4
    with ExitStack() as ctx:
        def sb(name, shape, dt=F32):
            return ctx.enter_context(nc.sbuf_tensor("f_" + name, shape, dt))

        def ps(name, shape):
            return ctx.enter_context(nc.psum_tensor("f_" + name, shape, F32))

        def sem(name):
            return ctx.enter_context(nc.semaphore("f_" + name))

        G4 = [P, GB, P]
        lnv, rstd = sb("lnv", [P, BATCHES]), sb("rstd", [P, BATCHES])
        before = sb("before", [P, P])
        xn = [sb(f"xn{p}", G4) for p in range(2)]
        xT = [sb(f"xT{p}", [P, GB * P]) for p in range(2)]
        wb, wd, eq, gt = sb("wb", G4), sb("wd", G4), sb("eq", G4), sb("gt", G4)
        w_tok, rank = sb("w_tok", [P, GB]), sb("rank", [P, GB])
        gate = sb("gate", [P, BATCHES])
        hT = [sb(f"hT{p}", [P, FC, GB * P]) for p in range(2)]
        yb = sb("yb", G4)
        ot = [sb(f"ot{p}", G4) for p in range(2)]

        tb, wp = ps("tb", [P, 512]), ps("wp", [P, 512])
        hp = ps("hp", [P, FC, 512])
        yp = [ps(f"yp{p}", [P, 512]) for p in range(2)]
        s = {n: sem(n) for n in (
            "made", "lnv_done", "rstd_ok", "xn_ok", "x_sum", "xT_ps", "xT_ok", "w_ps", "wb_ok", "wd_ok", "wt_ok",
            "eq_ok", "gt_ok", "rank_ok", "gate_ok", "h_ps", "h_ok", "y_ps", "yb_ok", "out_ok")}
        stored = [sem(f"stored{p}") for p in range(2)]

        def batch(ap, g, b):
            return ap[:, bass.ds(g * GB + b, 1), :]

        def dve_apply(dve, g, p):
            wait(dve, s["xT_ps"], g - 1)
            for b in range(GB):
                at = bass.ds(g * GB + b, 1)
                ins = dve.tensor_scalar(xn[p][:, b:b + 1, :], batch(k.x, g, b), k.mean_var[:, at, 0],
                                        rstd[:, at], ALU.subtract, ALU.mult)
            ins.then_inc(s["xn_ok"], 1)
            wait(dve, s["xn_ok"], g + 1)
            xg = k.x[:, bass.ds(g * GB, GB), :]
            dve.tensor_tensor(xg, xg, xn[p][:], ALU.add).then_inc(s["x_sum"], 1)

        def pe_transpose(pe, g, p):
            wait(pe, s["xT_ok"], g)
            wait(pe, s["xn_ok"], g + 1)
            for b in range(GB):
                ins = pe.transpose(tb[:, b * P:(b + 1) * P], xn[p][:, b, :], k.ident[:])
            ins.then_inc(s["xT_ps"], 1)

        def act_xT(act, g, p):
            wait(act, s["h_ps"], (g - 1) * FC)
            wait(act, s["xT_ps"], g + 1)
            nc.scalar.copy(xT[p][:], tb[:]).then_inc(s["xT_ok"], 1)

        def pe_weights(pe, g, p):
            wait(pe, s["wb_ok"], g)
            wait(pe, s["xT_ok"], g + 1)
            pe.matmul(wp[:], k.wr_rep[:], xT[p][:], start=True, stop=True).then_inc(s["w_ps"], 1)

        def act_weights(act, g):
            wait(act, s["gt_ok"], g)
            wait(act, s["wd_ok"], g)
            wait(act, s["w_ps"], g + 1)
            nc.scalar.activation(wb[:].rearrange("p b j -> p (b j)"), wp[:], ACT.Identity, bias=k.br_last[:])\
                .then_inc(s["wb_ok"], 1)

        def pool_diagonal(pool, g):
            wait(pool, s["wt_ok"], g)
            wait(pool, s["wb_ok"], g + 1)
            pool.tensor_tensor(wd[:], wb[:], k.ident[:].unsqueeze(1).to_broadcast(G4), ALU.mult).then_inc(s["wd_ok"], 1)

        def dve_rank(dve, g):
            wait(dve, s["gate_ok"], g)
            wait(dve, s["wd_ok"], g + 1)
            dve.tensor_reduce(w_tok[:], wd[:], AX.X, ALU.add).then_inc(s["wt_ok"], 1)
            wait(dve, s["wt_ok"], g + 1)
            for b in range(GB):
                ins = dve.scalar_tensor_tensor(eq[:, b, :], wb[:, b, :], w_tok[:, b:b + 1], before[:],
                                               ALU.is_equal, ALU.mult)
            ins.then_inc(s["eq_ok"], 1)
            wait(dve, s["eq_ok"], g + 1)
            for b in range(GB):
                ins = dve.scalar_tensor_tensor(gt[:, b, :], wb[:, b, :], w_tok[:, b:b + 1], eq[:, b, :],
                                               ALU.is_gt, ALU.add)
            ins.then_inc(s["gt_ok"], 1)
            wait(dve, s["gt_ok"], g + 1)
            dve.tensor_reduce(rank[:], gt[:], AX.X, ALU.add).then_inc(s["rank_ok"], 1)
            wait(dve, s["rank_ok"], g + 1)
            dve.scalar_tensor_tensor(gate[:, bass.ds(g * GB, GB)], rank[:], float(KEPT), w_tok[:],
                                     ALU.is_lt, ALU.mult).then_inc(s["gate_ok"], 1)

        def pe_up(pe, g, p):
            wait(pe, s["xT_ok"], g + 1)
            for c in range(FC):
                wait(pe, s["h_ok"], (g - 1) * FC + c + 1)
                pe.matmul(hp[:, c, :], k.w1_last[:, c * P:(c + 1) * P], xT[p][:], start=True, stop=True)\
                    .then_inc(s["h_ps"], 1)

        def act_gelu(act, g, p):
            wait(act, s["y_ps"], g - 1)
            for c in range(FC):
                wait(act, s["h_ps"], g * FC + c + 1)
                nc.scalar.activation(hT[p][:, c, :], hp[:, c, :], ACT.Gelu_apprx_tanh, bias=k.b1_last[:, c:c + 1])\
                    .then_inc(s["h_ok"], 1)

        def pe_down(pe, g, p):
            wait(pe, s["yb_ok"], g - 1)
            for c in range(FC):
                wait(pe, s["h_ok"], g * FC + c + 1)
                for b in range(GB):
                    ins = pe.matmul(yp[p][:, b * P:(b + 1) * P], hT[p][:, c, b * P:(b + 1) * P], k.w2_last[:, c, :],
                                    start=(c == 0 and b == 0), stop=(c == FC - 1), skip_group_check=True)
            ins.then_inc(s["y_ps"], 1)

        def dve_out(dve, g, half, p):
            wait(dve, s["out_ok"], g)
            wait(dve, s["y_ps"], g + 1)
            dve.tensor_tensor(yb[:], yp[p][:].rearrange("p (b d) -> p b d", b=GB),
                              k.b2_last[:].unsqueeze(1).to_broadcast(G4), ALU.add).then_inc(s["yb_ok"], 1)
            wait(dve, stored[p], half * 16)
            wait(dve, s["yb_ok"], g + 1)
            for b in range(GB):
                ins = dve.scalar_tensor_tensor(ot[p][:, b:b + 1, :], yb[:, b:b + 1, :],
                                               gate[:, bass.ds(g * GB + b, 1)], batch(k.x, g, b), ALU.mult, ALU.add)
            ins.then_inc(s["out_ok"], 1)

        def sp_store(sp, g, p):
            wait(sp, s["out_ok"], g + 1)
            sp.dma_start(out.rearrange("b t d -> t b d")[:, bass.ds(g * GB, GB), :], ot[p][:]).then_inc(stored[p], 16)

        def runs(g):
            return not isinstance(g, int) or 0 <= g < GROUPS

        def slots(slot, eng):
            for g in range(-3, 2):
                slot(eng, g, g // 2, g % 2)
            with eng.Fori(1, GROUPS // 2 - 2) as i:
                for p in range(2):
                    slot(eng, i * 2 + p, i, p)
            for g in range(GROUPS - 4, GROUPS):
                slot(eng, g, g // 2, g % 2)

        def pe_slot(pe, g, half, p):
            if runs(g + 2):
                pe_transpose(pe, g + 2, p)
            if runs(g + 1):
                pe_up(pe, g + 1, 1 - p)
            if runs(g + 2):
                pe_weights(pe, g + 2, p)
            if runs(g):
                pe_down(pe, g, p)

        def act_slot(act, g, half, p):
            if runs(g + 2):
                act_xT(act, g + 2, p)
            if runs(g + 1):
                act_gelu(act, g + 1, 1 - p)
            if runs(g + 2):
                act_weights(act, g + 2)

        def dve_slot(dve, g, half, p):
            if runs(g + 3):
                dve_apply(dve, g + 3, 1 - p)
            if runs(g + 2):
                dve_rank(dve, g + 2)
            if runs(g):
                dve_out(dve, g, half, p)

        with nc.Block() as block:
            @block.gpsimd
            def _(pool):
                pool.affine_select(out=before[:], in_=k.ones[:], compare_op=ALU.is_gt, fill=0.0, base=0,
                                   pattern=[[-1, P]], channel_multiplier=1).then_inc(s["made"], 1)
                for g in range(2):
                    pool_diagonal(pool, g)
                with pool.Fori(2, GROUPS) as g:
                    pool_diagonal(pool, g)

            @block.scalar
            def _(act):
                nc.scalar.activation(lnv[:], k.mean_var[:, :, 1], ACT.Ln, bias=k.eps_ln[:]).then_inc(s["lnv_done"], 1)
                act.wait_ge(s["lnv_done"], 1)
                nc.scalar.activation(rstd[:], lnv[:], ACT.Exp, scale=-0.5).then_inc(s["rstd_ok"], 1)
                slots(act_slot, act)

            @block.vector
            def _(dve):
                dve.wait_ge(s["rstd_ok"], 1)
                dve.wait_ge(s["made"], 1)
                slots(dve_slot, dve)

            @block.tensor
            def _(pe):
                slots(pe_slot, pe)

            @block.sync
            def _(sp):
                for g in range(2):
                    sp_store(sp, g, g)
                with sp.Fori(1, GROUPS // 2) as i:
                    for p in range(2):
                        sp_store(sp, i * 2 + p, p)
                for p in range(2):
                    sp.wait_ge(stored[p], 16 * (GROUPS // 2))


def build(nc, a, out):
    with ExitStack() as whole:
        k = persistent(nc, whole)
        with ExitStack() as buffers:
            add_attention_buffers(nc, buffers, k)
            setup_phase(nc, k, a)
            head_attention_phase(nc, k)
        with ExitStack() as buffers:
            add_expert_buffers(nc, buffers, k)
            router_phase(nc, k, a)
            shared_expert_phase(nc, k)
            routed_experts_phase(nc, k)
        combine_graph_phase(nc, k)
        last_ffn_phase(nc, k, out)


_INS = ['x', 'adj', 'L0_gnn_W', 'L0_gnn_a_src', 'L0_gnn_a_dst', 'L0_gnn_beta_tilde', 'L0_gnn_W_out', 'L0_ffn_Wr',
        'L0_ffn_W1s', 'L0_ffn_b1s', 'L0_ffn_W2s', 'L0_ffn_b2s', 'L0_ffn_W1p', 'L0_ffn_b1p', 'L0_ffn_W2p',
        'L0_ffn_b2p', 'L1_gnn_mlp1_w', 'L1_gnn_mlp1_b', 'L1_gnn_mlp2_w', 'L1_gnn_mlp2_b', 'L1_gnn_W_fc',
        'L1_gnn_a_fc', 'L1_gnn_W_hand', 'L1_gnn_a_hand', 'L1_ffn_wr', 'L1_ffn_br', 'L1_ffn_w1', 'L1_ffn_b1',
        'L1_ffn_w2', 'L1_ffn_b2']


def kernel(**inputs):
    import numpy as _np
    import concourse.bacc as _bacc
    from concourse import mybir as _mybir
    from concourse.bass_utils import run_bass_kernel_spmd as _run

    nc = _bacc.Bacc("TRN2", target_bir_lowering=False, num_devices=1)
    arrays, args = {}, {}
    for name in _INS:
        v = _np.ascontiguousarray(inputs[name])
        if v.ndim == 0:
            v = v.reshape(1)
        arrays[f"in_{name}_dram"] = v
        args[name] = nc.dram_tensor(f"in_{name}_dram", v.shape, _mybir.dt.from_np(v.dtype), kind="ExternalInput").ap()
    out = nc.dram_tensor("out_0_dram", (BATCHES, TOKENS, D), _mybir.dt.float32, kind="ExternalOutput").ap()
    build(nc, args, out)
    r = _run(nc, [arrays], core_ids=[0])
    return r.results[0]["out_0_dram"]
```

```python
from contextlib import ExitStack

import concourse.bass as bass
from concourse import mybir

F32 = mybir.dt.float32
F32R = mybir.dt.float32r
BF16 = mybir.dt.bfloat16
I32 = mybir.dt.int32
ALU = mybir.AluOpType
ACT = mybir.ActivationFunctionType
AX = mybir.AxisListType

P = 128
BATCHES, TOKENS, D = 64, 128, 128
GB = 4
GROUPS = BATCHES // GB
HEADS, DH = 8, 16
HB = GB * HEADS
VW = DH + 1
EXPERTS = 8
LG = 192
EPS_LN = 1e-5
EPS_PRIOR = 1e-6
EXP_LN_TABLES = 6
BIG = 3.0e38
NEG_INF_L1 = -9.0e15
F, FC = 512, 4
TOPK = 2
TILE = 256
TILES = -(-(TOPK * BATCHES * TOKENS // TILE + EXPERTS - 1) // 2) * 2
SLOTS = TILES * TILE
AHEAD = 6
MAX_TILES_OF_ONE = BATCHES * TOKENS // TILE
FETCHED = F + FC + D
EW = FETCHED + F


class Buffers:
    pass


def wait(eng, sem, count):
    if isinstance(count, int) and count <= 0:
        return
    eng.wait_ge(sem, count)


def buffer(nc, ctx, name, shape, dt=F32):
    unit = 64 // (2 if dt == BF16 else 4)
    size = 1
    for n in shape[1:]:
        size *= n
    if size % unit == 0:
        return ctx.enter_context(nc.sbuf_tensor(name, shape, dt))
    whole = ctx.enter_context(nc.sbuf_tensor(name, [shape[0], -(-size // unit) * unit], dt))
    flat = whole[:, 0:size]
    if len(shape) == 2:
        return flat
    if len(shape) == 3:
        return flat.rearrange("p (a b) -> p a b", a=shape[1])
    return flat.rearrange("p (a b c) -> p a b c", a=shape[1], b=shape[2])


def exp_ln_tables(nc, act):
    act.add_instruction(mybir.InstLoadActFuncSet(
        name=nc.get_next_instruction_name(), engine=mybir.EngineType.Activation,
        act_func_set_id=EXP_LN_TABLES, ins=[], outs=[]))


def layer_norm_stats(dve, x_of, st, mv, fence, stats, n_stats, var):
    for b in range(GB):
        ins = dve.bn_stats(st[:, b, :], x_of(b))
    ins.then_inc(stats, 1)
    wait(dve, stats, n_stats)
    dve.memset(fence[:], 0.0)
    for b in range(GB):
        ins = dve.bn_aggr(mv[:, b, :], st[:, b, :])
    ins.then_inc(var, 1)


class PhaseSemaphores:

    def __init__(self, nc, prefix):
        self.nc, self.prefix, self.mine = nc, prefix, []

    def make(self, name):
        self.mine.append(self.nc.alloc_semaphore(name=self.prefix + name))
        return self.mine[-1]

    def clear(self):
        self.nc.clear_and_free_semaphores(self.mine)
        with self.nc.Block():
            pass


def setup_phase(nc, k, a):
    with ExitStack() as ctx:
        def sb(name, shape, dt=F32):
            return buffer(nc, ctx, name, shape, dt)

        def sem(name):
            return ctx.enter_context(nc.semaphore(name))

        adj_i = sb("adj_i", [P, P], I32)
        adj_f = sb("adj_f", [P, P])
        mask = sb("mask", [P, P])
        logw = sb("logw", [P, P])
        m_ij = sb("m_ij", [P, P])
        u_ij = sb("u_ij", [P, P])
        row_stat = sb("row_stat", [P, 4])
        beta = sb("beta", [P, 4])
        w_out_in = sb("w_out_in", [P, D])
        a_heads = sb("a_heads", [P, 2, HEADS, DH])
        wa_prod = sb("wa_prod", [P, 2, HEADS, DH])
        wa = sb("wa", [P, 2, HEADS])
        tri_f = sb("tri_f", [P, P])
        diag_s, diag_d = sb("diag_s", [P, 32]), sb("diag_d", [P, 32])

        load_w, load_adj = sem("load_w"), sem("load_adj")
        pool_made, diag_made, ones_made, dve_s, act_s, pe_t = (sem("pool_made"), sem("diag_made"), sem("ones_made"), sem("dve_s"),
                                                    sem("act_s"), sem("pe_t"))
        tr = ctx.enter_context(nc.psum_tensor("setup_tr", [P, 4, 512], F32))

        with nc.Block() as block:
            @block.sync
            def _(sp):
                sp.dma_start(adj_i[:], a["adj"]).then_inc(load_adj, 16)
                sp.dma_start(beta[:, 0:1], a["L0_gnn_beta_tilde"].partition_broadcast(P)).then_inc(load_adj, 16)
                def load(dst, src):
                    sp.dma_start(dst, src, allow_slow_non_contiguous=True).then_inc(load_w, 16)
                load(w_out_in[:], a["L0_gnn_W_out"])
                load(k.w_heads[:, 0:D].rearrange("d (h f) -> d h f", h=HEADS), a["L0_gnn_W"].rearrange("h d f -> d h f"))
                load(a_heads[:, 0].rearrange("p h f -> p (h f)"),
                     a["L0_gnn_a_src"].rearrange("h f -> (h f)").partition_broadcast(P))
                load(a_heads[:, 1].rearrange("p h f -> p (h f)"),
                     a["L0_gnn_a_dst"].rearrange("h f -> (h f)").partition_broadcast(P))
                sp.wait_ge(load_w, 16 * 4)

            @block.gpsimd
            def _(pool):
                pool.memset(k.ident[:], 0.0).then_inc(pool_made, 1)
                pool.wait_ge(pool_made, 1)
                pool.affine_select(out=k.ident[:], in_=k.ident[:], compare_op=ALU.not_equal, fill=1.0, base=0,
                                   pattern=[[-1, P]], channel_multiplier=1).then_inc(pool_made, 1)
                pool.memset(k.diag32[:], 0.0).then_inc(pool_made, 1)
                pool.wait_ge(pool_made, 3)
                for q in range(4):
                    pool.affine_select(out=k.diag32[:], in_=k.diag32[:], compare_op=ALU.not_equal, fill=1.0,
                                       base=-32 * q, pattern=[[-1, 32]], channel_multiplier=1).then_inc(pool_made, 1)
                    pool.wait_ge(pool_made, 4 + q)
                pool.memset(diag_s[:], 0.0).then_inc(diag_made, 1)
                pool.wait_ge(diag_made, 1)
                pool.memset(diag_d[:], 0.0).then_inc(diag_made, 1)
                for q in range(4):
                    pool.wait_ge(diag_made, 2 + q)
                    rows = slice(32 * q, 32 * q + 32)
                    pool.tensor_copy((diag_s, diag_d)[q % 2][rows], k.diag32[rows]).then_inc(diag_made, 1)
                pool.wait_ge(diag_made, 6)
                pool.memset(k.ones[:], 1.0).then_inc(ones_made, 1)
                pool.memset(tri_f[:], 1.0).then_inc(ones_made, 1)
                pool.wait_ge(ones_made, 2)
                pool.affine_select(out=k.tri[:], in_=tri_f[:], compare_op=ALU.is_gt, fill=0.0, base=0,
                                   pattern=[[1, P]], channel_multiplier=-1).then_inc(ones_made, 1)
                pool.memset(k.zeros[:], 0.0).then_inc(ones_made, 1)
                pool.wait_ge(ones_made, 4)

            @block.scalar
            def _(act):
                def load_x(q):
                    act.dma_start(k.x[:, 16 * q:16 * q + 16, :],
                                  a["x"][16 * q:16 * q + 16].rearrange("b t d -> t b d")).then_inc(k.x_loaded[q], 16)

                load_x(0)
                exp_ln_tables(nc, act)
                act.wait_ge(diag_made, 6)
                nc.scalar.copy(k.sel_s[:], diag_s[:].unsqueeze(2).to_broadcast([P, HB, P]))
                act.wait_ge(load_adj, 32)
                nc.scalar.activation(beta[:, 1:2], beta[:, 0:1], ACT.Abs).then_inc(act_s, 1)
                act.wait_ge(act_s, 1)
                nc.scalar.activation(beta[:, 2:3], beta[:, 1:2], ACT.Exp, scale=-1.0).then_inc(act_s, 1)
                act.wait_ge(act_s, 2)
                act.wait_ge(ones_made, 1)
                nc.scalar.activation(beta[:, 3:4], beta[:, 2:3], ACT.Ln, bias=k.ones[:, 0:1]).then_inc(act_s, 1)
                act.wait_ge(dve_s, 4)
                nc.scalar.activation(logw[:], adj_f[:], ACT.Ln, bias=k.eps_prior[:]).then_inc(act_s, 1)
                act.wait_ge(dve_s, 9)
                nc.scalar.activation(m_ij[:], logw[:], ACT.Exp, bias=row_stat[:, 0:1]).then_inc(act_s, 1)
                act.wait_ge(pe_t, 1)
                nc.scalar.copy(k.w_outT[:], tr[:, 2, 0:P]).then_inc(act_s, 1)
                act.wait_ge(act_s, 6)
                act.wait_ge(load_w, 16 * 4)
                for q in range(1, 4):
                    load_x(q)

            @block.vector
            def _(dve):
                n = [0]

                def chain(ins):
                    n[0] += 1
                    ins.then_inc(dve_s, 1)
                    dve.wait_ge(dve_s, n[0])

                dve.wait_ge(diag_made, 6)
                dve.tensor_copy(k.sel_d[:], diag_d[:].unsqueeze(2).to_broadcast([P, HB, P]))
                dve.wait_ge(load_adj, 32)
                chain(dve.memset(k.eps_prior[:], EPS_PRIOR))
                dve.memset(k.neg_one[:], -1.0)
                chain(dve.memset(k.eps_ln[:], EPS_LN))
                chain(dve.tensor_copy(adj_f[:], adj_i[:]))
                chain(dve.tensor_scalar(adj_f[:], adj_f[:], 0.0, None, ALU.max))
                dve.wait_ge(act_s, 4)
                chain(dve.tensor_scalar(mask[:], adj_f[:], 0.0, None, ALU.is_gt))
                chain(dve.scalar_tensor_tensor(beta[:, 0:1], beta[:, 0:1], 0.0, beta[:, 3:4], ALU.max, ALU.add))
                chain(dve.tensor_scalar(k.cap[:], mask[:], BIG, -BIG, ALU.mult, ALU.add))
                chain(dve.scalar_tensor_tensor(logw[:], logw[:], beta[:, 0:1], k.cap[:], ALU.mult, ALU.add))
                chain(dve.tensor_reduce(row_stat[:, 0:1], logw[:], AX.X, ALU.max, negate=True))
                dve.wait_ge(act_s, 5)
                chain(dve.tensor_tensor(m_ij[:], m_ij[:], mask[:], ALU.mult))
                chain(dve.tensor_reduce(row_stat[:, 1:2], mask[:], AX.X, ALU.max))
                chain(dve.tensor_scalar(u_ij[:], mask[:], 0.0, row_stat[:, 1:2], ALU.mult, ALU.subtract))
                chain(dve.tensor_scalar(u_ij[:], u_ij[:], 1.0, None, ALU.add))
                chain(dve.tensor_scalar(k.cap[:], mask[:], BIG, NEG_INF_L1, ALU.mult, ALU.add))
                dve.wait_ge(load_w, 16 * 4)
                chain(dve.tensor_tensor(wa_prod[:],
                                        k.w_heads[:, 0:D].rearrange("d (o h f) -> d o h f", o=1, h=HEADS)
                                        .to_broadcast([P, 2, HEADS, DH]), a_heads[:], ALU.mult))
                chain(dve.tensor_reduce(wa[:], wa_prod[:], AX.X, ALU.add))
                dve.tensor_copy(k.w_heads[:, D:D + 16], wa[:].rearrange("p t h -> p (t h)"))
                chain(dve.tensor_copy(k.w_heads[:, D + 16:D + 32], wa[:].rearrange("p t h -> p (t h)")))
                dve.wait_ge(pe_t, 2)
                dve.tensor_copy(k.mT[:], tr[:, 0, 0:P])
                dve.tensor_scalar(k.neg_mT[:], tr[:, 0, 0:P], -1.0, None, ALU.mult)
                chain(dve.tensor_scalar(k.neg_uT[:], tr[:, 1, 0:P], -1.0, None, ALU.mult))
                dve.memset(k.v17[0][:, :, DH:VW], 1.0)
                chain(dve.memset(k.v17[1][:, :, DH:VW], 1.0))

            @block.tensor
            def _(pe):
                pe.wait_ge(pool_made, 2)
                pe.wait_ge(load_w, 16 * 4)
                pe.transpose(tr[:, 2, 0:P], w_out_in[:], k.ident[:]).then_inc(pe_t, 1)
                pe.wait_ge(dve_s, 13)
                pe.transpose(tr[:, 0, 0:P], m_ij[:], k.ident[:])
                pe.transpose(tr[:, 1, 0:P], u_ij[:], k.ident[:]).then_inc(pe_t, 1)


def head_attention_phase(nc, k, a):
    with ExitStack() as ctx:
        def sb(name, shape, dt=F32):
            return buffer(nc, ctx, name, shape, dt)

        def ps(name, shape):
            return ctx.enter_context(nc.psum_tensor(name, shape, F32))

        sems = PhaseSemaphores(nc, "l0_")
        sem = sems.make

        st = sb("l0_st", [P, GB, 6])
        mv = [sb(f"l0_mv{p}", [P, GB, 2]) for p in range(2)]
        lnv = sb("l0_lnv", [P, GB])
        rstd = [sb(f"l0_rstd{p}", [P, GB]) for p in range(2)]
        xn = sb("l0_xn", [P, GB, D])
        xnT = [sb(f"l0_xnT{p}", [P, GB * P]) for p in range(2)]
        sd = [sb(f"l0_sd{p}", [P, 4, GB, HEADS]) for p in range(2)]
        dmax = sb("l0_dmax", [P, 1])
        dmdiag = sb("l0_dmdiag", [P, HB])
        sparts = [sb(f"l0_sparts{p}", [P, P], BF16) for p in range(2)]
        fence = sb("l0_fence", [P, 1])
        pk = [sb(f"l0_pk{p}", [P, 4, HB]) for p in range(2)]
        us = sb("l0_us", [P, HB])
        bdfg = [sb(f"l0_bdfg{p}", [P, 4, HB]) for p in range(2)]
        vp = sb("l0_vp", [P, HB, 2 * VW])
        vres = sb("l0_vres", [P, HB, 2 * VW])
        vb = [sb(f"l0_vb{p}", [P, 3, HB, 2 * VW], BF16) for p in range(2)]
        mi = sb("l0_mi", [P, 2, HEADS, P], BF16)
        t1s = [sb(f"l0_t1{b}", [P, HEADS, VW]) for b in range(2)]
        t2s = [sb(f"l0_t2{b}", [P, HEADS, VW]) for b in range(2)]
        rdens = [sb(f"l0_rden{b}", [P, HEADS]) for b in range(2)]
        dens = [sb(f"l0_den{b}", [P, HEADS]) for b in range(2)]
        num = sb("l0_num", [P, HEADS, DH])
        shift = [sb(f"l0_shift{p}", [P, GB]) for p in range(2)]
        act_fence, act_fence_r = sb("l0_act_fence", [P, 1]), sb("l0_act_fence_r", [P, 1])
        st_r, mv_r, fence_r = sb("l0_st_r", [P, GB, 6]), sb("l0_mv_r", [P, GB, 2]), sb("l0_fence_r", [P, 1])
        lnv_r, rstd_r, shift_r = sb("l0_lnv_r", [P, GB]), sb("l0_rstd_r", [P, GB]), sb("l0_shift_r", [P, GB])
        xr, rT = sb("l0_xr", [P, GB, D]), sb("l0_rT", [P, GB, P])
        hn = [sb(f"l0_hn{p}", [P, GB, D]) for p in range(2)]
        hT = sb("l0_hT", [P, GB * P])

        tT = ps("l0_tT", [P, 512])
        vs = ps("l0_vs", [P, 2, 512])
        cc = ps("l0_cc", [P, 512])
        sbc = ps("l0_sbc", [P, 2, 512])
        oo = ps("l0_oo", [P, 512])
        yy = ps("l0_yy", [P, 512])

        names = ("stats", "var", "lnv_done", "rstd_ok", "xn_ok", "xT_ps", "xT_ok", "vs_ps", "vs_ok", "t_ps",
                 "hi_ok", "dg_self", "diag_ok", "dm_ps", "mid_ok", "sp_ok", "us_self", "pk_ok", "bdfg_ok",
                 "vp_ok", "vh_ok", "vr_ok", "vm_ok", "vb_ok", "s_ps", "mi_ok", "pv_ps", "o_read", "num_ok", "rden_ok",
                 "hn_ok", "hT_ps", "hT_ok", "y_ps", "x_ok",
                 "shift_ok", "sd_ok", "den_ok", "stats_r", "var_r", "lnv_r", "rstd_r", "shift_r", "xr_ok", "rT_ps",
                 "rT_ok", "rT_kept", "xr_kept", "lg_ps", "lg_ok")
        s = {n: sem(n) for n in names}

        def xs(g):
            return k.x[:, bass.ds(g * GB, GB), :]

        def dve_x_stats(dve, g, p):
            if isinstance(g, int):
                if g == 6:
                    for quarter in range(2, 4):
                        dve.wait_ge(k.x_loaded[quarter], 16)
                elif g % 4 == 0 and g < 6:
                    dve.wait_ge(k.x_loaded[g // 4], 16)
            for b in range(GB):
                ins = dve.bn_stats(st[:, b, :], k.x[:, bass.ds(g * GB + b, 1), :].rearrange("p o d -> p (o d)"))
            ins.then_inc(s["stats"], 1)
            wait(dve, s["stats"], g + 1)
            dve.memset(fence[:], 0.0)
            for b in range(GB):
                ins = dve.bn_aggr(mv[p][:, b, :], st[:, b, :])
            ins.then_inc(s["var"], 1)

        def act_x_rstd(act, g, p):
            wait(act, s["var"], g + 1)
            nc.scalar.activation(lnv[:], mv[p][:, :, 1], ACT.Ln, bias=k.eps_ln[:]).then_inc(s["lnv_done"], 1)
            wait(act, s["lnv_done"], g + 1)
            nc.scalar.activation(rstd[p][:], lnv[:], ACT.Exp, scale=-0.5).then_inc(s["rstd_ok"], 1)

        def dve_x_shift(dve, g, p):
            wait(dve, s["xn_ok"], g - 1)
            wait(dve, s["rstd_ok"], g + 1)
            dve.scalar_tensor_tensor(shift[p][:], mv[p][:, :, 0], -1.0, rstd[p][:], ALU.mult, ALU.mult)\
                .then_inc(s["shift_ok"], 1)

        def act_x_apply(act, g, p):
            wait(act, s["xT_ps"], g)
            wait(act, s["shift_ok"], g + 1)
            nc.scalar.copy(act_fence[:], shift[p][:, 0:1])
            for b in range(GB):
                ins = nc.scalar.activation(xn[:, b:b + 1, :], k.x[:, bass.ds(g * GB + b, 1), :], ACT.Identity,
                                           scale=rstd[p][:, b:b + 1], bias=shift[p][:, b:b + 1])
            ins.then_inc(s["xn_ok"], 1)

        def pe_x_transpose(pe, g, p):
            wait(pe, s["xn_ok"], g + 1)
            wait(pe, s["xT_ok"], g)
            wait(pe, s["hT_ok"], g - 3)
            for b in range(GB):
                ins = pe.transpose(tT[:, b * P:(b + 1) * P], xn[:, b, :], k.ident[:])
            ins.then_inc(s["xT_ps"], 1)

        def act_x_xT(act, g, p):
            wait(act, s["xT_ps"], g + 1)
            wait(act, s["vs_ps"], g - 1)
            nc.scalar.copy(xnT[p][:], tT[:]).then_inc(s["xT_ok"], 1)

        def pe_x_values(pe, g, p):
            wait(pe, s["xT_ok"], g + 1)
            wait(pe, s["vs_ok"], g)
            for b in range(GB):
                ins = pe.matmul(vs[:, b // 2, (b % 2) * 160:(b % 2) * 160 + 160], xnT[p][:, b * P:(b + 1) * P],
                                k.w_heads[:], start=(b % 2 == 0), stop=(b % 2 == 1), skip_group_check=True)
            ins.then_inc(s["vs_ps"], 1)

        def act_x_values(act, g, p):
            wait(act, s["vb_ok"], g - 1)
            wait(act, s["pv_ps"], (g - 1) * GB)
            for h in range(2):
                both = vs[:, h, 0:320].rearrange("p (b c) -> p b c", b=2)
                ins = nc.scalar.copy(k.v17[p][:, 16 * h:16 * h + 16, 0:DH].rearrange("p (b h) f -> p b h f", b=2),
                                     both[:, :, 0:D].rearrange("p b (h f) -> p b h f", h=HEADS))
            ins.then_inc(s["vs_ok"], 1)

        def act_x_scores(act, g, p):
            wait(act, s["vs_ps"], g + 1)
            wait(act, s["pk_ok"], g - 1)
            for h in range(2):
                both = vs[:, h, 0:320].rearrange("p (b c) -> p b c", b=2)
                ins = nc.scalar.copy(sd[p][:, :, 2 * h:2 * h + 2, :].rearrange("p k b h -> p b k h"),
                                     both[:, :, D:160].rearrange("p b (k h) -> p b k h", k=4))
            ins.then_inc(s["sd_ok"], 1)

        def pe_y_transpose(pe, g, p):
            wait(pe, s["sd_ok"], g + 1)
            wait(pe, s["pk_ok"], g)
            wait(pe, s["lg_ok"], g - 4)
            pe.transpose(cc[:, 0:P], sd[p][:].rearrange("p k b h -> p (k b h)"), k.ident[:]).then_inc(s["t_ps"], 1)

        def act_y_hi(act, g, p):
            wait(act, s["t_ps"], g + 1)
            wait(act, s["s_ps"], (g - 1) * 2 * GB)
            nc.scalar.copy(sparts[p][:], cc[:, 0:P]).then_inc(s["hi_ok"], 1)

        def dve_y_max(dve, g, p):
            wait(dve, s["hi_ok"], g + 1)
            wait(dve, s["dm_ps"], g)
            dve.tensor_reduce(dmax[32:64, :], cc[32:64, 0:P], AX.X, ALU.max).then_inc(s["dg_self"], 1)
            dve.tensor_tensor(sparts[p][64:128, :], cc[64:128, 0:P], sparts[p][64:128, :], ALU.subtract)\
                .then_inc(s["sp_ok"], 1)
            wait(dve, s["dg_self"], g + 1)
            dve.tensor_scalar(dmdiag[32:64, :], k.diag32[32:64, :], dmax[32:64, :], None, ALU.mult)\
                .then_inc(s["diag_ok"], 1)

        def pe_y_maxima(pe, g, p):
            wait(pe, s["diag_ok"], g + 1)
            pe.matmul(cc[:, P:P + HB], k.ones[32:64, :], dmdiag[32:64, :], start=True, stop=True)\
                .then_inc(s["dm_ps"], 1)

        def dve_y_small(dve, g, p):
            wait(dve, s["dm_ps"], g + 1)
            wait(dve, s["bdfg_ok"], g - 1)
            s_i = sd[p][:, 0].rearrange("p b h -> p (b h)")
            d_j = sd[p][:, 1].rearrange("p b h -> p (b h)")
            dve.tensor_tensor(pk[p][:, 0], d_j, cc[:, P:P + HB], ALU.subtract)
            dve.tensor_tensor(us[:], cc[:, P:P + HB], s_i, ALU.add).then_inc(s["us_self"], 1)
            wait(dve, s["us_self"], g + 1)
            dve.tensor_scalar(pk[p][:, 1], pk[p][:, 0], 0.2, None, ALU.mult)
            dve.tensor_scalar(pk[p][:, 2], us[:], 0.8, 0.0, ALU.mult, ALU.min)
            dve.tensor_scalar(pk[p][:, 3], us[:], -0.8, 0.0, ALU.mult, ALU.min).then_inc(s["pk_ok"], 1)

        def act_y_exp(act, g, p):
            wait(act, s["pk_ok"], g + 1)
            wait(act, s["o_read"], (g - 1) * GB)
            nc.scalar.activation(bdfg[p][:], pk[p][:], ACT.Exp).then_inc(s["bdfg_ok"], 1)

        def pool_y_scale(pool, g, p):
            wait(pool, s["bdfg_ok"], g + 1)
            wait(pool, s["vh_ok"], g)
            pool.tensor_tensor(vp[:, :, 0:VW], k.v17[p][:], bdfg[p][:, 0].unsqueeze(2).to_broadcast([P, HB, VW]),
                               ALU.mult)
            pool.tensor_tensor(vp[:, :, VW:2 * VW], k.v17[p][:],
                               bdfg[p][:, 1].unsqueeze(2).to_broadcast([P, HB, VW]), ALU.mult).then_inc(s["vp_ok"], 1)

        def act_y_vhi(act, g, p):
            wait(act, s["vp_ok"], g + 1)
            wait(act, s["pv_ps"], (g - 1) * GB)
            nc.scalar.copy(vb[p][:, 0], vp[:]).then_inc(s["vh_ok"], 1)

        def pool_y_res(pool, g, p):
            wait(pool, s["vh_ok"], g + 1)
            wait(pool, s["vm_ok"], g)
            pool.tensor_tensor(vres[:], vp[:], vb[p][:, 0], ALU.subtract).then_inc(s["vr_ok"], 1)

        def act_y_vmid(act, g, p):
            wait(act, s["vr_ok"], g + 1)
            nc.scalar.copy(vb[p][:, 1], vres[:]).then_inc(s["vm_ok"], 1)

        def pool_y_lo(pool, g, p):
            wait(pool, s["vm_ok"], g + 1)
            pool.tensor_tensor(vb[p][:, 2], vres[:], vb[p][:, 1], ALU.subtract).then_inc(s["vb_ok"], 1)

        def pe_z_scores(pe, g, p, b):
            if b == 0:
                wait(pe, s["sp_ok"], g + 1)
            for h in range(2):
                wait(pe, s["mi_ok"], g * 2 * GB + 2 * b + h - 1)
                c = b * HEADS + 4 * h
                pe.matmul(sbc[:, h, :].rearrange("p (q i) -> p q i", q=4), sparts[p][:], k.sel_d[:, c:c + 4, :],
                          start=True, stop=False, skip_group_check=True)
                for q in range(4):
                    ins = pe.matmul(sbc[:, h, q * P:(q + 1) * P], k.sel_s[:, c + q, :], sparts[p][:],
                                    start=False, stop=(q == 3), skip_group_check=True)
                ins.then_inc(s["s_ps"], 1)

        def dve_z_compare(dve, g, p, b, h):
            wait(dve, s["s_ps"], g * 2 * GB + 2 * b + h + 1)
            if h == 0:
                wait(dve, s["pv_ps"], g * GB + b - 1)
            ins = dve.scalar_tensor_tensor(mi[:, b % 2, 4 * h:4 * h + 4, :],
                                           sbc[:, h, :].rearrange("p (q i) -> p q i", q=4), 0.0,
                                           k.mT[:].unsqueeze(1).to_broadcast([P, 4, P]), ALU.is_gt, ALU.mult)
            ins.then_inc(s["mi_ok"], 1)

        def pe_z_sums(pe, g, p, b):
            if b == 0:
                wait(pe, s["vb_ok"], g + 1)
            wait(pe, s["o_read"], g * GB + b)
            out = oo[:, 0:HEADS * 2 * VW].rearrange("p (h c) -> p h c", h=HEADS)
            rows = slice(b * HEADS, (b + 1) * HEADS)
            for part in range(3):
                pe.matmul(out[:, :, VW:2 * VW], k.neg_mT[:], vb[p][:, part, rows, VW:2 * VW],
                          start=(part == 0), stop=False, skip_group_check=True)
            pe.matmul(out[:, :, VW:2 * VW], k.neg_uT[:], k.v17[p][:, rows, :], start=False, stop=False,
                      skip_group_check=True)
            for h in range(HEADS):
                if h % 4 == 0:
                    wait(pe, s["mi_ok"], g * 2 * GB + 2 * b + h // 4 + 1)
                for part in range(3):
                    ins = pe.matmul(out[:, h, :], mi[:, b % 2, h, :], vb[p][:, part, b * HEADS + h, :],
                                    start=False, stop=(h == HEADS - 1 and part == 2), skip_group_check=True)
            ins.then_inc(s["pv_ps"], 1)

        def dve_z_post(dve, g, p, b):
            rows = slice(b * HEADS, (b + 1) * HEADS)
            out = oo[:, 0:HEADS * 2 * VW].rearrange("p (h c) -> p h c", h=HEADS)
            wait(dve, s["hn_ok"], g * GB + b - 1)
            wait(dve, s["pv_ps"], g * GB + b + 1)
            dve.tensor_tensor(t1s[b % 2][:], out[:, :, 0:VW],
                              bdfg[p][:, 2, rows].unsqueeze(2).to_broadcast([P, HEADS, VW]), ALU.mult)
            dve.tensor_tensor(t2s[b % 2][:], out[:, :, VW:2 * VW],
                              bdfg[p][:, 3, rows].unsqueeze(2).to_broadcast([P, HEADS, VW]), ALU.mult)\
                .then_inc(s["o_read"], 1)

        def dve_z_den(dve, g, b):
            wait(dve, s["o_read"], g * GB + b + 1)
            dve.tensor_tensor(dens[b % 2][:], t1s[b % 2][:, :, DH], t2s[b % 2][:, :, DH], ALU.subtract)\
                .then_inc(s["den_ok"], 1)

        def dve_z_rden(dve, g, b):
            wait(dve, s["den_ok"], g * GB + b + 1)
            dve.reciprocal(rdens[b % 2][:], dens[b % 2][:]).then_inc(s["rden_ok"], 1)

        def pool_z_post(pool, g, p, b):
            n = g * GB + b
            wait(pool, s["hn_ok"], n)
            wait(pool, s["o_read"], n + 1)
            pool.tensor_tensor(num[:], t1s[b % 2][:, :, 0:DH], t2s[b % 2][:, :, 0:DH], ALU.subtract)\
                .then_inc(s["num_ok"], 1)
            if b == 0:
                wait(pool, s["hT_ps"], g - 1)
            wait(pool, s["num_ok"], n + 1)
            wait(pool, s["rden_ok"], n + 1)
            pool.tensor_tensor(hn[p][:, b, :].rearrange("p (h f) -> p h f", h=HEADS), num[:],
                               rdens[b % 2][:].unsqueeze(2).to_broadcast([P, HEADS, DH]), ALU.mult)\
                .then_inc(s["hn_ok"], 1)

        def pe_w_transpose(pe, g, p):
            wait(pe, s["hn_ok"], (g + 1) * GB)
            wait(pe, s["xT_ok"], min(g + 4, GROUPS) if isinstance(g, int) else g + 4)
            wait(pe, s["rT_ok"], g - 1)
            for b in range(GB):
                ins = pe.transpose(tT[:, b * P:(b + 1) * P], hn[p][:, b, :], k.ident[:])
            ins.then_inc(s["hT_ps"], 1)

        def act_w_hT(act, g, p):
            wait(act, s["hT_ps"], g + 1)
            wait(act, s["y_ps"], g)
            nc.scalar.copy(hT[:], tT[:]).then_inc(s["hT_ok"], 1)

        def pe_w_project(pe, g, p):
            wait(pe, s["hT_ok"], g + 1)
            wait(pe, s["x_ok"], g)
            for b in range(GB):
                ins = pe.matmul(yy[:, b * P:(b + 1) * P], hT[:, b * P:(b + 1) * P], k.w_outT[:],
                                start=(b == 0), stop=(b == GB - 1), skip_group_check=True)
            ins.then_inc(s["y_ps"], 1)

        def dve_w_add(dve, g, p):
            wait(dve, s["y_ps"], g + 1)
            dve.scalar_tensor_tensor(xs(g), yy[:].rearrange("p (b d) -> p b d", b=GB), 1.0, xs(g),
                                     ALU.mult, ALU.add).then_inc(s["x_ok"], 1)

        def dve_r_stats(dve, g):
            wait(dve, s["x_ok"], g + 1)
            dve.memset(fence_r[:], 0.0)
            layer_norm_stats(dve, lambda b: k.x[:, bass.ds(g * GB + b, 1), :].rearrange("p o d -> p (o d)"),
                             st_r, mv_r, fence_r, s["stats_r"], g + 1, s["var_r"])

        def act_r_rstd(act, g):
            wait(act, s["var_r"], g + 1)
            nc.scalar.activation(lnv_r[:], mv_r[:, :, 1], ACT.Ln, bias=k.eps_ln[:]).then_inc(s["lnv_r"], 1)
            wait(act, s["lnv_r"], g + 1)
            nc.scalar.activation(rstd_r[:], lnv_r[:], ACT.Exp, scale=-0.5).then_inc(s["rstd_r"], 1)

        def dve_r_shift(dve, g):
            wait(dve, s["rstd_r"], g + 1)
            dve.scalar_tensor_tensor(shift_r[:], mv_r[:, :, 0], -1.0, rstd_r[:], ALU.mult, ALU.mult)\
                .then_inc(s["shift_r"], 1)

        def act_r_apply(act, g):
            wait(act, s["rT_ps"], g)
            wait(act, s["xr_kept"], g)
            wait(act, s["shift_r"], g + 1)
            nc.scalar.copy(act_fence_r[:], shift_r[:, 0:1])
            for b in range(GB):
                at = bass.ds(g * GB + b, 1)
                ins = nc.scalar.activation(xr[:, b:b + 1, :], k.x[:, at, :], ACT.Identity,
                                           scale=rstd_r[:, b:b + 1], bias=shift_r[:, b:b + 1])
            ins.then_inc(s["xr_ok"], 1)

        def pe_l_transpose(pe, g):
            wait(pe, s["xT_ok"], min(g + 6, GROUPS) if isinstance(g, int) else g + 6)
            wait(pe, s["hT_ok"], g + 1)
            wait(pe, s["xr_ok"], g + 1)
            for b in range(GB):
                ins = pe.transpose(tT[:, b * P:(b + 1) * P], xr[:, b, :], k.ident[:])
            ins.then_inc(s["rT_ps"], 1)

        def act_l_rT(act, g):
            wait(act, s["rT_kept"], g)
            wait(act, s["lg_ps"], g)
            wait(act, s["rT_ps"], g + 1)
            nc.scalar.copy(rT[:].rearrange("p b t -> p (b t)"), tT[:]).then_inc(s["rT_ok"], 1)

        def dve_r_keep(dve, g):
            wait(dve, s["xr_ok"], g + 1)
            dve.tensor_scalar(k.xn[:, bass.ds(g * GB, GB), :], xr[:], 1.0, None, ALU.mult).then_inc(s["xr_kept"], 1)

        def dve_l_keep(dve, g):
            wait(dve, s["rT_ok"], g + 1)
            dve.tensor_scalar(k.xnT[:, bass.ds(g * GB, GB), :], rT[:], 1.0, None, ALU.mult).then_inc(s["rT_kept"], 1)

        def pe_l_logits(pe, g):
            if isinstance(g, int) and g == 0:
                pe.wait_ge(k.late_loaded, 16 * k.late_loads)
            wait(pe, s["lg_ok"], g)
            wait(pe, s["pk_ok"], min(g + 5, GROUPS) if isinstance(g, int) else g + 5)
            wait(pe, s["rT_ok"], g + 1)
            for b in range(GB):
                ins = pe.matmul(cc[:, LG + b * EXPERTS:LG + (b + 1) * EXPERTS], rT[:, b, :], k.w_router[:],
                                start=(b == 0), stop=(b == GB - 1), skip_group_check=True)
            ins.then_inc(s["lg_ps"], 1)

        def dve_l_logits(dve, g):
            wait(dve, s["lg_ps"], g + 1)
            dve.tensor_scalar(k.logits[:, bass.ds(g * GB, GB), :],
                              cc[:, LG:LG + GB * EXPERTS].rearrange("p (b e) -> p b e", b=GB), 1.0, None, ALU.mult)\
                .then_inc(s["lg_ok"], 1)

        def pe_slot(pe, g, p, on):
            q = 1 - p
            if on["z"]:
                pe_z_scores(pe, g, p, 0)
            if on["w"]:
                pe_z_sums(pe, g - 1, q, 3)
            if on["y"]:
                pe_y_transpose(pe, g + 1, q)
            if on["z"]:
                pe_z_scores(pe, g, p, 1)
            if on["y"]:
                pe_y_maxima(pe, g + 1, q)
            if on["z"]:
                pe_z_sums(pe, g, p, 0)
            if on["x"]:
                pe_x_transpose(pe, g + 2, p)
            if on["z"]:
                pe_z_scores(pe, g, p, 2)
            if on["l"]:
                pe_l_transpose(pe, g - 3)
            if on["z"]:
                pe_z_sums(pe, g, p, 1)
            if on["x"]:
                pe_x_values(pe, g + 2, p)
            if on["w"]:
                pe_w_transpose(pe, g - 1, q)
            if on["z"]:
                pe_z_scores(pe, g, p, 3)
                pe_z_sums(pe, g, p, 2)
            if on["w"]:
                pe_w_project(pe, g - 1, q)
            if on["l"]:
                pe_l_logits(pe, g - 3)

        def dve_slot(dve, g, p, on):
            q = 1 - p
            if on["z"]:
                dve_z_compare(dve, g, p, 0, 0)
                dve_z_compare(dve, g, p, 0, 1)
            if on["w"]:
                dve_z_post(dve, g - 1, q, 3)
            if on["y"]:
                dve_y_max(dve, g + 1, q)
            if on["w"]:
                dve_z_den(dve, g - 1, 3)
            if on["z"]:
                dve_z_compare(dve, g, p, 1, 0)
            if on["w"]:
                dve_z_rden(dve, g - 1, 3)
            if on["y"]:
                dve_y_small(dve, g + 1, q)
            if on["z"]:
                dve_z_compare(dve, g, p, 1, 1)
            if on["l"]:
                dve_r_keep(dve, g - 3)
            if on["r"]:
                dve_r_stats(dve, g - 2)
            if on["z"]:
                dve_z_post(dve, g, p, 0)
                dve_z_compare(dve, g, p, 2, 0)
                dve_z_den(dve, g, 0)
                dve_z_compare(dve, g, p, 2, 1)
                dve_z_rden(dve, g, 0)
            if on["n"]:
                dve_x_stats(dve, g + 3, q)
            if on["z"]:
                dve_z_post(dve, g, p, 1)
                dve_z_compare(dve, g, p, 3, 0)
                dve_z_den(dve, g, 1)
                dve_z_compare(dve, g, p, 3, 1)
                dve_z_rden(dve, g, 1)
            if on["l"]:
                dve_l_keep(dve, g - 3)
            if on["r"]:
                dve_r_shift(dve, g - 2)
            if on["n"]:
                dve_x_shift(dve, g + 3, q)
            if on["z"]:
                dve_z_post(dve, g, p, 2)
            if on["w"]:
                dve_w_add(dve, g - 1, q)
            if on["z"]:
                dve_z_den(dve, g, 2)
                dve_z_rden(dve, g, 2)
            if on["l"]:
                dve_l_logits(dve, g - 3)

        def act_slot(act, g, p, on):
            q = 1 - p
            if on["y"]:
                act_x_scores(act, g + 1, q)
                act_y_hi(act, g + 1, q)
                act_x_values(act, g + 1, q)
            if on["l"]:
                act_r_apply(act, g - 3)
            if on["y"]:
                act_y_exp(act, g + 1, q)
            if on["x"]:
                act_x_xT(act, g + 2, p)
            if on["l"]:
                act_l_rT(act, g - 3)
            if on["y"]:
                act_y_vhi(act, g + 1, q)
            if on["r"]:
                act_r_rstd(act, g - 2)
            if on["n"]:
                act_x_rstd(act, g + 3, q)
            if on["w"]:
                act_w_hT(act, g - 1, q)
            if on["y"]:
                act_y_vmid(act, g + 1, q)
            if on["n"]:
                act_x_apply(act, g + 3, q)

        def pool_slot(pool, g, p, on):
            q = 1 - p
            if on["w"]:
                pool_z_post(pool, g - 1, q, 3)
            if on["y"]:
                pool_y_scale(pool, g + 1, q)
            if on["z"]:
                pool_z_post(pool, g, p, 0)
            if on["y"]:
                pool_y_res(pool, g + 1, q)
            if on["z"]:
                pool_z_post(pool, g, p, 1)
            if on["y"]:
                pool_y_lo(pool, g + 1, q)
            if on["z"]:
                pool_z_post(pool, g, p, 2)

        def slots(slot, eng):
            def on(g):
                def runs(group):
                    return 0 <= group < GROUPS
                return dict(l=runs(g - 3), r=runs(g - 2), w=runs(g - 1), z=runs(g), y=runs(g + 1), x=runs(g + 2),
                            n=runs(g + 3))
            everything = on(3)
            first, last = 4, GROUPS - 4
            for g in range(-2, first):
                slot(eng, g, g % 2, on(g))
            with eng.Fori(first // 2, last // 2) as i:
                for p in range(2):
                    slot(eng, i * 2 + p, p, everything)
            for g in range(last, GROUPS + 3):
                slot(eng, g, g % 2, on(g))

        with nc.Block() as block:
            @block.sync
            def _(sp):
                def load_late(dst, src):
                    sp.dma_start(dst, src, allow_slow_non_contiguous=True).then_inc(k.late_loaded, 16)

                load_late(k.w_fc[:, :, 0:256], a["L1_gnn_W_fc"].rearrange("(c p) n -> p c n", p=P))
                load_late(k.fold_a1[:].rearrange("p t n -> p (t n)"),
                          a["L1_gnn_a_fc"].rearrange("n o -> (n o)").partition_broadcast(P))
                load_late(k.w_hand[:, 0:D], a["L1_gnn_W_hand"])
                load_late(k.fold_a2[:].rearrange("p t n -> p (t n)"),
                          a["L1_gnn_a_hand"].rearrange("n o -> (n o)").partition_broadcast(P))
                load_late(k.w_mlp1[:], a["L1_gnn_mlp1_w"])
                load_late(k.w_mlp2[:], a["L1_gnn_mlp2_w"].rearrange("(c p) n -> p c n", p=P))
                load_late(k.b_mlp1[:], a["L1_gnn_mlp1_b"].rearrange("(c p) -> p c", p=P))
                load_late(k.b_mlp2[:], a["L1_gnn_mlp2_b"].rearrange("(p o) -> p o", o=1))
                load_late(k.w_router[:], a["L0_ffn_Wr"])
                load_late(k.w1_shared[:], a["L0_ffn_W1s"])
                load_late(k.w2_shared[:], a["L0_ffn_W2s"].rearrange("(c p) n -> p c n", p=P))
                load_late(k.b1_shared[:], a["L0_ffn_b1s"].rearrange("(c p) -> p c", p=P))
                load_late(k.b2_shared[:], a["L0_ffn_b2s"].partition_broadcast(P))
                load_late(k.w1_last[:], a["L1_ffn_w1"])
                load_late(k.w2_last[:], a["L1_ffn_w2"].rearrange("(c p) n -> p c n", p=P))
                load_late(k.b1_last[:], a["L1_ffn_b1"].rearrange("(c p) -> p c", p=P))
                load_late(k.b2_last[:], a["L1_ffn_b2"].partition_broadcast(P))
                load_late(k.wr_last[:], a["L1_ffn_wr"])
                load_late(k.br_last[:], a["L1_ffn_br"].partition_broadcast(P))
                rows = k.rows_in.rearrange("(p n) d -> p (n d)", p=P)
                for c in range(k.zero_dmas):
                    sp.dma_start(rows[:, 2048 * c:2048 * c + 2048], k.zeros[:]).then_inc(k.slots_zeroed, 16)
                sp.wait_ge(k.slots_zeroed, 16 * k.zero_dmas)

            @block.vector
            def _(dve):
                dve_x_stats(dve, 0, 0)
                dve_x_shift(dve, 0, 0)
                slots(dve_slot, dve)

            @block.scalar
            def _(act):
                exp_ln_tables(nc, act)
                act_x_rstd(act, 0, 0)
                act_x_apply(act, 0, 0)
                slots(act_slot, act)

            @block.gpsimd
            def _(pool):
                slots(pool_slot, pool)

            @block.tensor
            def _(pe):
                slots(pe_slot, pe)
        sems.clear()


def persistent(nc, ctx):
    def sb(name, shape, dt=F32):
        return buffer(nc, ctx, name, shape, dt)
    k = Buffers()
    k.x = sb("x_tok", [P, BATCHES, D])
    k.ident = sb("ident", [P, P])
    k.ones = sb("ones", [P, P])
    k.tri = sb("tri", [P, P])
    k.cap = sb("cap", [P, P])
    k.eps_ln = sb("eps_ln", [P, 1])
    k.eps_prior = sb("eps_prior", [P, 1])
    k.neg_one = sb("neg_one", [P, 1])
    k.w_fc = sb("w_fc", [P, 2, 258])
    k.w_hand = sb("w_hand", [P, D + 2])
    k.w_f2_fc = sb("w_f2_fc", [P, 2, P])
    k.w_f2_hand = sb("w_f2_hand", [P, P])
    k.w_mlp1 = sb("w_mlp1", [P, 256])
    k.w_mlp2 = sb("w_mlp2", [P, 2, D])
    k.fold_a1, k.fold_a2 = sb("fold_a1", [P, 2, 256]), sb("fold_a2", [P, 2, P])
    k.b_mlp1 = sb("b_mlp1", [P, 2])
    k.b_mlp2 = sb("b_mlp2", [P, 1])
    k.w_router = sb("w_router", [P, 8])
    k.w1_shared = sb("w1_shared", [P, 512])
    k.w2_shared = sb("w2_shared", [P, 4, D])
    k.b1_shared = sb("b1_shared", [P, 4])
    k.b2_shared = sb("b2_shared", [P, D])
    k.w1_last = sb("w1_last", [P, 512])
    k.w2_last = sb("w2_last", [P, 4, D])
    k.b1_last = sb("b1_last", [P, 4])
    k.b2_last = sb("b2_last", [P, D])
    k.wr_last = sb("wr_last", [P, 1])
    k.br_last = sb("br_last", [P, 1])
    k.wr_rep = sb("wr_rep", [P, P])
    k.mean_var = sb("mean_var", [P, BATCHES, 2])
    k.slots = sb("slots", [P, 2, BATCHES], I32)
    k.weights = sb("weights", [P, 2, BATCHES])
    k.tile_expert = sb("tile_expert", [1, 72], I32)
    k.rows_in = nc.dram_tensor("slot_rows_in", [SLOTS, D], F32, kind="Internal").ap()
    k.rows_out = nc.dram_tensor("slot_rows_out", [SLOTS, D], F32, kind="Internal").ap()
    k.slots_zeroed = ctx.enter_context(nc.semaphore("slots_zeroed"))
    k.zero_dmas = 9
    k.expert_dmas = 32
    k.experts_loaded = ctx.enter_context(nc.semaphore("experts_loaded"))
    k.late_loads = 19
    k.late_loaded = ctx.enter_context(nc.semaphore("late_loaded"))
    k.x_loaded = [ctx.enter_context(nc.semaphore(f"x_loaded{q}")) for q in range(4)]
    return k


def add_attention_buffers(nc, ctx, k):
    def sb(name, shape, dt=F32):
        return buffer(nc, ctx, name, shape, dt)
    k.diag32, k.zeros = sb("diag32", [P, 32]), sb("zeros", [P, 2048])
    k.sel_s, k.sel_d = sb("sel_s", [P, HB, P], BF16), sb("sel_d", [P, HB, P], BF16)
    k.mT, k.neg_mT, k.neg_uT = sb("mT", [P, P], BF16), sb("neg_mT", [P, P], BF16), sb("neg_uT", [P, P])
    k.w_heads, k.w_outT = sb("w_heads", [P, D + 32]), sb("w_outT", [P, D])
    k.v17 = [sb(f"v17_{p}", [P, HB, VW]) for p in range(2)]


def add_token_buffers(nc, ctx, k):
    def sb(name, shape, dt=F32):
        return buffer(nc, ctx, name, shape, dt)
    k.xn, k.xnT = sb("xn_all", [P, BATCHES, D]), sb("xnT_all", [P, BATCHES, P])
    k.logits = sb("logits", [P, BATCHES, EXPERTS])


def add_expert_buffers(nc, ctx, k):
    k.w_experts = buffer(nc, ctx, "w_experts", [P, EXPERTS, EW])
    k.expert = [buffer(nc, ctx, f"expert{q}", [P, FETCHED]) for q in range(AHEAD)]
    k.expert_in = [ctx.enter_context(nc.semaphore(f"expert_in{q}")) for q in range(AHEAD)]


def router_phase(nc, k, a):
    with ExitStack() as ctx:
        def sb(name, shape, dt=F32):
            return buffer(nc, ctx, "r_" + name, shape, dt)

        def ps(name, shape):
            return ctx.enter_context(nc.psum_tensor("r_" + name, shape, F32))

        def sem(name):
            return ctx.enter_context(nc.semaphore("r_" + name))

        BE = [P, BATCHES, EXPERTS]
        logits, cand, left = k.logits, sb("cand", BE), sb("left", BE)
        first, second, both = sb("first", BE), sb("second", BE), sb("both", BE)
        top = sb("top", [P, 2, BATCHES])
        which = sb("which", [P, 2, BATCHES])
        em8 = sb("em8", [P, EXPERTS])
        k256 = sb("k256", [P, MAX_TILES_OF_ONE])
        tiles_i = sb("tiles_i", [P, TILES])
        tot_b = sb("tot_b", [BATCHES, EXPERTS])
        prefix_rhs = sb("prefix_rhs", [BATCHES, BATCHES, EXPERTS])
        total = sb("total", [P, EXPERTS])
        over = sb("over", [P, EXPERTS, MAX_TILES_OF_ONE])
        n_tiles, end, base = sb("n_tiles", [P, EXPERTS]), sb("end", [P, EXPERTS]), sb("base", [P, EXPERTS])
        upto = sb("upto", [P, EXPERTS, EXPERTS])
        slot_f = sb("slot_f", [P, 2, BATCHES])
        past = sb("past", [1, TILES, EXPERTS])
        tile_e = sb("tile_e", [1, TILES])

        prefix = ps("prefix", [P, BATCHES * EXPERTS])
        counts = ps("counts", [P, 512])

        s = {n: sem(n) for n in (
            "iota", "d", "e", "tot_ps", "pre_ps")}

        def over_experts(ap):
            return ap.unsqueeze(2).to_broadcast(BE)

        with nc.Block() as block:
            @block.sync
            def _(sp):
                for e in range(EXPERTS):
                    def load(dst, src):
                        sp.dma_start(dst, src, allow_slow_non_contiguous=True).then_inc(k.experts_loaded, 16)
                    load(k.w_experts[:, e, 0:F], a["L0_ffn_W1p"][e])
                    load(k.w_experts[:, e, F:F + FC], a["L0_ffn_b1p"][e].rearrange("(c p) -> p c", p=P))
                    load(k.w_experts[:, e, F + FC:FETCHED], a["L0_ffn_b2p"][e].partition_broadcast(P))
                    load(k.w_experts[:, e, FETCHED:EW].rearrange("p (c n) -> p c n", c=FC),
                         a["L0_ffn_W2p"][e].rearrange("(c p) n -> p c n", p=P))

            @block.gpsimd
            def _(pool):
                pool.iota(em8[:], [[1, EXPERTS]], base=-EXPERTS, channel_multiplier=0,
                          allow_small_or_imprecise_dtypes=True)
                pool.iota(k256[:], [[TILE, MAX_TILES_OF_ONE]], base=0, channel_multiplier=0,
                          allow_small_or_imprecise_dtypes=True)
                pool.iota(tiles_i[:], [[1, TILES]], base=0, channel_multiplier=0,
                          allow_small_or_imprecise_dtypes=True).then_inc(s["iota"], 1)

            @block.scalar
            def _(act):
                exp_ln_tables(nc, act)
                act.wait_ge(s["d"], 11)
                nc.scalar.activation(top[:, 1], which[:, 0], ACT.Exp).then_inc(s["e"], 1)

            @block.tensor
            def _(pe):
                pe.wait_ge(s["d"], 10)
                for e in range(EXPERTS):
                    pe.matmul(counts[0:BATCHES, e:e + 1], both[:, :, e], k.ones[:, 0:1], start=(e == 0),
                              stop=(e == EXPERTS - 1), skip_group_check=True)
                pe.matmul(prefix[:], k.tri[:], both[:].rearrange("p b e -> p (b e)"), start=True, stop=False,
                          skip_group_check=True).then_inc(s["tot_ps"], 1)
                pe.wait_ge(s["d"], 16)
                pe.matmul(prefix[:], k.ones[0:BATCHES, :], prefix_rhs[:].rearrange("p b e -> p (b e)"),
                          start=False, stop=True, skip_group_check=True)
                pe.matmul(counts[:, 64:64 + EXPERTS], k.ones[0:BATCHES, :], tot_b[:], start=True, stop=True)\
                    .then_inc(s["pre_ps"], 1)

            @block.vector
            def _(dve):
                n = [0]

                def chain(ins):
                    n[0] += 1
                    ins.then_inc(s["d"], 1)
                    dve.wait_ge(s["d"], n[0])

                dve.wait_ge(s["iota"], 1)
                e_of = em8[:].unsqueeze(1).to_broadcast(BE)
                chain(dve.tensor_reduce(top[:, 0], logits[:], AX.X, ALU.max))
                chain(dve.tensor_tensor(cand[:], logits[:], over_experts(top[:, 0]), ALU.is_equal))
                chain(dve.tensor_tensor(cand[:], cand[:], e_of, ALU.mult))
                chain(dve.tensor_reduce(which[:, 0], cand[:], AX.X, ALU.min))
                chain(dve.tensor_tensor(first[:], over_experts(which[:, 0]), e_of, ALU.is_equal))
                chain(dve.scalar_tensor_tensor(left[:], first[:], -BIG, logits[:], ALU.mult, ALU.add))
                dve.tensor_reduce(top[:, 1], left[:], AX.X, ALU.max).then_inc(s["e"], 1)
                dve.wait_ge(s["e"], 1)
                chain(dve.tensor_tensor(cand[:], left[:], over_experts(top[:, 1]), ALU.is_equal))
                dve.tensor_tensor(cand[:], cand[:], e_of, ALU.mult).then_inc(s["e"], 1)
                dve.wait_ge(s["e"], 2)
                chain(dve.tensor_reduce(which[:, 1], cand[:], AX.X, ALU.min))
                chain(dve.tensor_tensor(second[:], over_experts(which[:, 1]), e_of, ALU.is_equal))
                chain(dve.tensor_tensor(both[:], first[:], second[:], ALU.add))
                chain(dve.tensor_tensor(which[:, 0], top[:, 1], top[:, 0], ALU.subtract))
                dve.wait_ge(s["e"], 3)
                chain(dve.tensor_scalar(top[:, 0], top[:, 1], 1.0, None, ALU.add))
                chain(dve.reciprocal(k.weights[:, 0], top[:, 0]))
                chain(dve.tensor_tensor(k.weights[:, 1], top[:, 1], k.weights[:, 0], ALU.mult))
                dve.wait_ge(s["tot_ps"], 1)
                chain(dve.tensor_copy(tot_b[:], counts[0:BATCHES, 0:EXPERTS]))
                chain(dve.tensor_tensor(prefix_rhs[:],
                                        k.tri[0:BATCHES, 0:BATCHES].unsqueeze(2)
                                        .to_broadcast([BATCHES, BATCHES, EXPERTS]),
                                        tot_b[:].unsqueeze(1).to_broadcast([BATCHES, BATCHES, EXPERTS]),
                                        ALU.mult))
                dve.wait_ge(s["pre_ps"], 1)
                chain(dve.tensor_copy(total[:], counts[:, 64:64 + EXPERTS]))
                OV = [P, EXPERTS, MAX_TILES_OF_ONE]
                chain(dve.tensor_tensor(over[:], total[:].unsqueeze(2).to_broadcast(OV),
                                        k256[:].unsqueeze(1).to_broadcast(OV), ALU.is_gt))
                chain(dve.tensor_reduce(n_tiles[:], over[:], AX.X, ALU.add))
                EE = [P, EXPERTS, EXPERTS]
                chain(dve.tensor_tensor(upto[:], em8[:].unsqueeze(2).to_broadcast(EE),
                                        em8[:].unsqueeze(1).to_broadcast(EE), ALU.is_ge))
                chain(dve.tensor_tensor(upto[:], upto[:], n_tiles[:].unsqueeze(1).to_broadcast(EE), ALU.mult))
                chain(dve.tensor_reduce(end[:], upto[:], AX.X, ALU.add))
                chain(dve.tensor_tensor(base[:], end[:], n_tiles[:], ALU.subtract))
                chain(dve.tensor_scalar(base[:], base[:], float(TILE), None, ALU.mult))
                chain(dve.tensor_tensor(left[:], prefix[:].rearrange("p (b e) -> p b e", b=BATCHES),
                                        base[:].unsqueeze(1).to_broadcast(BE), ALU.add))
                dve.tensor_tensor(first[:], first[:], left[:], ALU.mult)
                chain(dve.tensor_tensor(second[:], second[:], left[:], ALU.mult))
                dve.tensor_reduce(slot_f[:, 0], first[:], AX.X, ALU.add)
                chain(dve.tensor_reduce(slot_f[:, 1], second[:], AX.X, ALU.add))
                chain(dve.tensor_copy(k.slots[:], slot_f[:]))
                TE = [1, TILES, EXPERTS]
                chain(dve.tensor_tensor(past[:], tiles_i[0:1].unsqueeze(2).to_broadcast(TE),
                                        end[0:1].unsqueeze(1).to_broadcast(TE), ALU.is_ge))
                chain(dve.tensor_reduce(tile_e[:], past[:], AX.X, ALU.add))
                chain(dve.tensor_scalar(tile_e[:], tile_e[:], float(EXPERTS - 1), None, ALU.min))
                chain(dve.tensor_copy(k.tile_expert[:], tile_e[:]))


def expert_of(eng, k, t):
    return eng.value_load(k.tile_expert[0:1, bass.ds(t, 1)], min_val=0, max_val=EXPERTS - 1)


def fetch_expert(sp, k, t, q):
    e = expert_of(sp, k, t)
    sp.dma_start(k.expert[q][:], k.w_experts[:, bass.ds(e, 1), 0:FETCHED].rearrange("p o n -> p (o n)"))\
        .then_inc(k.expert_in[q], 16)


def shared_expert_phase(nc, k):
    with ExitStack() as ctx:
        def sb(name, shape, dt=F32):
            return buffer(nc, ctx, "s_" + name, shape, dt)

        def ps(name, shape):
            return ctx.enter_context(nc.psum_tensor("s_" + name, shape, F32))

        def sem(name):
            return ctx.enter_context(nc.semaphore("s_" + name))

        hT = [sb(f"hT{p}", [P, FC, GB * P]) for p in range(2)]
        yb = [sb(f"yb{p}", [P, GB, D]) for p in range(2)]
        hp = ps("hp", [P, FC, 512])
        yp = [ps(f"yp{p}", [P, 512]) for p in range(2)]
        s = {n: sem(n) for n in ("h_ps", "h_ok", "y_ps", "y_read", "x_ok", "scattered", "d")}
        fold_p1, fold_1 = sb("fold_p1", [P, 2, 2, 256]), sb("fold_1", [P, 2, 2])
        fold_p2, fold_2 = sb("fold_p2", [P, 2, P]), sb("fold_2", [P, 2])

        def pe_up(pe, g, p):
            for c in range(FC):
                wait(pe, s["h_ok"], (g - 1) * FC + c + 1)
                pe.matmul(hp[:, c, :], k.w1_shared[:, c * P:(c + 1) * P],
                          k.xnT[:, bass.ds(g * GB, GB), :], start=True, stop=True).then_inc(s["h_ps"], 1)

        def pe_down(pe, g, p):
            wait(pe, s["y_read"], g - 1)
            for c in range(FC):
                wait(pe, s["h_ok"], g * FC + c + 1)
                for b in range(GB):
                    ins = pe.matmul(yp[p][:, b * P:(b + 1) * P], hT[p][:, c, b * P:(b + 1) * P], k.w2_shared[:, c, :],
                                    start=(c == 0 and b == 0), stop=(c == FC - 1), skip_group_check=True)
            ins.then_inc(s["y_ps"], 1)

        def act_gelu(act, g, p):
            wait(act, s["y_ps"], g - 1)
            for c in range(FC):
                wait(act, s["h_ps"], g * FC + c + 1)
                nc.scalar.activation(hT[p][:, c, :], hp[:, c, :], ACT.Gelu, bias=k.b1_shared[:, c:c + 1])\
                    .then_inc(s["h_ok"], 1)

        def dve_add(dve, g, p):
            wait(dve, s["y_ps"], g + 1)
            wait(dve, s["x_ok"], g - 1)
            dve.tensor_tensor(yb[p][:], yp[p][:].rearrange("p (b d) -> p b d", b=GB),
                              k.b2_shared[:].unsqueeze(1).to_broadcast([P, GB, D]), ALU.add).then_inc(s["y_read"], 1)
            wait(dve, s["y_read"], g + 1)
            xg = k.x[:, bass.ds(g * GB, GB), :]
            dve.tensor_tensor(xg, xg, yb[p][:], ALU.add).then_inc(s["x_ok"], 1)

        def paired(body, eng):
            for g in range(2):
                body(eng, g, g)
            with eng.Fori(1, GROUPS // 2) as i:
                for p in range(2):
                    body(eng, i * 2 + p, p)

        def pe_slot(pe, g, p):
            if not isinstance(g, int) or g + 1 < GROUPS:
                pe_up(pe, g + 1, 1 - p)
            pe_down(pe, g, p)

        with nc.Block() as block:
            @block.sync
            def _(sp):
                sp.wait_ge(k.experts_loaded, 16 * k.expert_dmas)
                for t in range(AHEAD):
                    fetch_expert(sp, k, t, t)

            @block.tensor
            def _(pe):
                pe_up(pe, 0, 0)
                for g in range(2):
                    pe_slot(pe, g, g)
                with pe.Fori(1, GROUPS // 2 - 1) as i:
                    for p in range(2):
                        pe_slot(pe, i * 2 + p, p)
                for g in range(GROUPS - 2, GROUPS):
                    pe_slot(pe, g, g % 2)

            @block.scalar
            def _(act):
                paired(act_gelu, act)

            @block.vector
            def _(dve):
                n = [0]

                def chain(ins):
                    n[0] += 1
                    ins.then_inc(s["d"], 1)
                    dve.wait_ge(s["d"], n[0])

                for c in range(2):
                    for t in range(2):
                        ins = dve.tensor_tensor(fold_p1[:, c, t], k.w_fc[:, c, 0:256], k.fold_a1[:, t], ALU.mult)
                chain(ins)
                chain(dve.tensor_reduce(fold_1[:], fold_p1[:], AX.X, ALU.add))
                for t in range(2):
                    ins = dve.tensor_tensor(fold_p2[:, t], k.w_hand[:, 0:D], k.fold_a2[:, t], ALU.mult)
                chain(ins)
                chain(dve.tensor_reduce(fold_2[:], fold_p2[:], AX.X, ALU.add))
                dve.tensor_copy(k.w_fc[:, :, 256:258], fold_1[:])
                dve.tensor_copy(k.w_hand[:, D:D + 2], fold_2[:])
                dve.tensor_copy(k.wr_rep[:], k.wr_last[:].to_broadcast([P, P]))
                dve.tensor_copy(k.w_f2_fc[:], fold_1[:, :, 1:2].to_broadcast([P, 2, P]))
                chain(dve.tensor_copy(k.w_f2_hand[:], fold_2[:, 1:2].to_broadcast([P, P])))
                paired(dve_add, dve)

            @block.gpsimd
            def _(pool):
                pool.wait_ge(k.slots_zeroed, 16 * k.zero_dmas)
                for b in range(BATCHES):
                    for c in range(TOPK):
                        pool.indirect_dma_start(k.rows_in, bass.IndirectOffsetOnAxis(ap=k.slots[:, c, b:b + 1], axis=0),
                                                k.xn[:, b, :], None).then_inc(s["scattered"], 16)
                pool.wait_ge(s["scattered"], 16 * TOPK * BATCHES)


def routed_experts_phase(nc, k):
    with ExitStack() as ctx:
        def sb(name, shape, dt=F32):
            return buffer(nc, ctx, "e_" + name, shape, dt)

        def ps(name, shape):
            return ctx.enter_context(nc.psum_tensor("e_" + name, shape, F32))

        def sem(name):
            return ctx.enter_context(nc.semaphore("e_" + name))

        H = TILE // P
        U = AHEAD
        wt, w_in = k.expert, k.expert_in
        xt = [sb(f"xt{q}", [P, H, D]) for q in range(U)]
        xh, xl = [[sb(f"x{c}{p}", [P, TILE], F32R) for p in range(2)] for c in "hl"]
        wh, wl = [[sb(f"w{c}{p}", [P, F], F32R) for p in range(2)] for c in "hl"]
        hT = [sb(f"hT{p}", [P, FC, TILE]) for p in range(2)]
        yt = [sb(f"yt{q}", [P, H, D]) for q in range(U)]
        tp = ps("tp", [P, TILE])
        hp = [ps(f"hp{c}", [P, 512]) for c in range(FC)]
        yp = [ps(f"yp{p}", [P, H * D]) for p in range(2)]
        s = {n: sem(n) for n in ("tp_ps", "xh_ok", "xT_ok", "wh_ok", "wl_ok", "h_ps", "h_ok", "y_ps", "y_ok")}
        x_in = [sem(f"x_in{q}") for q in range(U)]
        out = [sem(f"out{q}") for q in range(U)]

        def sp_load(sp, i, q):
            t = i * U + q
            wait(sp, s["tp_ps"], t - U + 1)
            if not isinstance(i, int) or i > 0:
                wait(sp, s["y_ok"], t - U + 1)
            sp.dma_start(xt[q][:], k.rows_in[bass.ds(t * TILE, TILE), :].rearrange("(h p) d -> p h d", p=P))\
                .then_inc(x_in[q], 16)
            if not isinstance(i, int) or i > 0:
                fetch_expert(sp, k, t, q)

        def sp_store(sp, i, q, waits):
            t = i * U + q
            if waits:
                wait(sp, s["y_ok"], t + 1)
            sp.dma_start(k.rows_out[bass.ds(t * TILE, TILE), :].rearrange("(h p) d -> p h d", p=P), yt[q][:])\
                .then_inc(out[q], 16)

        def pe_transpose(pe, i, q):
            t = i * U + q
            wait(pe, x_in[q], i * 16 + 16)
            wait(pe, s["xT_ok"], t)
            for h in range(H):
                ins = pe.transpose(tp[:, h * P:(h + 1) * P], xt[q][:, h, :], k.ident[:])
            ins.then_inc(s["tp_ps"], 1)

        def dve_xT(dve, i, q):
            t = i * U + q
            wait(dve, s["tp_ps"], t + 1)
            wait(dve, s["h_ps"], (t - 1) * FC)
            dve.tensor_copy(xh[q % 2][:], tp[:]).then_inc(s["xh_ok"], 1)
            wait(dve, s["xh_ok"], t + 1)
            dve.tensor_tensor(xl[q % 2][:], tp[:], xh[q % 2][:].bitcast(F32), ALU.subtract).then_inc(s["xT_ok"], 1)

        def act_w_high(act, i, q):
            t = i * U + q
            wait(act, s["h_ps"], (t - 1) * FC)
            wait(act, w_in[q], i * 16 + 16)
            nc.scalar.copy(wh[q % 2][:], wt[q][:, 0:F]).then_inc(s["wh_ok"], 1)

        def dve_w_low(dve, i, q):
            t = i * U + q
            wait(dve, s["wh_ok"], t + 1)
            dve.tensor_tensor(wl[q % 2][:], wt[q][:, 0:F], wh[q % 2][:].bitcast(F32), ALU.subtract)\
                .then_inc(s["wl_ok"], 1)

        def pe_up(pe, i, q):
            t = i * U + q
            wait(pe, s["wl_ok"], t + 1)
            wait(pe, s["xT_ok"], t + 1)
            for c in range(FC):
                wait(pe, s["h_ok"], (t - 1) * FC + c + 1)
                at, out_c = slice(c * P, (c + 1) * P), hp[c][:, 0:TILE]
                pe.matmul(out_c, wh[q % 2][:, at], xh[q % 2][:], start=True, stop=False)
                pe.matmul(out_c, wh[q % 2][:, at], xl[q % 2][:], start=False, stop=False)
                pe.matmul(out_c, wl[q % 2][:, at], xh[q % 2][:], start=False, stop=True).then_inc(s["h_ps"], 1)

        def act_gelu(act, i, q):
            t = i * U + q
            wait(act, s["y_ps"], t - 1)
            for c in range(FC):
                wait(act, s["h_ps"], t * FC + c + 1)
                nc.scalar.activation(hT[q % 2][:, c, :], hp[c][:, 0:TILE], ACT.Gelu,
                                     bias=wt[q][:, F + c:F + c + 1]).then_inc(s["h_ok"], 1)

        def pe_down(pe, i, q):
            t = i * U + q
            e = expert_of(pe, k, t)
            wait(pe, s["y_ok"], t - 1)
            for c in range(FC):
                wait(pe, s["h_ok"], t * FC + c + 1)
                w2 = k.w_experts[:, bass.ds(e, 1), FETCHED + c * D:FETCHED + (c + 1) * D]
                for h in range(H):
                    ins = pe.matmul(yp[q % 2][:, h * D:(h + 1) * D], hT[q % 2][:, c, h * P:(h + 1) * P], w2,
                                    start=(c == 0 and h == 0), stop=(c == FC - 1), skip_group_check=True)
            ins.then_inc(s["y_ps"], 1)

        def dve_bias(dve, i, q):
            t = i * U + q
            wait(dve, s["y_ps"], t + 1)
            wait(dve, out[q], i * 16)
            dve.tensor_tensor(yt[q][:], yp[q % 2][:].rearrange("p (h d) -> p h d", h=H),
                              wt[q][:, F + FC:FETCHED].unsqueeze(1).to_broadcast([P, H, D]), ALU.add)\
                .then_inc(s["y_ok"], 1)

        def ahead(i, q, n):
            return (i + (q + n) // U, (q + n) % U)

        def pe_slot(pe, i, q, more):
            if more > 1:
                pe_transpose(pe, *ahead(i, q, 2))
            if more > 0:
                pe_up(pe, *ahead(i, q, 1))
            pe_down(pe, i, q)

        def dve_slot(dve, i, q, more):
            if more > 1:
                dve_w_low(dve, *ahead(i, q, 2))
                dve_xT(dve, *ahead(i, q, 2))
            dve_bias(dve, i, q)

        def act_slot(act, i, q, more):
            if more > 1:
                act_w_high(act, *ahead(i, q, 2))
            if more > 0:
                act_gelu(act, *ahead(i, q, 1))

        def sp_slot(sp, i, q, more):
            if more >= U:
                sp_load(sp, i + 1, q)
            sp_store(sp, i, q, waits=more < U)

        def tiles(slot, eng):
            for q in range(U):
                slot(eng, 0, q, U)
            with eng.Fori(1, TILES // U - 1) as i:
                for q in range(U):
                    slot(eng, i, q, U)
            for q in range(U):
                slot(eng, TILES // U - 1, q, U - 1 - q)

        with nc.Block() as block:
            @block.sync
            def _(sp):
                sp.wait_ge(k.experts_loaded, 16 * k.expert_dmas)
                for q in range(U):
                    sp_load(sp, 0, q)
                tiles(sp_slot, sp)
                for q in range(U):
                    sp.wait_ge(out[q], 16 * (TILES // U))

            @block.tensor
            def _(pe):
                pe.wait_ge(k.experts_loaded, 16 * k.expert_dmas)
                pe_transpose(pe, 0, 0)
                pe_up(pe, 0, 0)
                pe_transpose(pe, 0, 1)
                tiles(pe_slot, pe)

            @block.vector
            def _(dve):
                for q in range(2):
                    dve_w_low(dve, 0, q)
                    dve_xT(dve, 0, q)
                tiles(dve_slot, dve)

            @block.scalar
            def _(act):
                for q in range(2):
                    act_w_high(act, 0, q)
                act_gelu(act, 0, 0)
                tiles(act_slot, act)


H1, FD = 2, 2 * D
W1C = FD + 1
W1S = FD + 4
W2C = D + 1


def combine_graph_phase(nc, k):
    with ExitStack() as ctx:
        def sb(name, shape, dt=F32):
            return buffer(nc, ctx, "g_" + name, shape, dt)

        def ps(name, shape):
            return ctx.enter_context(nc.psum_tensor("g_" + name, shape, F32))

        def sem(name):
            return ctx.enter_context(nc.semaphore("g_" + name))

        G4 = [P, GB, P]
        y_slot = [sb(f"y{c}", [P, BATCHES, D]) for c in range(TOPK)]
        st, fence, lnv = sb("st", [P, GB, 6]), sb("fence", [P, 1]), sb("lnv", [P, GB])
        mv = [sb(f"mv{p}", [P, GB, 2]) for p in range(2)]
        st4, mv4, fence4 = sb("st4", [P, GB, 6]), sb("mv4", [P, GB, 2]), sb("fence4", [P, 1])
        rstd = [sb(f"rstd{p}", [P, GB]) for p in range(2)]
        xn, xT = sb("xn", G4), sb("xT", [P, GB * P])
        r1T = [sb(f"r1T{p}", [P, H1, GB * P]) for p in range(2)]
        h1 = [sb(f"h1{p}", [P, GB, W1S]) for p in range(2)]
        y1, e1, p1, pn1 = sb("sum1", G4), sb("e1", G4), sb("p1", G4), sb("pn1", G4)
        nmax1, den1, rden1 = sb("nmax1", [P, GB]), sb("den1", [P, GB]), sb("rden1", [P, GB])
        p1T = sb("p1T", [P, GB * P])
        v1, w1, t1, u1 = (sb(n, [P, H1, GB * P]) for n in ("v1", "w1", "t1", "u1"))
        r2T = [sb(f"r2T{p}", [P, GB * P]) for p in range(2)]
        h2 = sb("h2", [P, GB, W2C])
        y2, l2, e2, p2 = sb("sum2", G4), sb("l2", G4), sb("e2", G4), sb("p2", G4)
        nmax2, den2 = sb("nmax2", [P, GB]), sb("den2", [P, GB])
        rden2 = [sb(f"rden2{p}", [P, GB]) for p in range(2)]
        p2T = sb("p2T", [P, GB * P])
        q2, v2, w2, t2, s2 = (sb(n, G4) for n in ("q2", "v2", "w2", "t2", "s2"))

        tb = ps("tb", [P, 512])
        mm = ps("mm", [P, H1, 512])
        hh = ps("hh", [P, 2, 512])
        ff = ps("ff", [P, 512])
        rr = ps("rr", [P, 512])
        av = ps("av", [P, 512])

        s = {n: sem(n) for n in (
            "one_in", "comb", "stats", "var", "lnv_done", "rstd_ok", "xn_ok",
            "xT_ps", "xT_ok", "r1_ps", "r1_ok",
            "h1_ps", "h1_ok", "f1_ps", "y1_ok", "l1_ok", "max1_ok", "p1_ok", "rden1_ok", "pn1_ok", "p1T_ps", "p1T_ok",
            "av1_ps", "v1_ok", "v1_cut", "w1_ok", "t1_ok", "u1_ok", "r2_ps", "r2_ok",
            "h2_ps", "h2_ok", "f2_ps", "y2_ok", "l2_ok", "e2_ok", "max2_ok", "p2_ok", "rden2_ok", "p2T_ps", "p2T_ok",
            "r2T_ps", "av2_ps", "q2_ok", "v2_ok", "v2_cut", "w2_ok", "t2_ok", "s2_ok", "x_ok", "stats4", "var4", "kept4")}
        gathered = [sem(f"gathered{p}") for p in range(2)]
        PER_GROUP = 16 * TOPK * GB

        def full(count, g, ahead):
            return count(min(g + ahead, GROUPS - 1) + 1) if isinstance(g, int) else count(g + ahead + 1)

        def batch(ap, g, b):
            return ap[:, bass.ds(g * GB + b, 1), :]

        def pool_gather(pool, g, which):
            for n in which:
                if n == 0:
                    wait(pool, gathered[g % 2], PER_GROUP * (g // 2))
                b, c = g * GB + n // TOPK, n % TOPK
                pool.indirect_dma_start(y_slot[c][:, b, :], None, k.rows_out,
                                        bass.IndirectOffsetOnAxis(ap=k.slots[:, c, b:b + 1], axis=0))\
                    .then_inc(gathered[g % 2], 16)

        def dve_n_combine(dve, g, half, p, c):
            if c == 0:
                wait(dve, gathered[p], (half + 1) * PER_GROUP)
            else:
                wait(dve, s["one_in"], g + 1)
            for b in range(GB):
                ins = dve.scalar_tensor_tensor(batch(k.x, g, b), batch(y_slot[c], g, b),
                                               k.weights[:, c, bass.ds(g * GB + b, 1)], batch(k.x, g, b),
                                               ALU.mult, ALU.add)
            ins.then_inc(s["one_in"] if c == 0 else s["comb"], 1)

        def dve_n_stats(dve, g, p):
            wait(dve, s["comb"], g + 1)
            dve.memset(fence[:], 0.0)
            layer_norm_stats(dve, lambda b: batch(k.x, g, b).rearrange("p o d -> p (o d)"),
                             st, mv[p], fence, s["stats"], g + 1, s["var"])

        def act_n_rstd(act, g, p):
            wait(act, s["var"], g + 1)
            nc.scalar.activation(lnv[:], mv[p][:, :, 1], ACT.Ln, bias=k.eps_ln[:]).then_inc(s["lnv_done"], 1)
            wait(act, s["lnv_done"], g + 1)
            nc.scalar.activation(rstd[p][:], lnv[:], ACT.Exp, scale=-0.5).then_inc(s["rstd_ok"], 1)

        def dve_n_apply(dve, g, p):
            wait(dve, s["xT_ps"], g)
            wait(dve, s["rstd_ok"], g + 1)
            for b in range(GB):
                ins = dve.tensor_scalar(xn[:, b:b + 1, :], batch(k.x, g, b), mv[p][:, b, 0:1],
                                        rstd[p][:, b:b + 1], ALU.subtract, ALU.mult)
            ins.then_inc(s["xn_ok"], 1)

        def pe_a_transpose(pe, g):
            wait(pe, s["xT_ok"], g)
            wait(pe, s["p1T_ok"], g - 1)
            wait(pe, s["xn_ok"], g + 1)
            for b in range(GB):
                ins = pe.transpose(tb[:, b * P:(b + 1) * P], xn[:, b, :], k.ident[:])
            ins.then_inc(s["xT_ps"], 1)

        def act_a_xT(act, g):
            wait(act, s["xT_ps"], g + 1)
            wait(act, s["r1_ps"], g * H1)
            nc.scalar.copy(xT[:], tb[:]).then_inc(s["xT_ok"], 1)

        def pe_a_dense(pe, g):
            wait(pe, s["t1_ok"], g - 1)
            wait(pe, s["r1_ok"], g * H1)
            wait(pe, s["xT_ok"], g + 1)
            for c in range(H1):
                pe.matmul(mm[:, c, :], k.w_mlp1[:, c * P:(c + 1) * P], xT[:], start=True, stop=True)\
                    .then_inc(s["r1_ps"], 1)

        def act_a_r1(act, g, p):
            wait(act, s["u1_ok"], g - 1)
            for c in range(H1):
                wait(act, s["r1_ps"], g * H1 + c + 1)
                nc.scalar.activation(r1T[p][:, c, :], mm[:, c, :], ACT.Relu, bias=k.b_mlp1[:, c:c + 1])\
                    .then_inc(s["r1_ok"], 1)

        def pe_b_h1(pe, g, p):
            wait(pe, s["r1_ok"], (g + 1) * H1)
            wait(pe, s["h2_ok"], g - 1)
            for b in range(GB):
                wait(pe, s["h1_ok"], g * GB + b - 1)
                for c in range(H1):
                    ins = pe.matmul(hh[:, b % 2, 0:W1C], r1T[p][:, c, b * P:(b + 1) * P], k.w_fc[:, c, 0:W1C],
                                    start=(c == 0), stop=(c == H1 - 1))
                ins.then_inc(s["h1_ps"], 1)

        def pe_b_f2(pe, g, p):
            wait(pe, s["y1_ok"], g)
            wait(pe, s["y2_ok"], g - 1)
            for c in range(H1):
                ins = pe.matmul(ff[:], k.w_f2_fc[:, c, :], r1T[p][:, c, :], start=(c == 0), stop=(c == H1 - 1))
            ins.then_inc(s["f1_ps"], 1)

        def act_b_h1(act, g, p, b):
            if b == 0:
                wait(act, s["av1_ps"], g - 1)
            wait(act, s["h1_ps"], g * GB + b + 1)
            nc.scalar.copy(h1[p][:, b, 0:W1C], hh[:, b % 2, 0:W1C]).then_inc(s["h1_ok"], 1)

        def act_b_sum(act, g, p):
            wait(act, s["l1_ok"], g)
            wait(act, s["h1_ok"], (g + 1) * GB)
            wait(act, s["f1_ps"], g + 1)
            for b in range(GB):
                ins = nc.scalar.activation(y1[:, b, :], ff[:, b * P:(b + 1) * P], ACT.Identity,
                                           bias=h1[p][:, b, FD:W1C])
            ins.then_inc(s["y1_ok"], 1)

        def dve_b_leaky(dve, g):
            wait(dve, s["p1_ok"], g)
            wait(dve, s["y1_ok"], g + 1)
            dve.scalar_tensor_tensor(e1[:], y1[:], 0.2, y1[:], ALU.mult, ALU.max).then_inc(s["l1_ok"], 1)
            wait(dve, s["l1_ok"], g + 1)
            dve.tensor_reduce(nmax1[:], e1[:], AX.X, ALU.max, negate=True).then_inc(s["max1_ok"], 1)

        def act_b_exp(act, g):
            wait(act, s["pn1_ok"], g)
            wait(act, s["max1_ok"], g + 1)
            for b in range(GB):
                ins = nc.scalar.activation(p1[:, b, :], e1[:, b, :], ACT.Exp, bias=nmax1[:, b:b + 1],
                                           accum_out=den1[:, b:b + 1])
            ins.then_inc(s["p1_ok"], 1)

        def dve_b_rden(dve, g):
            wait(dve, s["p1_ok"], g + 1)
            dve.reciprocal(rden1[:], den1[:]).then_inc(s["rden1_ok"], 1)

        def pool_b_scale(pool, g):
            wait(pool, s["p1T_ps"], g)
            wait(pool, s["rden1_ok"], g + 1)
            pool.tensor_tensor(pn1[:], p1[:], rden1[:].unsqueeze(2).to_broadcast(G4), ALU.mult).then_inc(s["pn1_ok"], 1)

        def pe_b_transpose(pe, g):
            wait(pe, s["xT_ok"], full(lambda n: n, g, 1))
            wait(pe, s["p2T_ok"], g - 1)
            wait(pe, s["p1T_ok"], g)
            wait(pe, s["pn1_ok"], g + 1)
            for b in range(GB):
                ins = pe.transpose(tb[:, b * P:(b + 1) * P], pn1[:, b, :], k.ident[:])
            ins.then_inc(s["p1T_ps"], 1)

        def act_b_p1T(act, g):
            wait(act, s["av1_ps"], g)
            wait(act, s["p1T_ps"], g + 1)
            nc.scalar.copy(p1T[:], tb[:]).then_inc(s["p1T_ok"], 1)

        def pe_b_sums(pe, g, p):
            wait(pe, s["r1_ok"], full(lambda n: n * H1, g, 1))
            wait(pe, s["t1_ok"], g)
            wait(pe, s["p1T_ok"], g + 1)
            for c in range(H1):
                for b in range(GB):
                    ins = pe.matmul(mm[:, c, b * P:(b + 1) * P], h1[p][:, b, c * P:(c + 1) * P],
                                    p1T[:, b * P:(b + 1) * P], start=(b == 0), stop=(b == GB - 1),
                                    skip_group_check=True)
            ins.then_inc(s["av1_ps"], 1)

        def act_c_exp(act, g):
            wait(act, s["w1_ok"], g)
            wait(act, s["av1_ps"], g + 1)
            nc.scalar.activation(v1[:], mm[:], ACT.Exp).then_inc(s["v1_ok"], 1)

        def dve_c_cut(dve, g):
            wait(dve, s["v1_ok"], g + 1)
            dve.tensor_scalar(v1[:], v1[:], 1.0, None, ALU.min).then_inc(s["v1_cut"], 1)

        def act_c_exp2(act, g):
            wait(act, s["t1_ok"], g)
            wait(act, s["v1_cut"], g + 1)
            nc.scalar.activation(w1[:], v1[:], ACT.Exp, bias=k.neg_one[:]).then_inc(s["w1_ok"], 1)

        def dve_c_max(dve, g):
            wait(dve, s["u1_ok"], g)
            wait(dve, s["w1_ok"], g + 1)
            dve.scalar_tensor_tensor(t1[:], w1[:], -1.0, mm[:], ALU.add, ALU.max).then_inc(s["t1_ok"], 1)

        def pool_c_residual(pool, g, p):
            wait(pool, s["r2_ps"], g)
            wait(pool, s["t1_ok"], g + 1)
            pool.tensor_tensor(u1[:], t1[:], r1T[p][:], ALU.add).then_inc(s["u1_ok"], 1)

        def pe_c_dense(pe, g):
            wait(pe, s["s2_ok"], g - 1)
            wait(pe, s["r2_ok"], g)
            wait(pe, s["u1_ok"], g + 1)
            for c in range(H1):
                ins = pe.matmul(rr[:], k.w_mlp2[:, c, :], u1[:, c, :], start=(c == 0), stop=(c == H1 - 1))
            ins.then_inc(s["r2_ps"], 1)

        def act_c_r2(act, g, p):
            wait(act, s["r2T_ps"], g - 1)
            wait(act, s["r2_ps"], g + 1)
            nc.scalar.activation(r2T[p][:], rr[:], ACT.Relu, bias=k.b_mlp2[:]).then_inc(s["r2_ok"], 1)

        def pe_d_h2(pe, g, p):
            wait(pe, s["h1_ok"], full(lambda n: n * GB, g, 1))
            wait(pe, s["h2_ok"], g)
            wait(pe, s["r2_ok"], g + 1)
            for b in range(GB):
                ins = pe.matmul(hh[:, b // 2, (b % 2) * W2C:(b % 2 + 1) * W2C], r2T[p][:, b * P:(b + 1) * P],
                                k.w_hand[:, 0:W2C], start=(b % 2 == 0), stop=(b % 2 == 1), skip_group_check=True)
            ins.then_inc(s["h2_ps"], 1)

        def pe_d_f2(pe, g, p):
            wait(pe, s["y1_ok"], full(lambda n: n, g, 1))
            wait(pe, s["y2_ok"], g)
            pe.matmul(ff[:], k.w_f2_hand[:], r2T[p][:], start=True, stop=True).then_inc(s["f2_ps"], 1)

        def act_d_h2(act, g):
            wait(act, s["av2_ps"], g)
            wait(act, s["h2_ps"], g + 1)
            nc.scalar.copy(h2[:].rearrange("p (t b) c -> p t (b c)", t=2), hh[:, :, 0:2 * W2C]).then_inc(s["h2_ok"], 1)

        def act_d_sum(act, g):
            wait(act, s["l2_ok"], g)
            wait(act, s["h2_ok"], g + 1)
            wait(act, s["f2_ps"], g + 1)
            for b in range(GB):
                ins = nc.scalar.activation(y2[:, b, :], ff[:, b * P:(b + 1) * P], ACT.Identity,
                                           bias=h2[:, b, D:W2C])
            ins.then_inc(s["y2_ok"], 1)

        def dve_d_leaky(dve, g):
            wait(dve, s["p2_ok"], g)
            wait(dve, s["y2_ok"], g + 1)
            dve.scalar_tensor_tensor(l2[:], y2[:], 0.2, y2[:], ALU.mult, ALU.max).then_inc(s["l2_ok"], 1)
            wait(dve, s["l2_ok"], g + 1)
            dve.tensor_tensor(e2[:], l2[:], k.cap[:].unsqueeze(1).to_broadcast(G4), ALU.min).then_inc(s["e2_ok"], 1)
            wait(dve, s["e2_ok"], g + 1)
            dve.tensor_reduce(nmax2[:], e2[:], AX.X, ALU.max, negate=True).then_inc(s["max2_ok"], 1)

        def act_d_exp(act, g):
            wait(act, s["p2T_ps"], g)
            wait(act, s["rden2_ok"], g)
            wait(act, s["max2_ok"], g + 1)
            for b in range(GB):
                ins = nc.scalar.activation(p2[:, b, :], e2[:, b, :], ACT.Exp, bias=nmax2[:, b:b + 1],
                                           accum_out=den2[:, b:b + 1])
            ins.then_inc(s["p2_ok"], 1)

        def dve_d_rden(dve, g, p):
            wait(dve, s["p2_ok"], g + 1)
            dve.reciprocal(rden2[p][:], den2[:]).then_inc(s["rden2_ok"], 1)

        def pe_d_transpose(pe, g):
            wait(pe, s["xT_ok"], full(lambda n: n, g, 3))
            wait(pe, s["p1T_ok"], full(lambda n: n, g, 1))
            wait(pe, s["p2T_ok"], g)
            wait(pe, s["p2_ok"], g + 1)
            for b in range(GB):
                ins = pe.transpose(tb[:, b * P:(b + 1) * P], p2[:, b, :], k.ident[:])
            ins.then_inc(s["p2T_ps"], 1)

        def act_d_p2T(act, g):
            wait(act, s["av2_ps"], g)
            wait(act, s["p2T_ps"], g + 1)
            nc.scalar.copy(p2T[:], tb[:]).then_inc(s["p2T_ok"], 1)

        def pe_d_r2(pe, g, p):
            wait(pe, s["r2_ok"], full(lambda n: n, g, 1))
            wait(pe, s["s2_ok"], g)
            for b in range(GB):
                ins = pe.transpose(rr[:, b * P:(b + 1) * P], r2T[p][:, b * P:(b + 1) * P], k.ident[:])
            ins.then_inc(s["r2T_ps"], 1)

        def pe_d_sums(pe, g):
            wait(pe, s["q2_ok"], g)
            wait(pe, s["p2T_ok"], g + 1)
            for b in range(GB):
                ins = pe.matmul(av[:, b * P:(b + 1) * P], p2T[:, b * P:(b + 1) * P], h2[:, b, 0:D],
                                start=(b == 0), stop=(b == GB - 1), skip_group_check=True)
            ins.then_inc(s["av2_ps"], 1)

        def as_batches(ap):
            return ap.rearrange("p (b d) -> p b d", b=GB)

        def dve_e_quotient(dve, g, p):
            wait(dve, s["t2_ok"], g)
            wait(dve, s["rden2_ok"], g + 1)
            wait(dve, s["av2_ps"], g + 1)
            dve.tensor_tensor(q2[:], as_batches(av[:]), rden2[p][:].unsqueeze(2).to_broadcast(G4), ALU.mult)\
                .then_inc(s["q2_ok"], 1)

        def act_e_exp(act, g):
            wait(act, s["w2_ok"], g)
            wait(act, s["q2_ok"], g + 1)
            nc.scalar.activation(v2[:], q2[:], ACT.Exp).then_inc(s["v2_ok"], 1)

        def dve_e_cut(dve, g):
            wait(dve, s["v2_ok"], g + 1)
            dve.tensor_scalar(v2[:], v2[:], 1.0, None, ALU.min).then_inc(s["v2_cut"], 1)

        def act_e_exp2(act, g):
            wait(act, s["t2_ok"], g)
            wait(act, s["v2_cut"], g + 1)
            nc.scalar.activation(w2[:], v2[:], ACT.Exp, bias=k.neg_one[:]).then_inc(s["w2_ok"], 1)

        def dve_e_out(dve, g):
            wait(dve, s["s2_ok"], g)
            wait(dve, s["w2_ok"], g + 1)
            dve.scalar_tensor_tensor(t2[:], w2[:], -1.0, q2[:], ALU.add, ALU.max).then_inc(s["t2_ok"], 1)
            wait(dve, s["x_ok"], g)
            wait(dve, s["r2T_ps"], g + 1)
            wait(dve, s["t2_ok"], g + 1)
            dve.tensor_tensor(s2[:], t2[:], as_batches(rr[:]), ALU.add).then_inc(s["s2_ok"], 1)

        def dve_e_add(dve, g):
            wait(dve, s["s2_ok"], g + 1)
            xg = k.x[:, bass.ds(g * GB, GB), :]
            dve.scalar_tensor_tensor(xg, s2[:], 0.0, xg, ALU.max, ALU.add).then_inc(s["x_ok"], 1)

        def dve_e_stats(dve, g):
            wait(dve, s["x_ok"], g + 1)
            dve.memset(fence4[:], 0.0)
            layer_norm_stats(dve, lambda b: batch(k.x, g, b).rearrange("p o d -> p (o d)"),
                             st4, mv4, fence4, s["stats4"], g + 1, s["var4"])
            wait(dve, s["var4"], g + 1)
            dve.tensor_scalar(k.mean_var[:, bass.ds(g * GB, GB), :], mv4[:], 1.0, None, ALU.mult)\
                .then_inc(s["kept4"], 1)

        def pe_slot(pe, g, half, p, on):
            q = 1 - p
            if on["d"]:
                pe_d_h2(pe, g, p)
                pe_d_f2(pe, g, p)
            if on["c"]:
                pe_b_sums(pe, g + 1, q)
            if on["b"]:
                pe_b_h1(pe, g + 2, p)
            if on["a"]:
                pe_a_transpose(pe, g + 3)
            if on["b"]:
                pe_b_f2(pe, g + 2, p)
            if on["d"]:
                pe_d_transpose(pe, g)
            if on["a"]:
                pe_a_dense(pe, g + 3)
            if on["c"]:
                pe_c_dense(pe, g + 1)
            if on["d"]:
                pe_d_sums(pe, g)
                pe_d_r2(pe, g, p)
            if on["b"]:
                pe_b_transpose(pe, g + 2)

        def act_slot(act, g, half, p, on):
            q = 1 - p
            if on["d"]:
                act_d_h2(act, g)
            if on["e"]:
                act_e_exp(act, g - 1)
            if on["d"]:
                act_d_sum(act, g)
            if on["a"]:
                act_n_rstd(act, g + 3, q)
            if on["e"]:
                act_e_exp2(act, g - 1)
            if on["c"]:
                act_c_exp(act, g + 1)
            if on["b"]:
                act_b_h1(act, g + 2, p, 0)
            if on["b"]:
                act_b_h1(act, g + 2, p, 1)
            if on["c"]:
                act_c_exp2(act, g + 1)
            if on["b"]:
                act_b_h1(act, g + 2, p, 2)
                act_b_h1(act, g + 2, p, 3)
            if on["a"]:
                act_a_xT(act, g + 3)
            if on["d"]:
                act_d_exp(act, g)
            if on["b"]:
                act_b_sum(act, g + 2, p)
            if on["d"]:
                act_d_p2T(act, g)
            if on["b"]:
                act_b_exp(act, g + 2)
            if on["c"]:
                act_c_r2(act, g + 1, q)
            if on["a"]:
                act_a_r1(act, g + 3, q)
            if on["b"]:
                act_b_p1T(act, g + 2)

        def dve_slot(dve, g, half, p, on):
            q = 1 - p
            if on["e"]:
                dve_e_cut(dve, g - 1)
            if on["d"]:
                dve_d_leaky(dve, g)
            if on["c"]:
                dve_c_cut(dve, g + 1)
            if on["a"]:
                dve_n_apply(dve, g + 3, q)
            if on["c"]:
                dve_c_max(dve, g + 1)
            if on["e"]:
                dve_e_out(dve, g - 1)
            if on["b"]:
                dve_b_leaky(dve, g + 2)
            if on["e"]:
                dve_e_add(dve, g - 1)
            if on["d"]:
                dve_d_rden(dve, g, p)
            if on["n"]:
                dve_n_combine(dve, g + 4, half + 2, p, 0)
            if on["b"]:
                dve_b_rden(dve, g + 2)
            if on["n"]:
                dve_n_combine(dve, g + 4, half + 2, p, 1)
            if on["d"]:
                dve_e_quotient(dve, g, p)
            if on["n"]:
                dve_n_stats(dve, g + 4, p)
            if on["e"]:
                dve_e_stats(dve, g - 1)
        def stages(g):
            def runs(group):
                return 0 <= group < GROUPS
            return dict(n=runs(g + 4), a=runs(g + 3), b=runs(g + 2), c=runs(g + 1), d=runs(g), e=runs(g - 1))

        def slots(slot, eng):
            everything = dict(n=True, a=True, b=True, c=True, d=True, e=True)
            first, last = 2, GROUPS - 4
            for g in range(-4, first):
                slot(eng, g, g // 2, g % 2, stages(g))
            with eng.Fori(first // 2, last // 2) as i:
                for p in range(2):
                    slot(eng, i * 2 + p, i, p, everything)
            for g in range(last, GROUPS + 1):
                slot(eng, g, g // 2, g % 2, stages(g))

        with nc.Block() as block:
            @block.vector
            def _(dve):
                slots(dve_slot, dve)

            @block.scalar
            def _(act):
                exp_ln_tables(nc, act)
                slots(act_slot, act)

            @block.gpsimd
            def _(pool):
                pool_gather(pool, 0, range(8))
                for g in range(-4, GROUPS):
                    on = stages(g)
                    more = g + 5 < GROUPS
                    if more:
                        pool_gather(pool, g + 5, range(0, 6))
                    if on["c"]:
                        pool_c_residual(pool, g + 1, (g + 1) % 2)
                    if more:
                        pool_gather(pool, g + 5, range(6, 8))
                    if on["b"]:
                        pool_b_scale(pool, g + 2)

            @block.tensor
            def _(pe):
                slots(pe_slot, pe)


def last_ffn_phase(nc, k, out):
    KEPT = max(1, TOKENS // 2) - 1
    FC = 4
    with ExitStack() as ctx:
        def sb(name, shape, dt=F32):
            return buffer(nc, ctx, "f_" + name, shape, dt)

        def ps(name, shape):
            return ctx.enter_context(nc.psum_tensor("f_" + name, shape, F32))

        def sem(name):
            return ctx.enter_context(nc.semaphore("f_" + name))

        G4 = [P, GB, P]
        lnv, rstd = sb("lnv", [P, BATCHES]), sb("rstd", [P, BATCHES])
        shift = sb("shift", [P, BATCHES])
        fence = [sb(f"fence{p}", [P, 1]) for p in range(2)]
        before = sb("before", [P, P])
        xn = [sb(f"xn{p}", G4) for p in range(2)]
        xh, xl = [[sb(f"x{c}{p}", [P, GB * P], F32R) for p in range(2)] for c in "hl"]
        w1h, w1l, wrh, wrl = (sb("w1h", [P, FC * P], F32R), sb("w1l", [P, FC * P], F32R), sb("wrh", [P, P], F32R),
                              sb("wrl", [P, P], F32R))
        wb, wd, eq, gt = sb("wb", G4), sb("wd", G4), sb("eq", G4), sb("gt", G4)
        w_tok, rank = sb("w_tok", [P, GB]), sb("rank", [P, GB])
        gate = sb("gate", [P, BATCHES])
        hT = [sb(f"hT{p}", [P, FC, GB * P]) for p in range(2)]
        yb = sb("yb", G4)
        ot = [sb(f"ot{p}", G4) for p in range(2)]

        tb, wp = ps("tb", [P, 512]), ps("wp", [P, 512])
        hp = ps("hp", [P, FC, 512])
        yp = [ps(f"yp{p}", [P, 512]) for p in range(2)]
        s = {n: sem(n) for n in (
            "made", "lnv_done", "rstd_ok", "shift_ok", "xn_ok", "x_sum", "xT_ps", "xh_ok", "xT_ok", "split", "w_ps", "wb_ok", "wd_ok", "wt_ok",
            "eq_ok", "gt_ok", "rank_ok", "gate_ok", "h_ps", "h_ok", "y_ps", "yb_ok", "out_ok")}
        stored = [sem(f"stored{p}") for p in range(2)]

        def batch(ap, g, b):
            return ap[:, bass.ds(g * GB + b, 1), :]

        def act_apply(act, g, p):
            wait(act, s["x_sum"], g - 1)
            wait(act, s["xT_ps"], g - 1)
            nc.scalar.copy(fence[p][:], shift[:, 0:1])
            for b in range(GB):
                at = bass.ds(g * GB + b, 1)
                ins = nc.scalar.activation(xn[p][:, b:b + 1, :], batch(k.x, g, b), ACT.Identity,
                                           scale=rstd[:, at], bias=shift[:, at])
            ins.then_inc(s["xn_ok"], 1)

        def dve_sum(dve, g, p):
            wait(dve, s["xn_ok"], g + 1)
            xg = k.x[:, bass.ds(g * GB, GB), :]
            dve.tensor_tensor(xg, xg, xn[p][:], ALU.add).then_inc(s["x_sum"], 1)

        def pe_transpose(pe, g, p):
            wait(pe, s["xT_ok"], g)
            wait(pe, s["xn_ok"], g + 1)
            for b in range(GB):
                ins = pe.transpose(tb[:, b * P:(b + 1) * P], xn[p][:, b, :], k.ident[:])
            ins.then_inc(s["xT_ps"], 1)

        def act_xT(act, g, p):
            wait(act, s["h_ps"], (g - 1) * FC)
            wait(act, s["xT_ps"], g + 1)
            nc.scalar.copy(xh[p][:], tb[:]).then_inc(s["xh_ok"], 1)

        def dve_xT(dve, g, p):
            wait(dve, s["xh_ok"], g + 1)
            dve.tensor_tensor(xl[p][:], tb[:], xh[p][:].bitcast(F32), ALU.subtract).then_inc(s["xT_ok"], 1)

        def pe_product(pe, out, w_high, w_low, p):
            pe.matmul(out, w_high, xh[p][:], start=True, stop=False)
            pe.matmul(out, w_high, xl[p][:], start=False, stop=False)
            return pe.matmul(out, w_low, xh[p][:], start=False, stop=True)

        def pe_weights(pe, g, p):
            wait(pe, s["wb_ok"], g)
            wait(pe, s["xT_ok"], g + 1)
            pe_product(pe, wp[:], wrh[:], wrl[:], p).then_inc(s["w_ps"], 1)

        def act_weights(act, g):
            wait(act, s["gt_ok"], g)
            wait(act, s["wd_ok"], g)
            wait(act, s["w_ps"], g + 1)
            nc.scalar.activation(wb[:].rearrange("p b j -> p (b j)"), wp[:], ACT.Identity, bias=k.br_last[:])\
                .then_inc(s["wb_ok"], 1)

        def pool_diagonal(pool, g):
            wait(pool, s["wt_ok"], g)
            wait(pool, s["wb_ok"], g + 1)
            pool.tensor_tensor(wd[:], wb[:], k.ident[:].unsqueeze(1).to_broadcast(G4), ALU.mult).then_inc(s["wd_ok"], 1)

        def dve_rank(dve, g):
            wait(dve, s["gate_ok"], g)
            wait(dve, s["wd_ok"], g + 1)
            dve.tensor_reduce(w_tok[:], wd[:], AX.X, ALU.add).then_inc(s["wt_ok"], 1)
            wait(dve, s["wt_ok"], g + 1)
            for b in range(GB):
                ins = dve.scalar_tensor_tensor(eq[:, b, :], wb[:, b, :], w_tok[:, b:b + 1], before[:],
                                               ALU.is_equal, ALU.mult)
            ins.then_inc(s["eq_ok"], 1)

        def dve_gate(dve, g):
            wait(dve, s["eq_ok"], g + 1)
            for b in range(GB):
                ins = dve.scalar_tensor_tensor(gt[:, b, :], wb[:, b, :], w_tok[:, b:b + 1], eq[:, b, :],
                                               ALU.is_gt, ALU.add)
            ins.then_inc(s["gt_ok"], 1)
            wait(dve, s["gt_ok"], g + 1)
            dve.tensor_reduce(rank[:], gt[:], AX.X, ALU.add).then_inc(s["rank_ok"], 1)
            wait(dve, s["rank_ok"], g + 1)
            dve.scalar_tensor_tensor(gate[:, bass.ds(g * GB, GB)], rank[:], float(KEPT), w_tok[:],
                                     ALU.is_lt, ALU.mult).then_inc(s["gate_ok"], 1)

        def pe_up(pe, g, p):
            wait(pe, s["xT_ok"], g + 1)
            for c in range(FC):
                wait(pe, s["h_ok"], (g - 1) * FC + c + 1)
                at = slice(c * P, (c + 1) * P)
                pe_product(pe, hp[:, c, :], w1h[:, at], w1l[:, at], p).then_inc(s["h_ps"], 1)

        def act_gelu(act, g, p):
            wait(act, s["y_ps"], g - 1)
            for c in range(FC):
                wait(act, s["h_ps"], g * FC + c + 1)
                nc.scalar.activation(hT[p][:, c, :], hp[:, c, :], ACT.Gelu_apprx_tanh, bias=k.b1_last[:, c:c + 1])\
                    .then_inc(s["h_ok"], 1)

        def pe_down(pe, g, p):
            wait(pe, s["yb_ok"], g - 1)
            for c in range(FC):
                wait(pe, s["h_ok"], g * FC + c + 1)
                for b in range(GB):
                    ins = pe.matmul(yp[p][:, b * P:(b + 1) * P], hT[p][:, c, b * P:(b + 1) * P], k.w2_last[:, c, :],
                                    start=(c == 0 and b == 0), stop=(c == FC - 1), skip_group_check=True)
            ins.then_inc(s["y_ps"], 1)

        def dve_out(dve, g, half, p):
            wait(dve, s["out_ok"], g)
            wait(dve, s["y_ps"], g + 1)
            dve.tensor_tensor(yb[:], yp[p][:].rearrange("p (b d) -> p b d", b=GB),
                              k.b2_last[:].unsqueeze(1).to_broadcast(G4), ALU.add).then_inc(s["yb_ok"], 1)
            wait(dve, stored[p], half * 16)
            wait(dve, s["yb_ok"], g + 1)
            for b in range(GB):
                ins = dve.scalar_tensor_tensor(ot[p][:, b:b + 1, :], yb[:, b:b + 1, :],
                                               gate[:, bass.ds(g * GB + b, 1)], batch(k.x, g, b), ALU.mult, ALU.add)
            ins.then_inc(s["out_ok"], 1)

        def sp_store(sp, g, p):
            wait(sp, s["out_ok"], g + 1)
            sp.dma_start(out.rearrange("b t d -> t b d")[:, bass.ds(g * GB, GB), :], ot[p][:]).then_inc(stored[p], 16)

        def runs(g):
            return not isinstance(g, int) or 0 <= g < GROUPS

        def slots(slot, eng):
            for g in range(-3, 4):
                slot(eng, g, g // 2, g % 2)
            with eng.Fori(2, GROUPS // 2 - 2) as i:
                for p in range(2):
                    slot(eng, i * 2 + p, i, p)
            for g in range(GROUPS - 4, GROUPS + 1):
                slot(eng, g, g // 2, g % 2)

        def pe_slot(pe, g, half, p):
            if runs(g + 1):
                pe_up(pe, g + 1, 1 - p)
            if runs(g + 2):
                pe_transpose(pe, g + 2, p)
            if runs(g):
                pe_down(pe, g, p)
            if runs(g + 2):
                pe_weights(pe, g + 2, p)

        def act_slot(act, g, half, p):
            if runs(g + 1):
                act_gelu(act, g + 1, 1 - p)
            if runs(g + 2):
                act_xT(act, g + 2, p)
            if runs(g + 3):
                act_apply(act, g + 3, 1 - p)
            if runs(g + 2):
                act_weights(act, g + 2)

        def dve_slot(dve, g, half, p):
            if runs(g - 1):
                dve_out(dve, g - 1, half - 1 + p, 1 - p)
            if runs(g + 1):
                dve_rank(dve, g + 1)
            if runs(g + 2):
                dve_xT(dve, g + 2, p)
            if runs(g + 1):
                dve_gate(dve, g + 1)
            if runs(g + 3):
                dve_sum(dve, g + 3, 1 - p)

        with nc.Block() as block:
            @block.gpsimd
            def _(pool):
                pool.affine_select(out=before[:], in_=k.ones[:], compare_op=ALU.is_gt, fill=0.0, base=0,
                                   pattern=[[-1, P]], channel_multiplier=1).then_inc(s["made"], 1)
                for g in range(2):
                    pool_diagonal(pool, g)
                with pool.Fori(2, GROUPS) as g:
                    pool_diagonal(pool, g)

            @block.scalar
            def _(act):
                nc.scalar.activation(lnv[:], k.mean_var[:, :, 1], ACT.Ln, bias=k.eps_ln[:]).then_inc(s["lnv_done"], 1)
                act.wait_ge(s["lnv_done"], 1)
                nc.scalar.activation(rstd[:], lnv[:], ACT.Exp, scale=-0.5).then_inc(s["rstd_ok"], 1)
                act.wait_ge(s["shift_ok"], 1)
                slots(act_slot, act)

            @block.vector
            def _(dve):
                dve.tensor_copy(w1h[:], k.w1_last[:])
                dve.tensor_copy(wrh[:], k.wr_rep[:]).then_inc(s["split"], 1)
                dve.wait_ge(s["split"], 1)
                dve.tensor_tensor(w1l[:], k.w1_last[:], w1h[:].bitcast(F32), ALU.subtract)
                dve.tensor_tensor(wrl[:], k.wr_rep[:], wrh[:].bitcast(F32), ALU.subtract).then_inc(s["split"], 1)
                dve.wait_ge(s["rstd_ok"], 1)
                dve.scalar_tensor_tensor(shift[:], k.mean_var[:, :, 0], -1.0, rstd[:], ALU.mult, ALU.mult)\
                    .then_inc(s["shift_ok"], 1)
                dve.wait_ge(s["made"], 1)
                slots(dve_slot, dve)

            @block.tensor
            def _(pe):
                pe.wait_ge(s["split"], 2)
                slots(pe_slot, pe)

            @block.sync
            def _(sp):
                for g in range(2):
                    sp_store(sp, g, g)
                with sp.Fori(1, GROUPS // 2) as i:
                    for p in range(2):
                        sp_store(sp, i * 2 + p, p)
                for p in range(2):
                    sp.wait_ge(stored[p], 16 * (GROUPS // 2))


def build(nc, a, out):
    with ExitStack() as whole:
        k = persistent(nc, whole)
        with ExitStack() as tokens:
            add_token_buffers(nc, tokens, k)
            with ExitStack() as buffers:
                add_attention_buffers(nc, buffers, k)
                setup_phase(nc, k, a)
                head_attention_phase(nc, k, a)
            with ExitStack() as buffers:
                add_expert_buffers(nc, buffers, k)
                router_phase(nc, k, a)
                shared_expert_phase(nc, k)
                routed_experts_phase(nc, k)
        combine_graph_phase(nc, k)
        last_ffn_phase(nc, k, out)


_INS = ['x', 'adj', 'L0_gnn_W', 'L0_gnn_a_src', 'L0_gnn_a_dst', 'L0_gnn_beta_tilde', 'L0_gnn_W_out', 'L0_ffn_Wr',
        'L0_ffn_W1s', 'L0_ffn_b1s', 'L0_ffn_W2s', 'L0_ffn_b2s', 'L0_ffn_W1p', 'L0_ffn_b1p', 'L0_ffn_W2p',
        'L0_ffn_b2p', 'L1_gnn_mlp1_w', 'L1_gnn_mlp1_b', 'L1_gnn_mlp2_w', 'L1_gnn_mlp2_b', 'L1_gnn_W_fc',
        'L1_gnn_a_fc', 'L1_gnn_W_hand', 'L1_gnn_a_hand', 'L1_ffn_wr', 'L1_ffn_br', 'L1_ffn_w1', 'L1_ffn_b1',
        'L1_ffn_w2', 'L1_ffn_b2']


def kernel(**inputs):
    import numpy as _np
    import concourse.bacc as _bacc
    from concourse import mybir as _mybir
    from concourse.bass_utils import run_bass_kernel_spmd as _run

    nc = _bacc.Bacc("TRN2", target_bir_lowering=False, num_devices=1)
    arrays, args = {}, {}
    for name in _INS:
        v = _np.ascontiguousarray(inputs[name])
        if v.ndim == 0:
            v = v.reshape(1)
        arrays[f"in_{name}_dram"] = v
        args[name] = nc.dram_tensor(f"in_{name}_dram", v.shape, _mybir.dt.from_np(v.dtype), kind="ExternalInput").ap()
    out = nc.dram_tensor("out_0_dram", (BATCHES, TOKENS, D), _mybir.dt.float32, kind="ExternalOutput").ap()
    build(nc, args, out)
    r = _run(nc, [arrays], core_ids=[0])
    return r.results[0]["out_0_dram"]
```
